# Optimizing a Trainium2 kernel written in Bass

```python
import numpy as np
import jax
import jax.numpy as jnp

def _softmax(x, axis=-1):
    return jax.nn.softmax(x, axis=axis)

def _gelu(x):
    return jax.nn.gelu(x, approximate=True)

def _silu(x):
    return jax.nn.silu(x)

def _sigmoid(x):
    return jax.nn.sigmoid(x)

def _layernorm(x, axis=-1, eps=1e-05):
    m = jnp.mean(x, axis=axis, keepdims=True)
    v = jnp.var(x, axis=axis, keepdims=True)
    return (x - m) / jnp.sqrt(v + eps)

def _scatter_add(tgt, idx, src, axis=0):
    return tgt.at[idx].add(src)

def _segment_sum(src, seg, n):
    return jax.ops.segment_sum(src, seg, n)
kernel_name = 'mk_adaln_d2_jaxref_r8_fe24c0'

def setup_inputs(seed: int=0):
    np.random.seed(seed)
    _w = jnp.asarray

    def _L0_attn_setup():
        import jax, jax.numpy as jnp
        import numpy as np
        N_HEAD = 16
        MAX_WAVELENGTH = 1250
        ROPE_PCT = 1.0

        def apply_p_rope(inputs, positions, head_dim, max_wavelength=MAX_WAVELENGTH, rope_percentage=ROPE_PCT):
            rope_angles = int(rope_percentage * head_dim // 2)
            nope_angles = head_dim // 2 - rope_angles
            fraction = 2.0 * jnp.arange(0, rope_angles) / head_dim
            timescale = max_wavelength ** fraction
            timescale = jnp.pad(timescale, (0, nope_angles), mode='constant', constant_values=(0, jnp.inf))
            sinusoid_inp = positions[..., None] / timescale[None, :]
            sin = jnp.sin(sinusoid_inp)
            cos = jnp.cos(sinusoid_inp)
            first_half, second_half = jnp.split(inputs, 2, axis=-1)
            first_part = first_half * cos - second_half * sin
            second_part = second_half * cos + first_half * sin
            return jnp.concatenate([first_part, second_part], axis=-1).astype(inputs.dtype)
        key = jax.random.key(seed)
        ks = jax.random.split(key, 4)
        B, T, C = (2, 256, 128)
        x = jax.random.normal(ks[0], (B, T, C), dtype=jnp.float32)
        W_attn = jax.random.normal(ks[1], (C, 3 * C), dtype=jnp.float32) * 0.02
        b_attn = jnp.zeros((3 * C,), dtype=jnp.float32)
        W_proj = jax.random.normal(ks[2], (C, C), dtype=jnp.float32) * 0.02
        b_proj = jnp.zeros((C,), dtype=jnp.float32)
        return {'x': x, 'W_attn': W_attn, 'b_attn': b_attn, 'W_proj': W_proj, 'b_proj': b_proj}
    _L0_attn_in = _L0_attn_setup()

    def _L0_ffn_setup():
        import jax, jax.numpy as jnp
        import numpy as np
        HIDDEN_SIZE = 128
        NUM_EXPERTS = 8
        MOE_INTERMEDIATE_SIZE = 176
        NUM_EXPERTS_PER_TOK = 2
        SHARED_EXPERT_INTERMEDIATE_SIZE = 352
        B, T = (2, 128)
        W_SCALE = 0.02
        key = jax.random.key(seed)
        ks = jax.random.split(key, 8)
        H, E, I, SI = (HIDDEN_SIZE, NUM_EXPERTS, MOE_INTERMEDIATE_SIZE, SHARED_EXPERT_INTERMEDIATE_SIZE)
        return {'x': jax.random.normal(ks[0], (B, T, H), jnp.float32), 'gate_w': jax.random.normal(ks[1], (E, H), jnp.float32) * W_SCALE, 'experts_gate_up': jax.random.normal(ks[2], (E, 2 * I, H), jnp.float32) * W_SCALE, 'experts_down': jax.random.normal(ks[3], (E, H, I), jnp.float32) * W_SCALE, 'shared_gate_w': jax.random.normal(ks[4], (SI, H), jnp.float32) * W_SCALE, 'shared_up_w': jax.random.normal(ks[5], (SI, H), jnp.float32) * W_SCALE, 'shared_down_w': jax.random.normal(ks[6], (H, SI), jnp.float32) * W_SCALE, 'shared_expert_gate_w': jax.random.normal(ks[7], (1, H), jnp.float32) * W_SCALE}
    _L0_ffn_in = _L0_ffn_setup()
    _L0_c = _w((lambda *s: np.random.randn(*s).astype(np.float32) * 0.05)(4, 128))
    _L0_wmod = _w((lambda *s: np.random.randn(*s).astype(np.float32) * 0.05)(128, 6 * 128) * 128 ** (-0.5))

    def _L1_attn_setup():
        import jax, jax.numpy as jnp
        import numpy as np
        B, L, D, N = (8, 128, 128, 32)
        DT_MIN, DT_MAX = (0.001, 0.1)
        key = jax.random.key(seed)
        ks = jax.random.split(key, 12)
        s = 1.0 / np.sqrt(D)
        inp = {'x': jax.random.normal(ks[0], (B, L, D), jnp.float32), 'in_W': jax.random.uniform(ks[1], (D, D), jnp.float32, -s, s), 'in_b': jax.random.uniform(ks[2], (D,), jnp.float32, -s, s), 'log_dt': (np.log(DT_MIN) + jax.random.uniform(ks[3], (D,), jnp.float32) * (np.log(DT_MAX) - np.log(DT_MIN))).astype(jnp.float32), 'C': jax.random.normal(ks[4], (D, N, 2), jnp.float32), 'log_A_real': jnp.log(0.5 * jnp.ones((D, N), jnp.float32)), 'A_imag': jnp.tile((np.pi * jnp.arange(N, dtype=np.float32))[None, :], (D, 1)), 'D_skip': jax.random.normal(ks[5], (D,), jnp.float32), 'glu_W': jax.random.uniform(ks[6], (2 * D, D), jnp.float32, -s, s), 'glu_b': jax.random.uniform(ks[7], (2 * D,), jnp.float32, -s, s), 'out_W': jax.random.uniform(ks[8], (D, D), jnp.float32, -s, s), 'out_b': jax.random.uniform(ks[9], (D,), jnp.float32, -s, s)}
        return inp
    _L1_attn_in = _L1_attn_setup()

    def _L1_ffn_setup():
        import jax, jax.numpy as jnp
        import numpy as np
        TOP_K = 2
        key = jax.random.key(seed)
        ks = jax.random.split(key, 5)
        B, S, D, H, E = (2, 256, 128, 352, 8)
        x = jax.random.normal(ks[0], (B, S, D), dtype=jnp.float32)
        Wg = jax.random.normal(ks[1], (E, D), dtype=jnp.float32) * 0.02
        W1 = jax.random.normal(ks[2], (E, H, D), dtype=jnp.float32) * 0.02
        W2 = jax.random.normal(ks[3], (E, H, D), dtype=jnp.float32) * 0.02
        W3 = jax.random.normal(ks[4], (E, D, H), dtype=jnp.float32) * 0.02
        return {'x': x, 'Wg': Wg, 'W1': W1, 'W2': W2, 'W3': W3}
    _L1_ffn_in = _L1_ffn_setup()
    _L1_c = _w((lambda *s: np.random.randn(*s).astype(np.float32) * 0.05)(4, 128))
    _L1_wmod = _w((lambda *s: np.random.randn(*s).astype(np.float32) * 0.05)(128, 6 * 128) * 128 ** (-0.5))
    _d = {'L0_attn_x': _L0_attn_in['x'], 'L0_attn_W_attn': _L0_attn_in['W_attn'], 'L0_attn_b_attn': _L0_attn_in['b_attn'], 'L0_attn_W_proj': _L0_attn_in['W_proj'], 'L0_attn_b_proj': _L0_attn_in['b_proj'], 'L0_ffn_gate_w': _L0_ffn_in['gate_w'], 'L0_ffn_experts_gate_up': _L0_ffn_in['experts_gate_up'], 'L0_ffn_experts_down': _L0_ffn_in['experts_down'], 'L0_ffn_shared_gate_w': _L0_ffn_in['shared_gate_w'], 'L0_ffn_shared_up_w': _L0_ffn_in['shared_up_w'], 'L0_ffn_shared_down_w': _L0_ffn_in['shared_down_w'], 'L0_ffn_shared_expert_gate_w': _L0_ffn_in['shared_expert_gate_w'], 'L0_c': _L0_c, 'L0_wmod': _L0_wmod, 'L1_attn_in_W': _L1_attn_in['in_W'], 'L1_attn_in_b': _L1_attn_in['in_b'], 'L1_attn_log_dt': _L1_attn_in['log_dt'], 'L1_attn_C': _L1_attn_in['C'], 'L1_attn_log_A_real': _L1_attn_in['log_A_real'], 'L1_attn_A_imag': _L1_attn_in['A_imag'], 'L1_attn_D_skip': _L1_attn_in['D_skip'], 'L1_attn_glu_W': _L1_attn_in['glu_W'], 'L1_attn_glu_b': _L1_attn_in['glu_b'], 'L1_attn_out_W': _L1_attn_in['out_W'], 'L1_attn_out_b': _L1_attn_in['out_b'], 'L1_ffn_Wg': _L1_ffn_in['Wg'], 'L1_ffn_W1': _L1_ffn_in['W1'], 'L1_ffn_W2': _L1_ffn_in['W2'], 'L1_ffn_W3': _L1_ffn_in['W3'], 'L1_c': _L1_c, 'L1_wmod': _L1_wmod}
    _x0 = _d['L0_attn_x']
    _d['L0_attn_x'] = jax.random.normal(jax.random.fold_in(jax.random.key(seed), 1), (4, 1024, 128), dtype=_x0.dtype)
    del _x0
    return _d

def reference(L0_attn_x, L0_attn_W_attn, L0_attn_b_attn, L0_attn_W_proj, L0_attn_b_proj, L0_ffn_gate_w, L0_ffn_experts_gate_up, L0_ffn_experts_down, L0_ffn_shared_gate_w, L0_ffn_shared_up_w, L0_ffn_shared_down_w, L0_ffn_shared_expert_gate_w, L0_c, L0_wmod, L1_attn_in_W, L1_attn_in_b, L1_attn_log_dt, L1_attn_C, L1_attn_log_A_real, L1_attn_A_imag, L1_attn_D_skip, L1_attn_glu_W, L1_attn_glu_b, L1_attn_out_W, L1_attn_out_b, L1_ffn_Wg, L1_ffn_W1, L1_ffn_W2, L1_ffn_W3, L1_c, L1_wmod):

    def _L0_attn_ref(x, W_attn, b_attn, W_proj, b_proj):
        import jax, jax.numpy as jnp
        import numpy as np
        N_HEAD = 16
        MAX_WAVELENGTH = 1250
        ROPE_PCT = 1.0

        def apply_p_rope(inputs, positions, head_dim, max_wavelength=MAX_WAVELENGTH, rope_percentage=ROPE_PCT):
            rope_angles = int(rope_percentage * head_dim // 2)
            nope_angles = head_dim // 2 - rope_angles
            fraction = 2.0 * jnp.arange(0, rope_angles) / head_dim
            timescale = max_wavelength ** fraction
            timescale = jnp.pad(timescale, (0, nope_angles), mode='constant', constant_values=(0, jnp.inf))
            sinusoid_inp = positions[..., None] / timescale[None, :]
            sin = jnp.sin(sinusoid_inp)
            cos = jnp.cos(sinusoid_inp)
            first_half, second_half = jnp.split(inputs, 2, axis=-1)
            first_part = first_half * cos - second_half * sin
            second_part = second_half * cos + first_half * sin
            return jnp.concatenate([first_part, second_part], axis=-1).astype(inputs.dtype)
        B, T, C = x.shape
        H = N_HEAD
        D = C // H
        qkv = x @ W_attn + b_attn
        q, k, v = jnp.split(qkv, 3, axis=-1)

        def split_heads(t):
            return t.reshape(B, T, H, D).transpose(0, 2, 1, 3)
        q, k, v = (split_heads(q), split_heads(k), split_heads(v))
        positions = jnp.arange(T, dtype=q.dtype)
        q = apply_p_rope(q, positions, D)
        k = apply_p_rope(k, positions, D)
        scale = jnp.sqrt(D).astype(k.dtype)
        attn = jnp.einsum('bhqd,bhkd->bhqk', q, k) / scale
        causal_mask = jnp.tril(jnp.ones((T, T))).astype(bool)
        attn = jnp.where(causal_mask, attn, jnp.finfo(attn.dtype).min)
        attn = jax.nn.softmax(attn, axis=-1)
        y = jnp.einsum('bhqk,bhkd->bhqd', attn, v)
        y = y.transpose(0, 2, 1, 3).reshape(B, T, C)
        return y @ W_proj + b_proj

    def _L0_ffn_ref(x, gate_w, experts_gate_up, experts_down, shared_gate_w, shared_up_w, shared_down_w, shared_expert_gate_w):
        import jax, jax.numpy as jnp
        import numpy as np
        HIDDEN_SIZE = 128
        NUM_EXPERTS = 8
        MOE_INTERMEDIATE_SIZE = 176
        NUM_EXPERTS_PER_TOK = 2
        SHARED_EXPERT_INTERMEDIATE_SIZE = 352
        B, T = (2, 128)
        W_SCALE = 0.02
        Bx, Tx, H = x.shape
        E = gate_w.shape[0]
        I = experts_down.shape[2]
        x_flat = x.reshape(Bx * Tx, H)
        logits = x_flat @ gate_w.T
        scores = jax.nn.softmax(logits, axis=-1)
        _, topk_ids = jax.lax.top_k(scores, NUM_EXPERTS_PER_TOK)
        in_topk = jax.nn.one_hot(topk_ids, E, dtype=x.dtype).sum(axis=1)
        w = scores * in_topk
        gu = jnp.einsum('nh,eih->nei', x_flat, experts_gate_up)
        g, u = (gu[..., :I], gu[..., I:])
        h = jax.nn.silu(g) * u
        expert_out = jnp.einsum('nei,ehi->neh', h, experts_down)
        out = jnp.einsum('neh,ne->nh', expert_out, w)
        shared = jax.nn.silu(x_flat @ shared_gate_w.T) * (x_flat @ shared_up_w.T) @ shared_down_w.T
        shared_weight = jax.nn.sigmoid(x_flat @ shared_expert_gate_w.T)
        out = out + shared_weight * shared
        return out.reshape(Bx, Tx, H)

    def _L1_attn_ref(x, in_W, in_b, log_dt, C, log_A_real, A_imag, D_skip, glu_W, glu_b, out_W, out_b):
        import jax, jax.numpy as jnp
        import numpy as np
        B, L, D, N = (8, 128, 128, 32)
        DT_MIN, DT_MAX = (0.001, 0.1)
        x_in = x @ in_W.T + in_b
        u = jnp.swapaxes(x_in, 1, 2)
        Lseq = u.shape[-1]
        dt = jnp.exp(log_dt)
        Cc = (C[..., 0] + 1j * C[..., 1]).astype(jnp.complex64)
        A = (-jnp.exp(log_A_real) + 1j * A_imag).astype(jnp.complex64)
        dtA = A * dt[:, None].astype(jnp.complex64)
        K = jnp.exp(dtA[:, :, None] * jnp.arange(Lseq, dtype=jnp.float32))
        Ceff = Cc * (jnp.exp(dtA) - 1.0) / A
        k = 2.0 * jnp.einsum('hn,hnl->hl', Ceff, K).real
        n = 2 * Lseq
        k_f = jnp.fft.rfft(k, n=n)
        u_f = jnp.fft.rfft(u, n=n)
        y = jnp.fft.irfft(u_f * k_f, n=n)[..., :Lseq]
        y = y + u * D_skip[:, None]
        y = jax.nn.gelu(y, approximate=False)
        z = jnp.einsum('oh,bhl->bol', glu_W, y) + glu_b[None, :, None]
        a, g = jnp.split(z, 2, axis=1)
        y = a * jax.nn.sigmoid(g)
        y = jnp.swapaxes(y, 1, 2)
        out = y @ out_W.T + out_b
        return out + x

    def _L1_ffn_ref(x, Wg, W1, W2, W3):
        import jax, jax.numpy as jnp
        import numpy as np
        TOP_K = 2
        B, S, D = x.shape
        E = Wg.shape[0]
        xt = x.reshape(B * S, D)
        scores = xt @ Wg.T
        topk_scores, topk_idx = jax.lax.top_k(scores, TOP_K)
        gate = jax.nn.silu(jnp.einsum('td,ehd->teh', xt, W1))
        up = jnp.einsum('td,ehd->teh', xt, W2)
        y = jnp.einsum('teh,edh->ted', gate * up, W3)
        onehot = jax.nn.one_hot(topk_idx, E, dtype=x.dtype)
        w = jnp.einsum('tke,tk->te', onehot, topk_scores)
        out = jnp.einsum('te,ted->td', w, y)
        return out.reshape(B, S, D)
    x = L0_attn_x
    mod = (_silu(L0_c) @ L0_wmod).reshape(L0_c.shape[0], 6, 1, -1)
    sa, ca, ga, sb, cb, gb = (mod[:, 0], mod[:, 1], mod[:, 2], mod[:, 3], mod[:, 4], mod[:, 5])
    ga = (2 * (ga >= 0) - 1) * jnp.maximum(jnp.abs(ga), 0.25)
    gb = (2 * (gb >= 0) - 1) * jnp.maximum(jnp.abs(gb), 0.25)
    h = _layernorm(x, axis=-1) * (1 + ca) + sa
    x = x + ga * _L0_attn_ref(h, L0_attn_W_attn, L0_attn_b_attn, L0_attn_W_proj, L0_attn_b_proj)
    h = _layernorm(x, axis=-1) * (1 + cb) + sb
    x = x + gb * _L0_ffn_ref(h, L0_ffn_gate_w, L0_ffn_experts_gate_up, L0_ffn_experts_down, L0_ffn_shared_gate_w, L0_ffn_shared_up_w, L0_ffn_shared_down_w, L0_ffn_shared_expert_gate_w)
    mod = (_silu(L1_c) @ L1_wmod).reshape(L1_c.shape[0], 6, 1, -1)
    sa, ca, ga, sb, cb, gb = (mod[:, 0], mod[:, 1], mod[:, 2], mod[:, 3], mod[:, 4], mod[:, 5])
    ga = (2 * (ga >= 0) - 1) * jnp.maximum(jnp.abs(ga), 0.25)
    gb = (2 * (gb >= 0) - 1) * jnp.maximum(jnp.abs(gb), 0.25)
    h = _layernorm(x, axis=-1) * (1 + ca) + sa
    x = x + ga * _L1_attn_ref(h, L1_attn_in_W, L1_attn_in_b, L1_attn_log_dt, L1_attn_C, L1_attn_log_A_real, L1_attn_A_imag, L1_attn_D_skip, L1_attn_glu_W, L1_attn_glu_b, L1_attn_out_W, L1_attn_out_b)
    h = _layernorm(x, axis=-1) * (1 + cb) + sb
    x = x + gb * _L1_ffn_ref(h, L1_ffn_Wg, L1_ffn_W1, L1_ffn_W2, L1_ffn_W3)
    return x

_drawn_inputs = setup_inputs


def setup_inputs(seed=0):
    import zlib

    import numpy as np

    out = dict(_drawn_inputs(seed))
    spreads = {'L0_attn_b_attn': (0.0, 0.8),
     'L0_attn_b_proj': (0.0, 0.315),
     'L1_attn_log_A_real': (-0.6931471824645996, 0.6)}
    factors = {'L0_attn_W_attn': 8.0,
     'L0_attn_W_proj': 8.0,
     'L0_ffn_gate_w': 8.0,
     'L0_ffn_experts_gate_up': 8.0,
     'L0_ffn_experts_down': 8.0,
     'L0_ffn_shared_gate_w': 8.0,
     'L0_ffn_shared_up_w': 8.0,
     'L0_ffn_shared_down_w': 8.0,
     'L0_ffn_shared_expert_gate_w': 8.0,
     'L1_attn_in_b': 8.0,
     'L1_attn_log_dt': 2.896,
     'L1_attn_C': 2.798,
     'L1_attn_A_imag': 2.879,
     'L1_attn_D_skip': 3.193,
     'L1_attn_glu_b': 8.0,
     'L1_attn_out_b': 4.154,
     'L1_ffn_Wg': 8.0,
     'L1_ffn_W1': 8.0,
     'L1_ffn_W2': 8.0,
     'L1_ffn_W3': 8.0}
    for name, (base, spread) in spreads.items():
        noise = np.random.default_rng([zlib.crc32(name.encode()), seed]).standard_normal(out[name].shape)
        drawn = base * np.exp(spread * noise) if base else spread * noise
        out[name] = jnp.asarray(drawn.astype(out[name].dtype))
    for name, factor in factors.items():
        out[name] = (out[name] * factor).astype(out[name].dtype)
    return out
```

```python
from contextlib import ExitStack

import numpy as np

import concourse.bass as bass
from concourse import mybir

F32 = mybir.dt.float32
BF16 = mybir.dt.bfloat16
U32 = mybir.dt.uint32
ALU = mybir.AluOpType
ACT = mybir.ActivationFunctionType
AX = mybir.AxisListType

P = 128
NB, T, C = 4, 1024, 128
TOK = NB * T
NT = TOK // P
TPB = T // P
ST = 512
NH, HD = 16, 8
HQ = 4
NQ = NH // HQ
NQUAD = NB * NQ
TERMS = 6
KR = TERMS * HD
MROW = 64
EPS = 1e-5
NEG = -1e30

QT = [0, 0, 1, 1, 0, 2]
KT = [0, 1, 0, 1, 2, 0]


def wait_before(eng, reg, sem, value, met):
    if isinstance(value, int):
        eng.wait_ge(sem, value)
        return
    eng.reg_mov(reg, value)
    eng.wait_ge(met, 1)
    eng.wait_ge(sem, reg)


def semaphore_of(nc, phase, name):
    s = phase.enter_context(nc.semaphore(name))
    phase.callback(nc.sync.sem_clear, s)
    return s


class Work:
    pass


class Chain:

    def __init__(self, eng, sem, base=0):
        self.eng, self.sem, self.base, self.n = eng, sem, base, 0

    def __call__(self, ins):
        self.n += 1
        ins.then_inc(self.sem, 1)
        self.eng.wait_ge(self.sem, self.base + self.n)


def layernorm_stats(nc, eng, link, x, w):
    st = w.bnst
    v = nc.vector
    for u in range(NT):
        ins = v.bn_stats(st[:, u, :], x[:, u, :])
    link(ins)
    link(v.tensor_tensor(w.mean[:], st[:, :, 1], st[:, :, 4], ALU.add))
    link(v.tensor_tensor(w.t0[:], st[:, :, 1], st[:, :, 4], ALU.subtract))
    link(v.tensor_tensor(w.t1[:], st[:, :, 2], st[:, :, 5], ALU.add))
    link(v.tensor_tensor(w.t0[:], w.t0[:], w.t0[:], ALU.mult))
    link(v.tensor_scalar(w.t1[:], w.t1[:], 1.0 / C, EPS, ALU.mult, ALU.add))
    link(v.tensor_scalar(w.mean[:], w.mean[:], 0.5, None, ALU.mult))
    return v.scalar_tensor_tensor(out=w.t1[:], in0=w.t0[:], scalar=0.25, in1=w.t1[:], op0=ALU.mult, op1=ALU.add)


def setup_phase(nc, w, d):
    with ExitStack() as ctx:
        sb = lambda n, s, t=F32: ctx.enter_context(nc.sbuf_tensor(n, s, t))
        ps = lambda n, s, t=F32: ctx.enter_context(nc.psum_tensor(n, s, t))
        sem = lambda n: semaphore_of(nc, ctx, n)
        root_done = sem("root_done")
        csT = sb("csT", [P, 2, NB])
        csS = sb("csS", [P, 2, NB])
        csB = sb("csB", [P, 2 * NB, P])
        wm = sb("wm", [P, 2, 6 * C])
        sgn = sb("sgn", [P, 4 * NB * C])
        mag = sb("mag", [P, 4 * NB * C])
        mps = ps("mps", [P, 2, 6, NB])
        gps = ps("gps", [P, 4, 4, C])
        c_in, x_in, attn_in, cst_in = sem("c_in"), sem("x_in"), sem("attn_in"), sem("cst_in")
        silu_done, cols_done, cols_ps, gate_ps = sem("silu_done"), sem("cols_done"), sem("cols_ps"), sem("gate_ps")
        vst, gate_out, zero_set, xg_zero = sem("vst"), sem("gate_out"), sem("zero_set"), sem("xg_zero")
        zero = sb("zero", [P, C])
        with nc.Block() as block:
            @block.sync
            def _(sp):
                for l in range(2):
                    with nc.allow_non_contiguous_dma(reason="4 conditioning rows as columns"):
                        sp.dma_start(csT[:, l, :], d.c[l].rearrange("b f -> f b")).then_inc(c_in, 16)
                    sp.dma_start(wm[:, l, :], d.wmod[l]).then_inc(c_in, 16)
                sp.dma_start(w.x[:], d.x.rearrange("b (n p) c -> p (b n) c", p=P)).then_inc(x_in, 16)
                sp.dma_start(w.wqkv[:], d.w_attn).then_inc(attn_in, 16)
                with nc.allow_non_contiguous_dma(reason="bias vectors as columns"):
                    for j in range(2):
                        sp.dma_start(w.bqk[:, 2 * j:2 * j + 1],
                                     d.b_attn[j * C:(j + 1) * C].rearrange("(p o) -> p o", o=1)).then_inc(attn_in, 16)
                        for s in range(2):
                            for h in range(NH):
                                sp.dma_start(w.bqk[h * HD + s * 4:h * HD + s * 4 + 4, 2 * j + 1:2 * j + 2],
                                             d.b_attn[j * C + h * HD + (1 - s) * 4:j * C + h * HD + (1 - s) * 4 + 4]
                                             .rearrange("(p o) -> p o", o=1)).then_inc(attn_in, 16)
                sp.dma_start(w.bv[:], d.b_attn[2 * C:].rearrange("(o c) -> o c", o=1).to_broadcast([P, C])).then_inc(cst_in, 16)
                sp.dma_start(w.bo[:], d.b_proj.rearrange("(o c) -> o c", o=1).to_broadcast([P, C])).then_inc(cst_in, 16)
                sp.dma_start(w.wo[:], d.w_proj).then_inc(cst_in, 16)
                sp.dma_start(w.rope[:], d.rope).then_inc(cst_in, 16)
                sp.dma_start(w.rotsign[:], d.rotsign).then_inc(attn_in, 16)
                sp.dma_start(w.ident[:], d.ident).then_inc(cst_in, 16)
                sp.dma_start(w.identb[:], d.identb).then_inc(cst_in, 16)
                sp.dma_start(w.maskb[:], d.maskb).then_inc(cst_in, 16)
                for src, dst in ((d.trib, w.trib), (d.onesb, w.onesb), (d.iota, w.iota), (d.flip, w.flip)):
                    sp.dma_start(dst[:], src).then_inc(cst_in, 16)
                sp.wait_ge(zero_set, 1)
                sp.dma_start(d.xg.rearrange("(p n) c -> p n c", p=P), zero[:].rearrange("p (o c) -> p o c", o=1)
                             .to_broadcast([P, NSLOT, C])).then_inc(xg_zero, 16)
                sp.wait_ge(cst_in, 16 * 11)
                sp.wait_ge(xg_zero, 16)

            @block.gpsimd
            def _(pool):
                pool.memset(zero[:], 0.0).then_inc(zero_set, 1)

            @block.scalar
            def _(act):
                act.wait_ge(c_in, 64)
                nc.scalar.activation(csS[:], csT[:], ACT.Silu).then_inc(silu_done, 1)
                act.wait_ge(vst, 8)
                nc.scalar.activation(w.t1[:], w.t1[:], ACT.Sqrt).then_inc(root_done, 1)

            @block.vector
            def _(dve):
                dve.wait_ge(x_in, 16)
                link = Chain(dve, vst)
                link(layernorm_stats(nc, dve, link, w.x, w))
                dve.wait_ge(root_done, 1)
                link(nc.vector.reciprocal(w.rstd[:], w.t1[:]))
                dve.wait_ge(silu_done, 1)
                for l in range(2):
                    for b in range(NB):
                        ins = nc.vector.tensor_copy(csB[:, l * NB + b, :], csS[:, l, b:b + 1].to_broadcast([P, P]))
                ins.then_inc(cols_done, 1)
                dve.wait_ge(attn_in, 16 * (1 + 2 * (1 + 2 * NH) + 1))
                wv = w.wqkv[:, 0:2 * C].rearrange("p (h s e) -> p h s e", s=2, e=4)
                rv = w.wrot[:].rearrange("p (h s e) -> p h s e", s=2, e=4)
                nc.vector.tensor_scalar(rv[:, :, 0, :], wv[:, :, 1, :], -1.0, None, ALU.mult)
                link(nc.vector.tensor_copy(rv[:, :, 1, :], wv[:, :, 0, :]))
                for j in range(2):
                    ins = nc.vector.tensor_tensor(w.bqk[:, 2 * j + 1:2 * j + 2], w.bqk[:, 2 * j + 1:2 * j + 2],
                                                  w.rotsign[:], ALU.mult)
                link(ins)
                dve.wait_ge(cols_ps, 1)
                link(nc.vector.tensor_copy(w.mod[:], mps[:]))
                for j in (1, 4):
                    ins = nc.vector.tensor_scalar(w.mod[:, :, j, :], w.mod[:, :, j, :], 1.0, None, ALU.add)
                link(ins)
                gb = w.gate[:].rearrange("p a b c -> p (a b c)")
                g = gb
                dve.wait_ge(gate_ps, 1)
                nc.vector.tensor_copy(gb, gps[:].rearrange("p a b c -> p (a b c)")).then_inc(gate_out, 1)
                dve.wait_ge(gate_out, 1)
                link(nc.vector.tensor_scalar(sgn[:], g, 0.0, 2.0, ALU.is_ge, ALU.mult))
                link(nc.vector.tensor_scalar(mag[:], g, -1.0, None, ALU.mult))
                link(nc.vector.tensor_tensor(mag[:], mag[:], g, ALU.max))
                link(nc.vector.tensor_scalar(mag[:], mag[:], 0.25, None, ALU.max))
                link(nc.vector.scalar_tensor_tensor(out=gb, in0=sgn[:], scalar=-1.0, in1=mag[:], op0=ALU.add, op1=ALU.mult))
                dve.wait_ge(gate_ps, 2)
                for l in range(2):
                    nc.vector.tensor_copy(w.modr[:, 2 * l], gps[:, 2 * l])
                    ins = nc.vector.tensor_scalar(w.modr[:, 2 * l + 1], gps[:, 2 * l + 1], 1.0, None, ALU.add)
                ins.then_inc(gate_out, 1)
                dve.wait_ge(gate_ps, 3)
                nc.vector.tensor_copy(w.moda[:, 0], gps[:, 2])
                nc.vector.tensor_scalar(w.moda[:, 1], gps[:, 3], 1.0, None, ALU.add)

            @block.tensor
            def _(pe):
                pe.wait_ge(silu_done, 1)
                for l in range(2):
                    for j in range(6):
                        ins = nc.tensor.matmul(mps[:, l, j, :], wm[:, l, j * C:(j + 1) * C], csS[:, l, :], start=True, stop=True)
                ins.then_inc(cols_ps, 1)
                pe.wait_ge(cols_done, 1)
                for rnd, comps in enumerate(((2, 5), (3, 4), (0, 1))):
                    pe.wait_ge(gate_out, rnd)
                    for l in range(2):
                        for a, j in enumerate(comps):
                            for b in range(NB):
                                ins = nc.tensor.matmul(gps[:, 2 * l + a, b, :], csB[:, l * NB + b, :], wm[:, l, j * C:(j + 1) * C],
                                                       start=True, stop=True)
                    ins.then_inc(gate_ps, 1)


def qkv_phase(nc, w, d):
    with ExitStack() as ctx:
        sb = lambda n, s, t=F32: ctx.enter_context(nc.sbuf_tensor(n, s, t))
        ps = lambda n, s, t=F32: ctx.enter_context(nc.psum_tensor(n, s, t))
        sem = lambda n: semaphore_of(nc, ctx, n)
        xn = [sb(f"xn{u}", [P, 4, C]) for u in range(2)]
        hT = [sb(f"hTq{u}", [P, ST]) for u in range(2)]
        raw = [sb(f"raw{u}", [P, 4, ST]) for u in range(2)]
        res = [sb(f"res{u}", [P, 2, ST]) for u in range(2)]
        term = [[sb(f"term{u}_{n}", [P, 2, ST], BF16) for n in range(3)] for u in range(2)]
        pT = ps("pT", [P, 2, ST])
        pq = ps("pq", [P, 4, ST])
        pv = ps("pv", [P, 2, ST])
        norm_done, tr_done, h_done, qk_ps, v_ps = sem("norm_done"), sem("tr_done"), sem("h_done"), sem("qk_ps"), sem("v_ps")
        qk_out, v_out, sin_done = sem("qk_out"), sem("v_out"), sem("sin_done")
        cos_done, rope_done, hi_done, r1_done, mid_done, lo_done = (sem("cos_done"), sem("rope_done"), sem("hi_done"),
                                                                   sem("r1_done"), sem("mid_done"), sem("lo_done"))
        stored = [sem(f"stored{u}") for u in range(2)]
        with nc.Block() as block:
            @block.vector
            def _(dve):
                def normed(b, u, s):
                    dve.wait_ge(tr_done, s)
                    for j in range(4):
                        t = b * TPB + u * 4 + j
                        ins = nc.vector.tensor_scalar(xn[u][:, j, :], w.x[:, t, :], w.mean[:, bass.ds(t, 1)],
                                                      w.rstd[:, bass.ds(t, 1)], ALU.subtract, ALU.mult)
                    ins.then_inc(norm_done, 1)
                with dve.Fori(0, NB) as b:
                    for u in range(2):
                        s = 2 * b + u
                        normed(b, u, s)
                        dve.wait_ge(v_ps, s + 1)
                        vt = w.v[:].rearrange("p (b q) k c -> p b k q c", q=NQ)[:, bass.ds(b, 1), u * 4:u * 4 + 4, :, :]
                        for j in range(4):
                            ins = nc.vector.tensor_tensor(vt[:, 0, j], pv[:, u, j * C:(j + 1) * C].rearrange("p (q c) -> p q c", q=NQ),
                                                          w.bv[:].rearrange("p (q c) -> p q c", q=NQ), ALU.add)
                        ins.then_inc(v_out, 1)
                        dve.wait_ge(qk_out, s + 1)
                        cosb = w.rope[:, 0:1, u * ST:(u + 1) * ST].to_broadcast([P, 2, ST])
                        nc.vector.tensor_tensor(raw[u][:, 0:2, :], raw[u][:, 0:2, :], cosb, ALU.mult).then_inc(cos_done, 1)
                        dve.wait_ge(cos_done, s + 1)
                        dve.wait_ge(sin_done, s + 1)
                        q = raw[u][:, 0:2, :]
                        nc.vector.tensor_tensor(q, q, raw[u][:, 2:4, :], ALU.add).then_inc(rope_done, 1)
                        dve.wait_ge(hi_done, s + 1)
                        nc.vector.tensor_tensor(res[u][:], q, term[u][0][:], ALU.subtract).then_inc(r1_done, 1)
                        dve.wait_ge(mid_done, s + 1)
                        nc.vector.tensor_tensor(term[u][2][:], res[u][:], term[u][1][:], ALU.subtract).then_inc(lo_done, 1)

            @block.gpsimd
            def _(pool):
                with pool.Fori(0, NB) as b:
                    for u in range(2):
                        s = 2 * b + u
                        pool.wait_ge(qk_out, s + 1)
                        sinb = w.rope[:, 1:2, u * ST:(u + 1) * ST].to_broadcast([P, 2, ST])
                        nc.gpsimd.tensor_tensor(raw[u][:, 2:4, :], raw[u][:, 2:4, :], sinb, ALU.mult).then_inc(sin_done, 1)

            @block.scalar
            def _(act):
                count = act.alloc_register("qkv_count")
                with act.Fori(0, NB) as b:
                    for u in range(2):
                        s = 2 * b + u
                        wait_before(act, count, tr_done, s + 1, norm_done)
                        nc.scalar.activation(hT[u][:], pT[:, u, :], ACT.Identity, bias=w.mod[:, 0, 0, bass.ds(b, 1)],
                                             scale=w.mod[:, 0, 1, bass.ds(b, 1)]).then_inc(h_done, 1)
                        act.wait_ge(qk_ps, s + 1)
                        act.wait_ge(lo_done, s)
                        for n in range(4):
                            ins = nc.scalar.activation(raw[u][:, n, :], pq[:, n, :], ACT.Identity,
                                                       bias=w.bqk[:, (0, 2, 1, 3)[n]:(0, 2, 1, 3)[n] + 1])
                        ins.then_inc(qk_out, 1)
                        act.wait_ge(rope_done, s + 1)
                        act.wait_ge(stored[u], b * 16 * 2 * TERMS)
                        nc.scalar.copy(term[u][0][:], raw[u][:, 0:2, :]).then_inc(hi_done, 1)
                        act.wait_ge(r1_done, s + 1)
                        nc.scalar.copy(term[u][1][:], res[u][:]).then_inc(mid_done, 1)

            @block.tensor
            def _(pe):
                with pe.Fori(0, NB) as b:
                    for u in range(2):
                        s = 2 * b + u
                        pe.wait_ge(norm_done, s + 1)
                        pe.wait_ge(h_done, s)
                        for j in range(4):
                            ins = nc.tensor.transpose(pT[:, u, j * C:(j + 1) * C], xn[u][:, j, :], w.ident[:])
                        ins.then_inc(tr_done, 1)
                        pe.wait_ge(h_done, s + 1)
                        pe.wait_ge(qk_out, s)
                        for n, wt in enumerate((w.wqkv[:, 0:C], w.wqkv[:, C:2 * C], w.wrot[:, 0:C], w.wrot[:, C:2 * C])):
                            ins = nc.tensor.matmul(pq[:, n, :], wt, hT[u][:], start=True, stop=True)
                        ins.then_inc(qk_ps, 1)
                        pe.wait_ge(v_out, s)
                        for j in range(4):
                            ins = nc.tensor.matmul(pv[:, u, j * C:(j + 1) * C], hT[u][:, j * C:(j + 1) * C],
                                                   w.wqkv[:, 2 * C:3 * C], start=True, stop=True)
                        ins.then_inc(v_ps, 1)

            @block.sync
            def _(sp):
                with sp.Fori(0, NB) as b:
                    for u in range(2):
                        s = 2 * b + u
                        sp.wait_ge(lo_done, s + 1)
                        for side, terms in ((0, QT), (1, KT)):
                            for r in range(TERMS):
                                dst = d.qk[side].rearrange("(b g) r e t -> b r g e t", b=NB)[bass.ds(b, 1), r, :, :, u * ST:(u + 1) * ST]
                                sp.dma_start(dst, term[u][terms[r]][:, side, :]).then_inc(stored[u], 16)
                for u in range(2):
                    sp.wait_ge(stored[u], NB * 16 * 2 * TERMS)


CHUNKS = [
    (0, [(0, 0, 512, 0)]),
    (0, [(1, 128, 384, 0), (3, 384, 128, 384)]),
    (0, [(2, 256, 256, 0)]),
    (1, [(0, 512, 512, 0)]), (1, [(1, 512, 512, 0)]), (1, [(2, 512, 512, 0)]), (1, [(3, 512, 512, 0)]),
    (1, [(4, 512, 512, 0)]),
    (1, [(5, 640, 384, 0), (7, 896, 128, 384)]),
    (1, [(6, 768, 256, 0)]),
]
NCH = len(CHUNKS)
HALF_END = [2, 9]
SITEMS = ([(0, [0, 1, 2, 3], 128), (1, [0, 1, 2, 3], 256), (2, [0, 1], 512), (2, [2, 3], 512), (3, [0, 1], 512), (3, [2, 3], 512)]
          + [(i, [h], 1024) for i in range(4, 8) for h in range(4)])
PLAN = {c: [] for c in range(NCH)}
for _n, _it in enumerate(sorted(range(len(SITEMS)), key=lambda n: SITEMS[n][0])):
    PLAN[min(_n * 8 // len(SITEMS), 7)].append(_it)
MAXT, O0, O1 = "max", "o0", "o1"


def items_of(first, nxt):
    out = []
    for c in range(NCH):
        here = [("s", n) for n in PLAN[c]] if nxt else []
        if c == 2 and not first:
            here.append((O1, None))
        if c == 6:
            here.append((O0, None))
        if c == 8 and nxt:
            here.append((MAXT, None))
        out.append(here)
    return out


def attention_phase(nc, w, d):
    with ExitStack() as ctx:
        sb = lambda n, s, t=F32: ctx.enter_context(nc.sbuf_tensor(n, s, t))
        ps = lambda n, s, t=F32: ctx.enter_context(nc.psum_tensor(n, s, t))
        sem = lambda n: semaphore_of(nc, ctx, n)
        qa = [sb(f"qa{p}", [P, HQ, T], BF16) for p in range(2)]
        ka = [sb(f"ka{p}", [P, HQ, T], BF16) for p in range(2)]
        qb = [sb(f"qb{p}", [P, HQ, T], BF16) for p in range(2)]
        kb = [sb(f"kb{p}", [P, HQ, T], BF16) for p in range(2)]
        vs = [sb(f"vs{p}", [P, TPB, HQ, 32]) for p in range(2)]
        prob = [sb(f"prob{p}", [P, HQ, ST]) for p in range(2)]
        osb = [sb(f"osb{p}", [P, ST]) for p in range(2)]
        part = [sb(f"part{p}", [P, HQ, TPB]) for p in range(2)]
        mrow = [sb(f"mrow{p}", [HQ * TPB, 2, P], BF16) for p in range(2)]
        rec = [sb(f"rec{p}", [P, 4, HQ]) for p in range(2)]
        sps = [ps(f"sps{p}", [P, 2 * ST]) for p in range(2)]
        tps = ps("tps", [P, 3, ST])
        ops = ps("ops", [P, ST])
        s_ready, s_free, t_ready, exp_done, masked = sem("s_ready"), sem("s_free"), sem("t_ready"), sem("exp_done"), sem("masked")
        pv_done, o_out, v_copied, rec_done, zeroed = (sem("pv_done"), sem("o_out"), sem("v_copied"),
                                                     sem("rec_done"), sem("zeroed"))
        max_hi, ones_set = sem("max_hi"), sem("ones_set")
        a_in = [sem(f"a_in{p}") for p in range(2)]
        b_in = [sem(f"b_in{p}") for p in range(2)]
        m_in = [sem(f"m_in{p}") for p in range(2)]

        NS = len(SITEMS)
        first_items = sum(len(x) for x in items_of(True, True))
        body_items = sum(len(x) for x in items_of(False, True))

        def item_base(t):
            return (NS + 1) if isinstance(t, int) and t == 0 else (NS + 1 + first_items - body_items) + body_items * t

        def sched(t, p, first, nxt):
            return items_of(first, nxt)

        mask_count = [0]
        for half, parts in CHUNKS:
            mask_count.append(mask_count[-1] + sum(1 for j, q0, n, col in parts if q0 == j * P))
        NM = mask_count[-1]

        def bodies(eng, body):
            body(0, 0, True, True)
            with eng.Fori(0, (NQUAD - 2) // 2) as i:
                body(2 * i + 1, 1, False, True)
                body(2 * i + 2, 0, False, True)
            body(NQUAD - 1, 1, False, False)

        with nc.Block() as block:
            @block.gpsimd
            def _(pool):
                for p in range(2):
                    for z in (qa[p], ka[p], qb[p], kb[p]):
                        pool.memset(z[:].rearrange("p h t -> p (h t)").bitcast(F32), 0.0)
                    ins = pool.memset(vs[p][:], 0.0)
                ins.then_inc(zeroed, 1)
                pool.wait_ge(zeroed, 1)
                for p in range(2):
                    ins = pool.memset(vs[p][:, :, :, HD:HD + 1], 1.0)
                ins.then_inc(zeroed, 1)
                pool.wait_ge(zeroed, 2)

                def copy_v(t, p):
                    src = w.v[:, t] if isinstance(t, int) else w.v[:, bass.ds(t, 1)][:, 0]
                    nc.gpsimd.tensor_copy(vs[p][:, :, :, 0:HD], src.rearrange("p k (h e) -> p k h e", h=HQ)).then_inc(v_copied, 1)

                def body(t, p, first, nxt):
                    for c, (half, parts) in enumerate(CHUNKS):
                        if mask_count[c + 1] > mask_count[c]:
                            wait_before(pool, count, exp_done, 4 * NCH * t + 4 * (c + 1), t_ready)
                        for j, q0, n, col in parts:
                            if q0 == j * P:
                                blk = prob[c % 2][:, :, col:col + P]
                                nc.gpsimd.affine_select(out=blk, in_=blk, pattern=[[0, HQ], [1, P]], compare_op=ALU.is_ge,
                                                        fill=0.0, base=0, channel_multiplier=-1).then_inc(masked, 1)
                        if c == 2 and nxt:
                            if not (isinstance(t, int) and t == 0):
                                pool.wait_ge(pv_done, NCH * t)
                            copy_v(t + 1, 1 - p)
                count = pool.alloc_register("exp_count")
                copy_v(0, 0)
                bodies(pool, body)

            @block.sync
            def _(sp):
                def load(t, p, s_in, qq, kk):
                    for side, buf in ((0, qq), (1, kk)):
                        src = d.qk[side].rearrange("(t h) r e n -> t (r e) h n", h=HQ)
                        src = src[t] if isinstance(t, int) else src[bass.ds(t, 1)][0]
                        sp.dma_start(buf[0:KR, :, :], src).then_inc(s_in, 16)

                sp.wait_ge(zeroed, 1)
                sp.wait_ge(ones_set, 1)
                load(0, 0, a_in[0], qa[0], ka[0])
                load(0, 0, b_in[0], qb[0], kb[0])
                load(1, 1, a_in[1], qa[1], ka[1])
                load(1, 1, b_in[1], qb[1], kb[1])

                def max_to_rows(n, p):
                    sp.wait_ge(s_free, item_base(n))
                    for r in range(2):
                        sp.dma_start(qb[p][MROW + r:MROW + r + 1, :, :].rearrange("o h (k q) -> o (h k) q", k=TPB),
                                     mrow[p][:, r, :]).then_inc(m_in[p], 16)
                max_to_rows(0, 0)

                def body(t, p, first, nxt):
                    if nxt:
                        tn = t + 2
                        if not isinstance(t, int):
                            tn = (t + 2) & (NQUAD - 1)
                        load(tn, p, a_in[p], qa[p], ka[p])
                    if nxt:
                        max_to_rows(t + 1, 1 - p)
                        sp.wait_ge(t_ready, 4 * NCH * (t + 1))
                        load(tn, p, b_in[p], qb[p], kb[p])
                bodies(sp, body)
                for p in range(2):
                    sp.wait_ge(a_in[p], 32 * (NQUAD // 2 + (1 if p == 0 else 0)))
                    sp.wait_ge(b_in[p], 32 * (NQUAD // 2 + (1 if p == 0 else 0)))

            @block.tensor
            def _(pe):
                item = [0, 0]

                def slot():
                    return sps[(item[1] + par[0]) % 2]

                par = [0]

                def acquire():
                    n = item[0] + item[1]
                    if not (isinstance(n, int) and n < 2):
                        pe.wait_ge(s_free, n - 1)

                def filled(ins):
                    ins.then_inc(s_ready, 1)
                    item[1] += 1

                def s_item(n, p):
                    i, heads, step = SITEMS[n]
                    acquire()
                    out = slot()
                    for x, h in enumerate(heads):
                        for c0 in range(0, (i + 1) * P, ST):
                            n1 = min(ST, (i + 1) * P - c0)
                            diag = c0 + n1 == (i + 1) * P
                            ins = nc.tensor.matmul(out[:, x * step + c0:x * step + c0 + n1], qa[p][:, h, i * P:(i + 1) * P],
                                                   ka[p][:, h, c0:c0 + n1], start=True, stop=not diag, skip_group_check=True)
                        e = x * step + i * P
                        ins = nc.tensor.matmul(out[:, e:e + P], w.identb[:], w.maskb[:], start=False, stop=True, skip_group_check=True)
                    filled(ins)

                def max_item(n, p, last):
                    pe.wait_ge(s_free, last)
                    acquire()
                    filled(nc.tensor.transpose(slot()[0:HQ * TPB, 0:P], part[p][:].rearrange("p h k -> p (h k)"), w.ident[:]))

                def o_item(half, count):
                    pe.wait_ge(o_out, count)
                    acquire()
                    out = slot()
                    for x in range(4):
                        ins = nc.tensor.transpose(out[:, x * P:(x + 1) * P], osb[half][:, x * P:(x + 1) * P], w.ident[:])
                    filled(ins)

                def pv(t, p, c):
                    half, parts = CHUNKS[c]
                    if mask_count[c + 1] > mask_count[c]:
                        pe.wait_ge(masked, NM * t + mask_count[c + 1])
                    else:
                        pe.wait_ge(exp_done, 4 * NCH * t + 4 * (c + 1))
                    if c == 0:
                        pe.wait_ge(v_copied, t + 1)
                    new = c == 0 or c == HALF_END[0] + 1
                    if new:
                        n = 2 * t + half
                        if not (isinstance(n, int) and n == 0):
                            pe.wait_ge(o_out, n)
                    for j, q0, n, col in parts:
                        o0 = q0 - half * ST
                        for h in range(HQ):
                            ins = nc.tensor.matmul(ops[32 * h:32 * h + 32, o0:o0 + n], vs[p][:, j, h, :],
                                                   prob[c % 2][:, h, col:col + n], start=new, stop=c in HALF_END,
                                                   skip_group_check=True, tile_position=(0, 32 * h))
                    ins.then_inc(pv_done, 1)

                def body(t, p, first, nxt):
                    base = item_base(t)
                    item[0], item[1] = base, 0
                    par[0] = (NS + 1 + (0 if first else first_items) + (0 if first or p == 1 else body_items)) % 2
                    todo = items_of(first, nxt)
                    done = 0
                    for c, (half, parts) in enumerate(CHUNKS):
                        if c == 0:
                            pe.wait_ge(b_in[p], t_loads(t, p))
                            pe.wait_ge(m_in[p], t_max(t, p))
                        todo_c = list(todo[c])
                        for h in range(HQ):
                            k = 4 * c + h
                            prev = 4 * NCH * t + k - 2 if k >= 3 else 4 * NCH * (t - 1) + {0: 40, 1: 38, 2: 39}[k]
                            if not (isinstance(prev, int) and prev <= 0):
                                pe.wait_ge(exp_done, prev)
                            for j, q0, n, col in parts:
                                ins = nc.tensor.matmul(tps[:, k % 3, col:col + n], kb[p][:, h, j * P:(j + 1) * P],
                                                       qb[p][:, h, q0:q0 + n], start=True, stop=True)
                            ins.then_inc(t_ready, 1)
                            if h in (1, 2) and todo_c and todo_c[0][0] == "s":
                                if done == 0:
                                    pe.wait_ge(a_in[1 - p], a_loads(t + 1, 1 - p))
                                s_item(todo_c.pop(0)[1], 1 - p)
                                done = item[1]
                        if c > 0:
                            pv(t, p, c - 1)
                        elif not first:
                            pv(t - 1, 1 - p, NCH - 1)
                        for kind, n in todo_c:
                            if kind == "s":
                                s_item(n, 1 - p)
                                done = item[1]
                            elif kind == O1:
                                o_item(1, 2 * t)
                            elif kind == O0:
                                o_item(0, 2 * t + 1)
                            else:
                                max_item(t + 1, 1 - p, base + done)

                def t_loads(t, p):
                    return 32 * (t // 2 + 1) if isinstance(t, int) else 16 * (t - p) + 32

                a_loads = t_loads

                def t_max(t, p):
                    return t_loads(t, p)

                pe.wait_ge(a_in[0], 32)
                for n in range(NS):
                    s_item(n, 0)
                max_item(0, 0, NS)
                bodies(pe, body)
                t = NQUAD - 1
                pv(t, 1, NCH - 1)
                o_item(1, 2 * NQUAD)

            @block.scalar
            def _(act):
                def o_copy(half):
                    nc.scalar.copy(osb[half][:], ops[:]).then_inc(o_out, 1)

                def body(t, p, first, nxt):
                    for c, (half, parts) in enumerate(CHUNKS):
                        n = sum(x[2] for x in parts)
                        for h in range(HQ):
                            k = 4 * c + h
                            act.wait_ge(t_ready, 4 * NCH * t + k + 1)
                            if h == 0:
                                v = NCH * t + c - 1
                                if not (isinstance(v, int) and v <= 0):
                                    act.wait_ge(pv_done, v)
                            nc.scalar.activation(prob[c % 2][:, h, 0:n], tps[:, k % 3, 0:n], ACT.Exp,
                                                 scale=float(HD) ** -0.5).then_inc(exp_done, 1)
                        if c == 0 and not first:
                            act.wait_ge(pv_done, NCH * t)
                            o_copy(1)
                        if c == 3:
                            act.wait_ge(pv_done, NCH * t + 3)
                            o_copy(0)
                bodies(act, body)
                act.wait_ge(pv_done, NCH * NQUAD)
                o_copy(1)

            @block.vector
            def _(dve):
                item = [0, 0]
                par = [0]

                def ready():
                    dve.wait_ge(s_ready, item[0] + item[1] + 1)
                    return sps[(item[1] + par[0]) % 2]

                def freed(ins):
                    ins.then_inc(s_free, 1)
                    item[1] += 1

                def s_item(n, p):
                    i, heads, step = SITEMS[n]
                    src = ready()
                    wd = (i + 1) * P
                    if len(heads) > 1:
                        src = src[:, 0:len(heads) * step].rearrange("p (h k) -> p h k", h=len(heads))[:, :, 0:wd]
                    else:
                        src = src[:, 0:wd].rearrange("p (h k) -> p h k", h=1)
                    freed(nc.vector.tensor_reduce(part[p][:, heads[0]:heads[-1] + 1, i:i + 1].rearrange("p h o -> p (h o)"),
                                                  src, AX.X, ALU.max, negate=True))

                def max_item(n, p):
                    src = ready()
                    nc.vector.tensor_copy(mrow[p][:, 0, :], src[0:HQ * TPB, 0:P]).then_inc(max_hi, 1)
                    dve.wait_ge(max_hi, n + 1)
                    ins = nc.vector.tensor_tensor(mrow[p][:, 1, :], src[0:HQ * TPB, 0:P], mrow[p][:, 0, :], ALU.subtract)
                    freed(ins)

                def o_item(t, half):
                    src = ready()[:, 0:ST].rearrange("p (x h e) -> p x h e", x=4, h=HQ)
                    nc.vector.reciprocal(rec[half][:], src[:, :, :, HD]).then_inc(rec_done, 1)
                    dve.wait_ge(rec_done, 2 * t + half + 1)
                    dst = (w.y[:, t] if isinstance(t, int) else w.y[:, bass.ds(t, 1)][:, 0])[:, half * 4:half * 4 + 4, :]
                    recb = rec[half][:].rearrange("p x (h o) -> p x h o", o=1).to_broadcast([P, 4, HQ, HD])
                    freed(nc.vector.tensor_tensor(dst.rearrange("p x (h e) -> p x h e", h=HQ), src[:, :, :, 0:HD], recb, ALU.mult))

                def body(t, p, first, nxt):
                    item[0], item[1] = item_base(t), 0
                    par[0] = (NS + 1 + (0 if first else first_items) + (0 if first or p == 1 else body_items)) % 2
                    for here in items_of(first, nxt):
                        for kind, n in here:
                            if kind == "s":
                                s_item(n, 1 - p)
                            elif kind == O1:
                                o_item(t - 1, 1)
                            elif kind == O0:
                                o_item(t, 0)
                            else:
                                max_item(t + 1, 1 - p)
                dve.wait_ge(zeroed, 1)
                for p in range(2):
                    ins = nc.vector.memset(kb[p][MROW:MROW + 2, :, :], 1.0)
                ins.then_inc(ones_set, 1)
                for n in range(NS):
                    s_item(n, 0)
                max_item(0, 0)
                bodies(dve, body)
                o_item(NQUAD - 1, 1)


def project_phase(nc, w, d):
    with ExitStack() as ctx:
        sb = lambda n, s, t=F32: ctx.enter_context(nc.sbuf_tensor(n, s, t))
        ps = lambda n, s, t=F32: ctx.enter_context(nc.psum_tensor(n, s, t))
        sem = lambda n: semaphore_of(nc, ctx, n)
        ys = [sb(f"ys{u}", [P, 4, C]) for u in range(2)]
        yT = [sb(f"yT{u}", [P, ST]) for u in range(2)]
        o = [sb(f"o{u}", [P, 4, C]) for u in range(2)]
        pT = ps("pTo", [P, 2, ST])
        po = ps("po", [P, 2, ST])
        y_in, y_tr, y_T, o_ps, o_step, x_done = sem("y_in"), sem("y_tr"), sem("y_T"), sem("o_ps"), sem("o_step"), sem("x_done")
        with nc.Block() as block:
            @block.scalar
            def _(act):
                with act.Fori(0, NB) as b:
                    for u in range(2):
                        s = 2 * b + u
                        act.wait_ge(y_tr, s)
                        yb = w.y[:].rearrange("p (b q) k c -> p b k q c", q=NQ)[:, bass.ds(b, 1), u * 4:u * 4 + 4, :, :]
                        for j in range(4):
                            ins = nc.scalar.copy(ys[u][:, j, :].rearrange("p (q c) -> p q c", q=NQ), yb[:, 0, j])
                        ins.then_inc(y_in, 1)

            @block.tensor
            def _(pe):
                with pe.Fori(0, NB) as b:
                    for u in range(2):
                        s = 2 * b + u
                        pe.wait_ge(y_in, s + 1)
                        pe.wait_ge(y_T, s)
                        for j in range(4):
                            ins = nc.tensor.transpose(pT[:, u, j * C:(j + 1) * C], ys[u][:, j, :], w.ident[:])
                        ins.then_inc(y_tr, 1)
                        pe.wait_ge(y_T, s + 1)
                        pe.wait_ge(x_done, s)
                        for j in range(4):
                            ins = nc.tensor.matmul(po[:, u, j * C:(j + 1) * C], yT[u][:, j * C:(j + 1) * C], w.wo[:], start=True, stop=True)
                        ins.then_inc(o_ps, 1)

            @block.vector
            def _(dve):
                with dve.Fori(0, NB) as b:
                    for u in range(2):
                        s = 2 * b + u
                        dve.wait_ge(y_tr, s + 1)
                        nc.vector.tensor_copy(yT[u][:], pT[:, u, :]).then_inc(y_T, 1)
                        dve.wait_ge(o_ps, s + 1)
                        link = Chain(dve, o_step, 2 * s)
                        bo4 = w.bo[:].rearrange("p (o c) -> p o c", o=1).to_broadcast([P, 4, C])
                        link(nc.vector.tensor_tensor(o[u][:], po[:, u, :].rearrange("p (j c) -> p j c", j=4), bo4, ALU.add))
                        g4 = w.gate[:, 0, bass.ds(b, 1), :].to_broadcast([P, 4, C])
                        link(nc.vector.tensor_tensor(o[u][:], o[u][:], g4, ALU.mult))
                        xs = w.x[:, bass.ds(b * TPB + u * 4, 4), :]
                        nc.vector.tensor_tensor(xs, xs, o[u][:], ALU.add).then_inc(x_done, 1)


def stats_phase(nc, w, name):
    with ExitStack() as ctx:
        st_step, root = semaphore_of(nc, ctx, f"st_step{name}"), semaphore_of(nc, ctx, f"root{name}")
        with nc.Block() as block:
            @block.vector
            def _(dve):
                link = Chain(dve, st_step)
                link(layernorm_stats(nc, dve, link, w.x, w))
                dve.wait_ge(root, 1)
                nc.vector.reciprocal(w.rstd[:], w.t1[:])

            @block.scalar
            def _(act):
                act.wait_ge(st_step, 8)
                nc.scalar.activation(w.t1[:], w.t1[:], ACT.Sqrt).then_inc(root, 1)


NE = 8
SI = 352
NSLOT = 2 * NT + NE
UN = 4


def chunks_of(width):
    return {176: [88, 88], 352: [128, 128, 96]}[width]


def weights_phase(nc, w, d, layer):
    I = (176, 352)[layer]
    NK = layer + 1
    with ExitStack() as ctx:
        sb = lambda n, s, t=F32: ctx.enter_context(nc.sbuf_tensor(f"{n}_w{layer}", s, t))
        ps = lambda n, s, t=F32: ctx.enter_context(nc.psum_tensor(f"{n}_w{layer}", s, t))
        sem = lambda n: semaphore_of(nc, ctx, f"{n}_w{layer}")
        R = 88
        rows = [sb(f"rows{u}", [R, 3, 4, C]) for u in range(2)]
        dn = [sb(f"dn{u}", [P, 352]) for u in range(2)]
        gp = ps("gp", [P, 3, ST])
        dp = ps("dp", [P, ST])
        w_in = [sem(f"w_in{u}") for u in range(2)]
        w_tr, w_out = sem("w_tr"), sem("w_out")
        const = lambda e: isinstance(e, int)
        ups, down = ((d.gu0,), d.dn0) if layer == 0 else ((d.w1, d.w2), d.w3)
        at = lambda a, e: a[:, e] if const(e) else a[:, bass.ds(e, 1)][:, 0]

        def turns(eng, turn, last):
            turn(0, 0)
            turn(1, 1)
            with eng.Fori(1, NE // 2) as i:
                for u in range(2):
                    turn(2 * i + u, u)
            last()

        with nc.Block() as block:
            @block.sync
            def _(sp):
                def turn(e, u):
                    if not (const(e) and e < 2):
                        sp.wait_ge(w_tr, e - 1)
                    pick = lambda a: a[e] if const(e) else a[bass.ds(e, 1)][0]
                    for k, src in enumerate(ups):
                        sp.dma_start(rows[u][:, k], pick(src).rearrange("(n p) c -> p n c", p=R)).then_inc(w_in[u], 16)
                    sp.dma_start(dn[u][:, 0:I], pick(down)).then_inc(w_in[u], 16)

                def last():
                    sp.wait_ge(w_tr, NE - 1)
                    sp.dma_start(rows[0][0:NE, 2, 0, :], (d.gate_w, d.wg)[layer]).then_inc(w_in[0], 16)
                    if layer == 0:
                        for k, src in enumerate((d.sg, d.su)):
                            sp.dma_start(rows[0][:, k], src.rearrange("(n p) c -> p n c", p=R)).then_inc(w_in[0], 16)
                        sp.dma_start(rows[0][0:1, 2, 1, :], d.seg).then_inc(w_in[0], 16)
                        sp.dma_start(dn[0][:], d.sd).then_inc(w_in[0], 16)
                turns(sp, turn, last)

            @block.tensor
            def _(pe):
                def up_tr(u, k):
                    for m in range(4):
                        ins = nc.tensor.transpose(gp[:, k, m * R:(m + 1) * R], rows[u][:, k, m, :], w.ident[0:R, 0:R])
                    return ins

                def down_tr(u, width):
                    c0 = 0
                    for m, cw in enumerate(chunks_of(width)):
                        ins = nc.tensor.transpose(dp[0:cw, m * C:(m + 1) * C], dn[u][:, c0:c0 + cw], w.ident[:])
                        c0 += cw
                    return ins

                def turn(e, u):
                    n = 16 * (NK + 1)
                    pe.wait_ge(w_in[u], n * (e // 2 + 1) if const(e) else (e - u) * (n // 2) + n)
                    pe.wait_ge(w_out, e)
                    for k in range(NK):
                        up_tr(u, k)
                    down_tr(u, I).then_inc(w_tr, 1)

                def last():
                    pe.wait_ge(w_in[0], 16 * (NK + 1) * (NE // 2) + 16 * (5 if layer == 0 else 1))
                    pe.wait_ge(w_out, NE)
                    ins = nc.tensor.transpose(gp[:, 2, 0:NE], rows[0][0:NE, 2, 0, :], w.ident[0:NE, 0:NE])
                    if layer == 0:
                        nc.tensor.transpose(gp[:, 2, NE:NE + 1], rows[0][0:1, 2, 1, :], w.ident[0:1, 0:1])
                        up_tr(0, 0)
                        up_tr(0, 1)
                        ins = down_tr(0, SI)
                    ins.then_inc(w_tr, 1)
                turns(pe, turn, last)

            @block.vector
            def _(dve):
                def down_out(dst, width):
                    cs = chunks_of(width)
                    full = [m for m, cw in enumerate(cs) if cw == cs[0]]
                    ins = nc.vector.tensor_copy(dst[0:cs[0], 0:len(full), :], dp[0:cs[0], 0:len(full) * C].rearrange("p (m c) -> p m c", c=C))
                    if len(full) < len(cs):
                        ins = nc.vector.tensor_copy(dst[0:cs[-1], len(full), :], dp[0:cs[-1], len(full) * C:len(cs) * C])
                    return ins

                def turn(e, u):
                    dve.wait_ge(w_tr, e + 1)
                    nc.vector.tensor_copy(at(w.up, e), gp[:, 0:NK, 0:352])
                    down_out(at(w.down, e), I).then_inc(w_out, 1)

                def last():
                    dve.wait_ge(w_tr, NE + 1)
                    nc.vector.tensor_copy(w.rt[:], gp[:, 2, 0:w.rt.shape[1]])
                    if layer == 0:
                        nc.vector.tensor_copy(w.shgu[:], gp[:, 0:2, 0:352])
                        down_out(w.shd, SI)
                turns(dve, turn, last)


def route_phase(nc, w, d, layer):
    NR = NE + 1 if layer == 0 else NE
    cols = [128, 128, 96]
    with ExitStack() as ctx:
        sb = lambda n, s, t=F32: ctx.enter_context(nc.sbuf_tensor(f"{n}_{layer}", s, t))
        ps = lambda n, s, t=F32: ctx.enter_context(nc.psum_tensor(f"{n}_{layer}", s, t))
        sem = lambda n: semaphore_of(nc, ctx, f"{n}_{layer}")
        hs = [sb(f"hs{u}", [P, 4, C]) for u in range(2)]
        hT = [sb(f"hTr{u}", [P, ST]) for u in range(2)]
        sg = [sb(f"sg{u}", [P, SI]) for u in range(2)]
        hid = [sb(f"hid{u}", [P, SI]) for u in range(2)]
        hidT = [sb(f"hidT{u}", [P, 3, P]) for u in range(2)]
        lg = sb("lg", [P, NT, NR])
        pT = ps("pTr", [P, 2, ST])
        pl = ps("pl", [P, ST])
        pg = ps("pg", [P, 2, ST])
        ph = ps("ph", [P, ST])
        pd = ps("pd", [P, ST])
        r_step, h_done, h_kept, tr_done, hT_done, lg_ps, lg_out = (sem("r_step"), sem("h_done"), sem("h_kept"), sem("tr_done"),
                                                                  sem("hT_done"), sem("lg_ps"), sem("lg_out"))
        g_ps, s_done, hid_done, hidT_ps, hidT_done, d_ps, sh_out = (sem("g_ps"), sem("s_done"), sem("hid_done"), sem("hidT_ps"),
                                                                   sem("hidT_done"), sem("d_ps"), sem("sh_out"))
        with nc.Block() as block:
            @block.vector
            def _(dve):
                with dve.Fori(0, NB) as b:
                    for u in range(2):
                        s = 2 * b + u
                        dve.wait_ge(tr_done, s)
                        dve.wait_ge(h_kept, s)
                        link = Chain(dve, r_step, 2 * s)
                        for j in range(4):
                            t = b * TPB + u * 4 + j
                            ins = nc.vector.tensor_scalar(hs[u][:, j, :], w.x[:, t, :], w.mean[:, bass.ds(t, 1)],
                                                          w.rstd[:, bass.ds(t, 1)], ALU.subtract, ALU.mult)
                        link(ins)
                        link(nc.vector.tensor_tensor(hs[u][:], hs[u][:], w.modr[:, 2 * layer + 1, bass.ds(b, 1), :].to_broadcast([P, 4, C]), ALU.mult))
                        nc.vector.tensor_tensor(hs[u][:], hs[u][:], w.modr[:, 2 * layer, bass.ds(b, 1), :].to_broadcast([P, 4, C]), ALU.add).then_inc(h_done, 1)
                        dve.wait_ge(lg_ps, s + 1)
                        nc.vector.tensor_copy(lg[:, bass.ds(b * TPB + u * 4, 4), :],
                                              pl[:, 0:4 * NR].rearrange("p (j r) -> p j r", j=4)).then_inc(lg_out, 1)
                        if layer == 0:
                            for j in range(4):
                                n = 4 * s + j
                                dve.wait_ge(s_done, n + 1)
                                nc.vector.tensor_tensor(hid[j % 2][:], sg[j % 2][:], pg[:, 1, 0:SI], ALU.mult).then_inc(hid_done, 1)
                                dve.wait_ge(hidT_ps, n + 1)
                                nc.vector.tensor_copy(hidT[j % 2][:, 0:2, :], ph[:, 0:256].rearrange("p (m c) -> p m c", m=2))
                                nc.vector.tensor_copy(hidT[j % 2][0:96, 2, :], ph[0:96, 256:384]).then_inc(hidT_done, 1)

            @block.gpsimd
            def _(pool):
                with pool.Fori(0, NB) as b:
                    for u in range(2):
                        pool.wait_ge(h_done, 2 * b + u + 1)
                        nc.gpsimd.tensor_copy(w.h[:, bass.ds(b * TPB + u * 4, 4), :], hs[u][:]).then_inc(h_kept, 1)

            @block.scalar
            def _(act):
                with act.Fori(0, NB) as b:
                    for u in range(2):
                        s = 2 * b + u
                        act.wait_ge(tr_done, s + 1)
                        nc.scalar.copy(hT[u][:], pT[:, u, :]).then_inc(hT_done, 1)
                        if layer == 0:
                            for j in range(4):
                                n = 4 * s + j
                                act.wait_ge(g_ps, n + 1)
                                nc.scalar.activation(sg[j % 2][:], pg[:, 0, 0:SI], ACT.Silu).then_inc(s_done, 1)
                                act.wait_ge(d_ps, n + 1)
                                nc.scalar.copy(w.sh[:, bass.ds(b * TPB + u * 4 + j, 1), :].rearrange("p o c -> p (o c)"), pd[:, 0:C]).then_inc(sh_out, 1)

            @block.tensor
            def _(pe):
                with pe.Fori(0, NB) as b:
                    for u in range(2):
                        s = 2 * b + u
                        pe.wait_ge(h_done, s + 1)
                        pe.wait_ge(hT_done, s)
                        for j in range(4):
                            ins = nc.tensor.transpose(pT[:, u, j * C:(j + 1) * C], hs[u][:, j, :], w.ident[:])
                        ins.then_inc(tr_done, 1)
                        pe.wait_ge(hT_done, s + 1)
                        pe.wait_ge(lg_out, s)
                        for j in range(4):
                            ins = nc.tensor.matmul(pl[:, j * NR:(j + 1) * NR], hT[u][:, j * C:(j + 1) * C], w.rt[:],
                                                   start=True, stop=True)
                        ins.then_inc(lg_ps, 1)
                        if layer == 0:
                            for j in range(4):
                                n = 4 * s + j
                                pe.wait_ge(hid_done, n)
                                for k in range(2):
                                    ins = nc.tensor.matmul(pg[:, k, 0:SI], hT[u][:, j * C:(j + 1) * C], w.shgu[:, k, :], start=True, stop=True)
                                ins.then_inc(g_ps, 1)
                                pe.wait_ge(hid_done, n + 1)
                                pe.wait_ge(hidT_done, n)
                                c0 = 0
                                for m, cw in enumerate(cols):
                                    ins = nc.tensor.transpose(ph[0:cw, m * P:(m + 1) * P], hid[j % 2][:, c0:c0 + cw], w.ident[:])
                                    c0 += cw
                                ins.then_inc(hidT_ps, 1)
                                pe.wait_ge(hidT_done, n + 1)
                                pe.wait_ge(sh_out, n)
                                for m, cw in enumerate(cols):
                                    ins = nc.tensor.matmul(pd[:, 0:C], hidT[j % 2][0:cw, m, :], w.shd[0:cw, m, :], start=m == 0, stop=m == 2)
                                ins.then_inc(d_ps, 1)

        sc = sb("sc", [P, NT, NE])
        m1 = sb("m1", [P, NT])
        top = sb("top", [P, NT, 8])
        idx = sb("idx", [P, NT, 8], U32)
        idf = sb("idf", [P, NT, 2])
        hot = [sb(f"hot{k}", [P, NE, NT]) for k in range(2)]
        both = sb("both", [P, NE, NT], BF16)
        bsum = sb("bsum", [P, NE * NT])
        ones = sb("ones", [P, NE * NT])
        excl = sb("excl", [P, NE, NT])
        base = sb("base", [P, NE])
        nt = sb("nt", [P, NE])
        off = sb("off", [P, NE])
        tmp = sb("tmp", [P, NE, NT])
        slf = sb("slf", [P, NT])
        ge = sb("ge", [P, NSLOT, NE])
        te = sb("te", [P, NSLOT])
        pp = pg
        q_step, ex_done, both_done, pre_ps = sem("q_step"), sem("ex_done"), sem("both_done"), sem("pre_ps")
        slots_done, scattered = sem("slots_done"), sem("scattered")
        with nc.Block() as block:
            @block.vector
            def _(dve):
                link = Chain(dve, q_step)
                v = nc.vector
                if layer == 0:
                    link(v.tensor_reduce(m1[:], lg[:, :, 0:NE], AX.X, ALU.max))
                    link(v.tensor_tensor(sc[:], lg[:, :, 0:NE], m1[:].rearrange("p (t o) -> p t o", o=1).to_broadcast([P, NT, NE]), ALU.subtract))
                    dve.wait_ge(ex_done, 2)
                    link(v.tensor_scalar(w.shw[:], w.shw[:], 1.0, None, ALU.add))
                    link(v.reciprocal(w.shw[:], w.shw[:]))
                    link(v.tensor_reduce(m1[:], sc[:], AX.X, ALU.add))
                    link(v.reciprocal(m1[:], m1[:]))
                    link(v.tensor_tensor(sc[:], sc[:], m1[:].rearrange("p (t o) -> p t o", o=1).to_broadcast([P, NT, NE]), ALU.mult))
                else:
                    link(v.tensor_copy(sc[:], lg[:]))
                for t in range(NT):
                    ins = v.max(top[:, t, :], sc[:, t, :])
                link(ins)
                for t in range(NT):
                    ins = v.max_index(idx[:, t, :], top[:, t, :], sc[:, t, :])
                link(ins)
                link(v.tensor_copy(idf[:], idx[:, :, 0:2]))
                eb = w.iota[:, 0:NE].rearrange("p (e o) -> p e o", o=1).to_broadcast([P, NE, NT])
                for k in range(2):
                    ins = v.tensor_tensor(hot[k][:], eb, idf[:, :, k:k + 1].rearrange("p t o -> p o t").to_broadcast([P, NE, NT]), ALU.is_equal)
                link(ins)
                v.tensor_tensor(both[:], hot[0][:], hot[1][:], ALU.add).then_inc(both_done, 1)
                for k in range(2):
                    link(v.tensor_tensor(tmp[:], hot[k][:], sc[:].rearrange("p t e -> p e t"), ALU.mult))
                    link(v.tensor_reduce(w.wt[k][:], tmp[:].rearrange("p e t -> p t e"), AX.X, ALU.add))
                link(v.memset(ones[:], 1.0))
                dve.wait_ge(pre_ps, 1)
                link(v.tensor_copy(bsum[:], pp[:, 1, 0:NE * NT]))
                link(v.tensor_tensor_scan(out=excl[:].rearrange("p e t -> p (e t)"), data0=ones[:], data1=bsum[:], initial=0.0,
                                          op0=ALU.mult, op1=ALU.add))
                link(v.tensor_tensor(excl[:], excl[:], bsum[:].rearrange("p (e t) -> p e t", e=NE), ALU.subtract))
                link(v.tensor_copy(base[:], excl[:, :, 0]))
                link(v.tensor_reduce(nt[:], bsum[:].rearrange("p (e t) -> p e t", e=NE), AX.X, ALU.add))
                link(v.tensor_scalar(nt[:], nt[:], 63.5, 1.0 / P, ALU.add, ALU.mult))
                link(v.tensor_scalar(nt[:], nt[:], 12582912.0, 12582912.0, ALU.add, ALU.subtract))
                link(v.tensor_tensor_scan(out=off[:], data0=ones[:, 0:NE], data1=nt[:], initial=0.0, op0=ALU.mult, op1=ALU.add))
                link(v.tensor_tensor(ge[:], w.iota[:, 0:NSLOT].rearrange("p (i o) -> p i o", o=1).to_broadcast([P, NSLOT, NE]),
                                     off[:].rearrange("p (o e) -> p o e", o=1).to_broadcast([P, NSLOT, NE]), ALU.is_ge))
                link(v.tensor_reduce(te[:], ge[:], AX.X, ALU.add))
                link(v.tensor_scalar(w.tile_expert[:], te[:], float(NE - 1), None, ALU.min))
                link(v.tensor_tensor(off[:], off[:], nt[:], ALU.subtract))
                link(v.scalar_tensor_tensor(out=off[:], in0=off[:], scalar=float(P), in1=base[:], op0=ALU.mult, op1=ALU.subtract))
                link(v.tensor_tensor(excl[:], excl[:], off[:].rearrange("p (e o) -> p e o", o=1).to_broadcast([P, NE, NT]), ALU.add))
                link(v.tensor_tensor(excl[:], excl[:], pp[:, 0, 0:NE * NT].rearrange("p (e t) -> p e t", e=NE), ALU.add))
                for k in range(2):
                    link(v.tensor_tensor(tmp[:], hot[k][:], excl[:], ALU.mult))
                    link(v.tensor_reduce(slf[:], tmp[:].rearrange("p e t -> p t e"), AX.X, ALU.add))
                    link(v.tensor_copy(w.slot[k][:], slf[:]))
                dve.sem_inc(slots_done, 1)

            @block.scalar
            def _(act):
                if layer == 0:
                    act.wait_ge(q_step, 2)
                    nc.scalar.activation(sc[:], sc[:], ACT.Exp).then_inc(ex_done, 1)
                    nc.scalar.activation(w.shw[:], lg[:, :, NE], ACT.Exp, scale=-1.0).then_inc(ex_done, 1)

            @block.tensor
            def _(pe):
                pe.wait_ge(both_done, 1)
                nc.tensor.matmul(pp[:, 0, 0:NE * NT], w.trib[:], both[:].rearrange("p e t -> p (e t)"), start=True, stop=True)
                nc.tensor.matmul(pp[:, 1, 0:NE * NT], w.onesb[:], both[:].rearrange("p e t -> p (e t)"), start=True, stop=True).then_inc(pre_ps, 1)

            @block.gpsimd
            def _(pool):
                pool.wait_ge(slots_done, 1)
                for t in range(NT):
                    for k in range(2):
                        nc.gpsimd.indirect_dma_start(out=d.xg, out_offset=bass.IndirectOffsetOnAxis(ap=w.slot[k][:, t:t + 1], axis=0),
                                                     in_=w.h[:, t, :], in_offset=None).then_inc(scattered, 16)
                pool.wait_ge(scattered, 16 * 2 * NT)


def experts_phase(nc, w, d, layer):
    I = (176, 352)[layer]
    cols = chunks_of(I)
    M = len(cols)
    with ExitStack() as ctx:
        sb = lambda n, s, t=F32: ctx.enter_context(nc.sbuf_tensor(f"{n}_{layer}", s, t))
        ps = lambda n, s, t=F32: ctx.enter_context(nc.psum_tensor(f"{n}_{layer}", s, t))
        sem = lambda n: semaphore_of(nc, ctx, f"{n}_{layer}")
        xt = [sb(f"xt{u}", [P, C]) for u in range(UN)]
        xT = [sb(f"xT{u}", [P, P]) for u in range(UN)]
        sg = [sb(f"esg{u}", [P, I]) for u in range(2)]
        hid = [sb(f"ehid{u}", [P, I]) for u in range(2)]
        hidT = [sb(f"ehidT{u}", [P, M, P]) for u in range(2)]
        yo = [sb(f"yo{u}", [P, C]) for u in range(UN)]
        pT = ps("epT", [P, ST])
        pg = ps("epg", [P, 2, 2, ST])
        ph = ps("eph", [P, 2, ST])
        pd = ps("epd", [P, ST])
        g_of = lambda u: pg[:, u, 0, 0:I]
        u_of = lambda u: pg[:, u, 1, 0:I]
        x_in = [sem(f"xin{u}") for u in range(UN)]
        y_out = [sem(f"yout{u}") for u in range(UN)]
        in_ps, in_T, up_ps, s_done, hid_done, hid_ps, hid_T, dn_ps, y_done = (
            sem("in_ps"), sem("in_T"), sem("up_ps"), sem("s_done"), sem("ehid_done"), sem("hid_ps"), sem("hid_T"), sem("dn_ps"), sem("y_done"))
        const = lambda n: isinstance(n, int)

        def rows_of(a, n):
            v = a.rearrange("(i p) c -> i p c", p=P)
            return v[n] if const(n) else v[bass.ds(n, 1)][0]

        def after(eng, sem_, n):
            if not (const(n) and n <= 0):
                eng.wait_ge(sem_, n)

        def loop(eng, step):
            for u in range(UN):
                step(u, u)
            with eng.Fori(1, NSLOT // UN) as i:
                for u in range(UN):
                    step(UN * i + u, u)

        def skewed(eng, *stages):
            def step(n, u):
                for k, f in stages:
                    if not (const(n) and not 0 <= n + k < NSLOT):
                        f(n + k, (u + k) % UN)
            for n in range(UN):
                step(n, n)
            with eng.Fori(1, NSLOT // UN - 1) as i:
                for u in range(UN):
                    step(UN * i + u, u)
            for n in range(NSLOT - UN, NSLOT + 1):
                step(n, n % UN)

        with nc.Block() as block:
            @block.sync
            def _(sp):
                def step(n, u):
                    after(sp, in_ps, n - UN + 1)
                    sp.dma_start(xt[u][:], rows_of(d.xg, n)).then_inc(x_in[u], 16)
                loop(sp, step)

            @block.gpsimd
            def _(pool):
                def step(n, u):
                    pool.wait_ge(y_done, n + 1)
                    pool.dma_start(rows_of(d.yg, n), yo[u][:]).then_inc(y_out[u], 16)
                loop(pool, step)
                for u in range(UN):
                    pool.wait_ge(y_out[u], 16 * (NSLOT // UN))

            @block.scalar
            def _(act):
                def x_copy(n, u):
                    act.wait_ge(in_ps, n + 1)
                    nc.scalar.copy(xT[u][:], pT[:, 0:P]).then_inc(in_T, 1)

                def silu(n, u):
                    act.wait_ge(up_ps, n + 1)
                    nc.scalar.activation(sg[u % 2][:], g_of(u % 2), ACT.Silu).then_inc(s_done, 1)

                def y_copy(n, u):
                    act.wait_ge(dn_ps, n + 1)
                    if not (const(n) and n < UN):
                        act.wait_ge(y_out[u], 4 * (n - u))
                    nc.scalar.copy(yo[u][:], pd[:, 0:C]).then_inc(y_done, 1)

                x_copy(0, 0)
                x_copy(1, 1)
                silu(0, 0)
                skewed(act, (2, x_copy), (1, silu), (-1, y_copy))

            @block.vector
            def _(dve):
                def product(n, u):
                    dve.wait_ge(s_done, n + 1)
                    nc.vector.tensor_tensor(hid[u % 2][:], sg[u % 2][:], u_of(u % 2), ALU.mult).then_inc(hid_done, 1)

                def hid_copy(n, u):
                    dve.wait_ge(hid_ps, n + 1)
                    if I == 176:
                        ins = nc.vector.tensor_copy(hidT[u % 2][0:88, :, :], ph[0:88, u % 2, 0:M * P].rearrange("p (m c) -> p m c", m=M))
                    else:
                        nc.vector.tensor_copy(hidT[u % 2][:, 0:2, :], ph[:, u % 2, 0:2 * P].rearrange("p (m c) -> p m c", m=2))
                        ins = nc.vector.tensor_copy(hidT[u % 2][0:96, 2, :], ph[0:96, u % 2, 2 * P:3 * P])
                    ins.then_inc(hid_T, 1)

                product(0, 0)
                skewed(dve, (1, product), (0, hid_copy))

            @block.tensor
            def _(pe):
                def t_in(n, u):
                    if const(n):
                        pe.wait_ge(x_in[u], 16 * (n // UN + 1))
                    else:
                        pe.wait_ge(x_in[u], 4 * (n - u) + 16)
                    after(pe, in_T, n)
                    nc.tensor.transpose(pT[:, 0:P], xt[u][:], w.ident[:]).then_inc(in_ps, 1)

                def up(n, u):
                    e = pe.value_load(w.tile_expert[0:1, n:n + 1] if const(n) else w.tile_expert[0:1, bass.ds(n, 1)], min_val=0, max_val=NE - 1)
                    pe.wait_ge(in_T, n + 1)
                    after(pe, hid_done, n - 1)
                    wt = w.up[:, bass.ds(e, 1)][:, 0]
                    for k in range(2):
                        rhs = wt[:, 0, k * I:(k + 1) * I] if layer == 0 else wt[:, k, :]
                        ins = nc.tensor.matmul((g_of, u_of)[k](u % 2), xT[u][:], rhs, start=True, stop=True)
                    ins.then_inc(up_ps, 1)
                    return e

                def t_hid(n, u):
                    pe.wait_ge(hid_done, n + 1)
                    after(pe, hid_T, n - 1)
                    c0 = 0
                    for m, cw in enumerate(cols):
                        ins = nc.tensor.transpose(ph[0:cw, u % 2, m * P:(m + 1) * P], hid[u % 2][:, c0:c0 + cw], w.ident[:])
                        c0 += cw
                    ins.then_inc(hid_ps, 1)

                def down(n, u):
                    e = pe.value_load(w.tile_expert[0:1, n:n + 1] if const(n) else w.tile_expert[0:1, bass.ds(n, 1)], min_val=0, max_val=NE - 1)
                    pe.wait_ge(hid_T, n + 1)
                    after(pe, y_done, n)
                    wt = w.down[:, bass.ds(e, 1)][:, 0]
                    for m, cw in enumerate(cols):
                        ins = nc.tensor.matmul(pd[:, 0:C], hidT[u % 2][0:cw, m, :], wt[0:cw, m, :], start=m == 0, stop=m == M - 1)
                    ins.then_inc(dn_ps, 1)

                t_in(0, 0)
                t_in(1, 1)
                up(0, 0)
                skewed(pe, (2, t_in), (1, up), (0, t_hid), (-1, down))


def combine_phase(nc, w, d, layer):
    with ExitStack() as ctx:
        sb = lambda n, s, t=F32: ctx.enter_context(nc.sbuf_tensor(f"{n}_{layer}", s, t))
        sem = lambda n: semaphore_of(nc, ctx, f"{n}_{layer}")
        gat = [[sb(f"gat{k}_{u}", [P, 4, C]) for u in range(2)] for k in range(2)]
        got = [sem(f"got{u}") for u in range(2)]
        c_step, x_done, stored = sem("c_step"), sem("x_done"), sem("stored")
        NSTEP = 6 if layer == 0 else 4
        with nc.Block() as block:
            @block.gpsimd
            def _(pool):
                for s in range(2 * NB):
                    u = s % 2
                    if s >= 2:
                        pool.wait_ge(x_done, s - 1)
                    for j in range(4):
                        for k in range(2):
                            nc.gpsimd.indirect_dma_start(out=gat[k][u][:, j, :], out_offset=None, in_=d.yg,
                                                         in_offset=bass.IndirectOffsetOnAxis(ap=w.slot[k][:, 4 * s + j:4 * s + j + 1], axis=0)
                                                         ).then_inc(got[u], 16)

            @block.vector
            def _(dve):
                v = nc.vector
                for s in range(2 * NB):
                    u, b = s % 2, s // 2
                    dve.wait_ge(got[u], 16 * 8 * (s // 2 + 1))
                    link = Chain(dve, c_step, NSTEP * s)
                    tw = lambda a: a[:, 4 * s:4 * s + 4].rearrange("p (j o) -> p j o", o=1).to_broadcast([P, 4, C])
                    a0, a1 = gat[0][u][:], gat[1][u][:]
                    v.tensor_tensor(a0, a0, tw(w.wt[0][:]), ALU.mult)
                    link(v.tensor_tensor(a1, a1, tw(w.wt[1][:]), ALU.mult))
                    link(v.tensor_tensor(a0, a0, a1, ALU.add))
                    if layer == 0:
                        sh = w.sh[:, 4 * s:4 * s + 4, :]
                        link(v.tensor_tensor(a1, sh, tw(w.shw[:]), ALU.mult))
                        link(v.tensor_tensor(a0, a0, a1, ALU.add))
                    link(v.tensor_tensor(a0, a0, w.gate[:, 2 * layer + 1, b:b + 1, :].to_broadcast([P, 4, C]), ALU.mult))
                    link(v.tensor_tensor(w.x[:, 4 * s:4 * s + 4, :], w.x[:, 4 * s:4 * s + 4, :], a0, ALU.add))
                    dve.sem_inc(x_done, 1)

            @block.sync
            def _(sp):
                if layer == 1:
                    xo = d.out.rearrange("b (n p) c -> p (b n) c", p=P)
                    for s in range(2 * NB):
                        sp.wait_ge(x_done, s + 1)
                        sp.dma_start(xo[:, 4 * s:4 * s + 4, :], w.x[:, 4 * s:4 * s + 4, :]).then_inc(stored, 16)
                    sp.wait_ge(stored, 16 * 2 * NB)


NSTATE = 32
CG = P // NSTATE
NG = C // CG
LW = P + 1
GI = 4
TWO_PI = 6.283185
ROUND = 12582912.0


def s4_phase(nc, w, d):
    with ExitStack() as whole:
        sbw = lambda n, s, t=F32: whole.enter_context(nc.sbuf_tensor(n, s, t))
        inT = sbw("inT", [P, C])
        gluT = sbw("gluT", [P, 2, C])
        outT = sbw("outT", [P, C])
        glub = sbw("glub", [P, 2])
        inb = sbw("inb", [P, C])
        outb = sbw("outb", [P, C])
        cols = sbw("cols", [P, 6, NG])
        powr = sbw("powr", [P, 2, NG, LW])
        s_all = sbw("s_all", [P, NG, 2, NB, TPB])
        h_all = sbw("h_all", [P, NG, 2, NB, TPB])
        h_c = sbw("h_c", [P, NG, 2, NT])
        cdiag = sbw("cdiag", [P, NG, 2, CG])
        k_lh = sbw("k_lh", [P, C])
        k_hl = sbw("k_hl", [P, P])
        dskip = sbw("dskip", [P, 1])
        R_, PH_, CR_, CI_, DR_, DI_ = range(6)
        u_all = w.v[:].rearrange("p a b c -> p (a b c)").rearrange("p (c t) -> p c t", t=NT)
        h_keep = w.sh
        s4_coefficients(nc, w, d, locals())
        s4_input(nc, w, d, locals())
        s4_states(nc, w, d, locals())
        y_all = sbw("y_all", [P, NT, C])
        s4_output(nc, w, d, locals())
        s4_gate(nc, w, d, locals())


def s4_coefficients(nc, w, d, m):
    inT, gluT, outT, glub, inb, outb, cols, powr, cdiag, dskip = (m[k] for k in (
        "inT", "gluT", "outT", "glub", "inb", "outb", "cols", "powr", "cdiag", "dskip"))
    R_, PH_, CR_, CI_, DR_, DI_ = range(6)
    with ExitStack() as ctx:
        sb = lambda n, s, t=F32: ctx.enter_context(nc.sbuf_tensor(n, s, t))
        ps = lambda n, s, t=F32: ctx.enter_context(nc.psum_tensor(n, s, t))
        sem = lambda n: semaphore_of(nc, ctx, n)
        wsrc = sb("wsrc", [P, 4, C])
        raw = sb("sraw", [P, 3, NSTATE])
        cc = sb("cc", [P, NSTATE, 2])
        ldt = sb("ldt", [P, 1])
        co = sb("co", [P, 6, NSTATE])
        ea = sb("ea", [P, NSTATE])
        tt = sb("tt", [P, 4, NSTATE])
        rn = sb("rn", [P, 4, NSTATE])
        ex = sb("ex", [P, 2, NSTATE])
        zz = sb("zz", [P, 4, NSTATE])
        q = sb("qtmp", [P, 4, NSTATE])
        den = sb("den", [P, NSTATE])
        rowsg = sb("rowsg", [NG, 6, P])
        rnd = sb("rnd", [P, NG, LW])
        mag = sb("smag", [P, NG, LW])
        pw = ps("pw", [P, ST])
        pc = ps("pc", [P, ST])
        s_in, w_tr, w_out, c_step, e_done, z_done, co_out, rows_in, cols_ps, m_done, sin_done = (sem(n) for n in (
            "s_in", "sw_tr", "sw_out", "c_step", "e_done", "z_done", "co_out", "rows_in", "cols_ps4", "m_done", "ssin_done"))
        p_step = sem("p_step")
        with nc.Block() as block:
            @block.sync
            def _(sp):
                srcs = [d.in_W, d.glu_W[0:C], d.glu_W[C:2 * C], d.out_W]
                for k, src in enumerate(srcs):
                    sp.dma_start(wsrc[:, k, :], src).then_inc(s_in, 16)
                sp.dma_start(raw[:, 0, :], d.log_A_real).then_inc(s_in, 16)
                sp.dma_start(raw[:, 1, :], d.A_imag).then_inc(s_in, 16)
                sp.dma_start(cc[:], d.C).then_inc(s_in, 16)
                col = lambda a: a.rearrange("(p o) -> p o", o=1)
                with nc.allow_non_contiguous_dma(reason="vectors as columns"):
                    sp.dma_start(ldt[:], col(d.log_dt)).then_inc(s_in, 16)
                    sp.dma_start(dskip[:], col(d.D_skip)).then_inc(s_in, 16)
                    for k in range(2):
                        sp.dma_start(glub[:, k:k + 1], col(d.glu_b[k * C:(k + 1) * C])).then_inc(s_in, 16)
                sp.dma_start(inb[:], d.in_b.rearrange("(o c) -> o c", o=1).to_broadcast([P, C])).then_inc(s_in, 16)
                sp.dma_start(outb[:], d.out_b.rearrange("(o c) -> o c", o=1).to_broadcast([P, C])).then_inc(s_in, 16)
                sp.wait_ge(z_done, 1)
                sp.dma_start(d.coef.rearrange("a (h n) -> h a n", n=NSTATE), co[:]).then_inc(co_out, 16)
                sp.wait_ge(co_out, 16)
                sp.dma_start(rowsg[:], d.coef.rearrange("a (g p) -> g a p", p=P)).then_inc(rows_in, 16)

            @block.tensor
            def _(pe):
                pe.wait_ge(s_in, 16 * 13)
                for k in range(4):
                    ins = nc.tensor.transpose(pw[:, k * C:(k + 1) * C], wsrc[:, k, :], w.ident[:])
                ins.then_inc(w_tr, 1)
                pe.wait_ge(rows_in, 16)
                for a in range(6):
                    ins = nc.tensor.transpose(pc[:, a * NG:(a + 1) * NG], rowsg[:, a, :], w.ident[0:NG, 0:NG])
                ins.then_inc(cols_ps, 1)

            @block.scalar
            def _(act):
                act.wait_ge(s_in, 16 * 13)
                nc.scalar.activation(ldt[:], ldt[:], ACT.Exp).then_inc(e_done, 1)
                nc.scalar.activation(ea[:], raw[:, 0, :], ACT.Exp).then_inc(e_done, 1)
                act.wait_ge(c_step, 1)
                nc.scalar.activation(ex[:, 0, :], co[:, R_, :], ACT.Exp)
                nc.scalar.activation(ex[:, 1, :], co[:, R_, :], ACT.Exp, scale=float(P)).then_inc(e_done, 1)
                act.wait_ge(c_step, 5)
                nc.scalar.activation(zz[:], tt[:], ACT.Sin, scale=TWO_PI).then_inc(e_done, 1)
                act.wait_ge(p_step, 1)
                nc.scalar.activation(mag[:], mag[:], ACT.Exp).then_inc(m_done, 1)
                for k in range(2):
                    act.wait_ge(p_step, 4 + 2 * k)
                    nc.scalar.activation(powr[:, 1 - k], powr[:, 1 - k], ACT.Sin, scale=TWO_PI).then_inc(sin_done, 1)

            @block.vector
            def _(dve):
                v = nc.vector
                link = Chain(dve, c_step)
                dve.wait_ge(e_done, 2)
                link(v.tensor_scalar(co[:, R_, :], ea[:], ldt[:], -1.0, ALU.mult, ALU.mult))
                link(v.tensor_scalar(co[:, PH_, :], raw[:, 1, :], ldt[:], 1.0 / (2.0 * np.pi), ALU.mult, ALU.mult))
                v.tensor_copy(tt[:, 0, :], co[:, PH_, :])
                v.tensor_scalar(tt[:, 1, :], co[:, PH_, :], 0.25, None, ALU.add)
                v.tensor_scalar(tt[:, 2, :], co[:, PH_, :], float(P), None, ALU.mult)
                link(v.tensor_scalar(tt[:, 3, :], co[:, PH_, :], float(P), 0.25, ALU.mult, ALU.add))
                link(v.tensor_scalar(rn[:], tt[:], ROUND, ROUND, ALU.add, ALU.subtract))
                link(v.tensor_tensor(tt[:], tt[:], rn[:], ALU.subtract))
                dve.wait_ge(e_done, 4)
                v.tensor_tensor(zz[:, 0:2, :], zz[:, 0:2, :], ex[:, 0:1, :].to_broadcast([P, 2, NSTATE]), ALU.mult)
                v.tensor_tensor(co[:, DI_, :], zz[:, 2, :], ex[:, 1, :], ALU.mult)
                v.tensor_tensor(co[:, DR_, :], zz[:, 3, :], ex[:, 1, :], ALU.mult)
                v.tensor_tensor(den[:], ea[:], ea[:], ALU.mult)
                link(v.tensor_tensor(q[:, 0, :], raw[:, 1, :], raw[:, 1, :], ALU.mult))
                link(v.tensor_tensor(den[:], den[:], q[:, 0, :], ALU.add))
                v.reciprocal(den[:], den[:])
                link(v.tensor_scalar(zz[:, 1, :], zz[:, 1, :], -1.0, None, ALU.add))

                def cmul(o_r, o_i, a_r, a_i, b_r, b_i):
                    v.tensor_tensor(q[:, 0, :], a_r, b_r, ALU.mult)
                    v.tensor_tensor(q[:, 1, :], a_i, b_i, ALU.mult)
                    v.tensor_tensor(q[:, 2, :], a_r, b_i, ALU.mult)
                    link(v.tensor_tensor(q[:, 3, :], a_i, b_r, ALU.mult))
                    v.tensor_tensor(o_r, q[:, 0, :], q[:, 1, :], ALU.subtract)
                    link(v.tensor_tensor(o_i, q[:, 2, :], q[:, 3, :], ALU.add))
                cmul(co[:, CR_, :], co[:, CI_, :], cc[:, :, 0], cc[:, :, 1], zz[:, 1, :], zz[:, 0, :])
                v.tensor_scalar(zz[:, 2, :], ea[:], -1.0, None, ALU.mult)
                link(v.tensor_scalar(zz[:, 3, :], raw[:, 1, :], -1.0, None, ALU.mult))
                cmul(zz[:, 0, :], zz[:, 1, :], co[:, CR_, :], co[:, CI_, :], zz[:, 2, :], zz[:, 3, :])
                link(v.tensor_scalar(den[:], den[:], 2.0, None, ALU.mult))
                v.tensor_tensor(co[:, CR_, :], zz[:, 0, :], den[:], ALU.mult)
                v.tensor_tensor(co[:, CI_, :], zz[:, 1, :], den[:], ALU.mult).then_inc(z_done, 1)
                dve.wait_ge(w_tr, 1)
                v.tensor_copy(inT[:], pw[:, 0:C])
                v.tensor_copy(gluT[:], pw[:, C:3 * C].rearrange("p (a c) -> p a c", a=2))
                v.tensor_copy(outT[:], pw[:, 3 * C:4 * C])
                dve.wait_ge(cols_ps, 1)
                link(v.tensor_copy(cols[:], pc[:, 0:6 * NG].rearrange("p (a g) -> p a g", a=6)))
                pl = Chain(dve, p_step)
                ib = w.iota[:, 0:LW].rearrange("p (o l) -> p o l", o=1).to_broadcast([P, NG, LW])
                cb = lambda a: cols[:, a, :].rearrange("p (g o) -> p g o", o=1).to_broadcast([P, NG, LW])
                pl(v.tensor_tensor(mag[:], ib, cb(R_), ALU.mult))
                pl(v.tensor_tensor(powr[:, 1], ib, cb(PH_), ALU.mult))
                v.tensor_scalar(powr[:, 0], powr[:, 1], 0.25, None, ALU.add)
                for k in range(2):
                    pl(v.tensor_scalar(rnd[:], powr[:, 1 - k], ROUND, ROUND, ALU.add, ALU.subtract))
                    pl(v.tensor_tensor(powr[:, 1 - k], powr[:, 1 - k], rnd[:], ALU.subtract))
                link(v.memset(cdiag[:], 0.0))
                for h in range(CG):
                    r = slice(h * NSTATE, (h + 1) * NSTATE)
                    v.tensor_copy(cdiag[r, :, 0, h], cols[r, CR_, :])
                    v.tensor_scalar(cdiag[r, :, 1, h], cols[r, CI_, :], -1.0, None, ALU.mult)
                dve.wait_ge(m_done, 1)
                for k in range(2):
                    dve.wait_ge(sin_done, k + 1)
                    v.tensor_tensor(powr[:, 1 - k], powr[:, 1 - k], mag[:], ALU.mult)


def s4_input(nc, w, d, m):
    inT, inb, u_all, h_keep = (m[k] for k in ("inT", "inb", "u_all", "h_keep"))
    with ExitStack() as ctx:
        sb = lambda n, s, t=F32: ctx.enter_context(nc.sbuf_tensor(n, s, t))
        ps = lambda n, s, t=F32: ctx.enter_context(nc.psum_tensor(n, s, t))
        sem = lambda n: semaphore_of(nc, ctx, n)
        hs = [sb(f"shs{u}", [P, 4, C]) for u in range(2)]
        hT = [sb(f"shT{u}", [P, ST]) for u in range(2)]
        pT = ps("spT", [P, 2, ST])
        pu = ps("spu", [P, 2, ST])
        i_step, h_done, h_kept, tr_done, hT_done, u_ps, u_out = (sem(n) for n in (
            "i_step", "sh_done", "sh_kept", "str_done", "shT_done", "u_ps", "u_out"))
        with nc.Block() as block:
            @block.vector
            def _(dve):
                with dve.Fori(0, NB) as b:
                    for u in range(2):
                        s = 2 * b + u
                        dve.wait_ge(tr_done, s)
                        dve.wait_ge(h_kept, s)
                        link = Chain(dve, i_step, 2 * s)
                        for j in range(4):
                            t = b * TPB + u * 4 + j
                            ins = nc.vector.tensor_scalar(hs[u][:, j, :], w.x[:, t, :], w.mean[:, bass.ds(t, 1)],
                                                          w.rstd[:, bass.ds(t, 1)], ALU.subtract, ALU.mult)
                        link(ins)
                        link(nc.vector.tensor_tensor(hs[u][:], hs[u][:], w.moda[:, 1, bass.ds(b, 1), :].to_broadcast([P, 4, C]), ALU.mult))
                        nc.vector.tensor_tensor(hs[u][:], hs[u][:], w.moda[:, 0, bass.ds(b, 1), :].to_broadcast([P, 4, C]), ALU.add).then_inc(h_done, 1)
                        dve.wait_ge(u_ps, s + 1)
                        dst = u_all.rearrange("p c t -> p t c")[:, bass.ds(b * TPB + u * 4, 4), :]
                        nc.vector.tensor_tensor(dst, pu[:, u, :].rearrange("p (j c) -> p j c", j=4),
                                                inb[:].rearrange("p (o c) -> p o c", o=1).to_broadcast([P, 4, C]), ALU.add).then_inc(u_out, 1)

            @block.gpsimd
            def _(pool):
                with pool.Fori(0, NB) as b:
                    for u in range(2):
                        pool.wait_ge(h_done, 2 * b + u + 1)
                        nc.gpsimd.tensor_copy(h_keep[:, bass.ds(b * TPB + u * 4, 4), :], hs[u][:]).then_inc(h_kept, 1)

            @block.scalar
            def _(act):
                with act.Fori(0, NB) as b:
                    for u in range(2):
                        act.wait_ge(tr_done, 2 * b + u + 1)
                        nc.scalar.copy(hT[u][:], pT[:, u, :]).then_inc(hT_done, 1)

            @block.tensor
            def _(pe):
                with pe.Fori(0, NB) as b:
                    for u in range(2):
                        s = 2 * b + u
                        pe.wait_ge(h_done, s + 1)
                        pe.wait_ge(hT_done, s)
                        for j in range(4):
                            ins = nc.tensor.matmul(pT[:, u, j * C:(j + 1) * C], hs[u][:, j, :], w.flip[:], start=True, stop=True)
                        ins.then_inc(tr_done, 1)
                        pe.wait_ge(hT_done, s + 1)
                        pe.wait_ge(u_out, s)
                        for j in range(4):
                            ins = nc.tensor.matmul(pu[:, u, j * C:(j + 1) * C], hT[u][:, j * C:(j + 1) * C], inT[:], start=True, stop=True)
                        ins.then_inc(u_ps, 1)


def s4_states(nc, w, d, m):
    powr, s_all, h_all, h_c, cdiag, k_lh, k_hl, u_all, cols, dskip = (m[k] for k in (
        "powr", "s_all", "h_all", "h_c", "cdiag", "k_lh", "k_hl", "u_all", "cols", "dskip"))
    R_, PH_, CR_, CI_, DR_, DI_ = range(6)
    with ExitStack() as ctx:
        sb = lambda n, s, t=F32: ctx.enter_context(nc.sbuf_tensor(n, s, t))
        ps = lambda n, s, t=F32: ctx.enter_context(nc.psum_tensor(n, s, t))
        sem = lambda n: semaphore_of(nc, ctx, n)
        wr = [sb(f"wr{u}", [P, 2, GI, LW]) for u in range(2)]
        vr = [sb(f"vr{u}", [P, 2, GI, P]) for u in range(2)]
        zk = sb("zk", [P, P])
        q = sb("hq", [P, 2, NG, 2, NB])
        qc = sb("hqc", [P, 4, NG, NT])
        pv = ps("spv", [P, 2, ST])
        pS = ps("sps4", [P, 2, ST])
        pk = ps("spk", [P, ST])
        w_in = [sem(f"sw_in{u}") for u in range(2)]
        v_ps, v_out, s_ps, s_out, r_step, k_tr, k_done, k_stored = (sem(n) for n in (
            "v_ps4", "v_out4", "s_ps4", "s_out4", "r_step4", "k_tr", "k_done", "k_stored"))
        NI = NG // GI
        with nc.Block() as block:
            @block.sync
            def _(sp):
                with sp.Fori(0, NI // 2) as i:
                    for u in range(2):
                        n = 2 * i + u
                        sp.wait_ge(s_ps, n)
                        sp.dma_start(wr[u][:], powr[:, :, bass.ds(n * GI, GI), :]).then_inc(w_in[u], 16)
                sp.wait_ge(k_done, 1)
                sp.dma_start(d.kpad[:, 0:P], zk[:]).then_inc(k_stored, 16)
                sp.dma_start(d.kpad[:, P:2 * P], k_hl[:]).then_inc(k_stored, 16)
                sp.wait_ge(k_stored, 32)

            @block.scalar
            def _(act):
                with act.Fori(0, NI // 2) as i:
                    for u in range(2):
                        n = 2 * i + u
                        act.wait_ge(v_ps, n + 1)
                        for a in range(2):
                            ins = nc.scalar.copy(vr[u][:, a], pv[:, a, :].rearrange("p (g l) -> p g l", g=GI))
                        ins.then_inc(v_out, 1)

            @block.tensor
            def _(pe):
                with pe.Fori(0, NI // 2) as i:
                    for u in range(2):
                        n = 2 * i + u
                        pe.wait_ge(w_in[u], 16 * i + 16)
                        pe.wait_ge(v_out, n)
                        for a in range(2):
                            for g in range(GI):
                                ins = nc.tensor.transpose(pv[:, a, g * P:(g + 1) * P], wr[u][:, a, g, 0:P], w.ident[:])
                        ins.then_inc(v_ps, 1)
                        pe.wait_ge(s_out, n)
                        for g in range(GI):
                            for a in range(2):
                                nc.tensor.matmul(pk[:, g * CG:(g + 1) * CG], wr[u][:, a, g, 0:P],
                                                 cdiag[:, bass.ds(n * GI + g, 1), a, :].rearrange("p o c -> p (o c)"),
                                                 start=a == 0, stop=a == 1)
                        pe.wait_ge(v_out, n + 1)
                        for a in range(2):
                            for g in range(GI):
                                ins = nc.tensor.matmul(pS[:, a, g * P:(g + 1) * P], vr[u][:, a, g, :],
                                                       u_all[:, bass.ds((n * GI + g) * CG, CG), :].rearrange("p c t -> p (c t)"),
                                                       start=True, stop=True)
                        ins.then_inc(s_ps, 1)
                pe.wait_ge(s_out, NI)
                nc.tensor.transpose(pk[:, 0:P], k_lh[:], w.ident[:]).then_inc(k_tr, 1)

            @block.vector
            def _(dve):
                v = nc.vector
                with dve.Fori(0, NI // 2) as i:
                    for u in range(2):
                        n = 2 * i + u
                        dve.wait_ge(s_ps, n + 1)
                        v.tensor_copy(k_lh[:, bass.ds(n * GI * CG, GI * CG)], pk[:, 0:GI * CG])
                        for h in range(CG):
                            r = slice(h * NSTATE, (h + 1) * NSTATE)
                            src = pS[r, :, :].rearrange("p a (g c t) -> p a g c t", g=GI, c=CG)[:, :, :, h, :]
                            dst = s_all[:].rearrange("p g a b t -> p a g (b t)")[r, :, bass.ds(n * GI, GI), :]
                            ins = v.tensor_copy(dst, src)
                        ins.then_inc(s_out, 1)
                dve.wait_ge(k_tr, 1)
                link = Chain(dve, r_step)
                link(v.tensor_copy(k_hl[:], pk[:, 0:P]))
                v.memset(zk[:], 0.0)
                v.tensor_tensor(k_hl[:, 0:1], k_hl[:, 0:1], dskip[:], ALU.add).then_inc(k_done, 1)
                link(v.memset(h_all[:, :, :, :, 0], 0.0))
                for t in range(1, TPB):
                    hp = h_all[:, :, :, :, t - 1]
                    for k, a in enumerate((DR_, DI_)):
                        cb = cols[:, a, :].rearrange("p (g o) -> p g o", o=1).to_broadcast([P, NG, 2 * NB])
                        ins = v.tensor_tensor(q[:, k].rearrange("p g a b -> p g (a b)"), hp.rearrange("p g a b -> p g (a b)"), cb, ALU.mult)
                    link(ins)
                    link(v.tensor_tensor(q[:, 0], q[:, 0], s_all[:, :, :, :, t - 1], ALU.add))
                    v.tensor_tensor(h_all[:, :, 0, :, t], q[:, 0, :, 0, :], q[:, 1, :, 1, :], ALU.subtract)
                    link(v.tensor_tensor(h_all[:, :, 1, :, t], q[:, 0, :, 1, :], q[:, 1, :, 0, :], ALU.add))
                hr, hi = (h_all[:, :, a, :, :].rearrange("p g b t -> p g (b t)") for a in range(2))
                cb = lambda a: cols[:, a, :].rearrange("p (g o) -> p g o", o=1).to_broadcast([P, NG, NT])
                v.tensor_tensor(qc[:, 0], hr, cb(CR_), ALU.mult)
                v.tensor_tensor(qc[:, 1], hi, cb(CI_), ALU.mult)
                v.tensor_tensor(qc[:, 2], hr, cb(CI_), ALU.mult)
                link(v.tensor_tensor(qc[:, 3], hi, cb(CR_), ALU.mult))
                v.tensor_tensor(h_c[:, :, 0, :], qc[:, 0], qc[:, 1], ALU.subtract)
                v.scalar_tensor_tensor(out=h_c[:, :, 1, :], in0=qc[:, 2], scalar=-1.0, in1=qc[:, 3], op0=ALU.mult, op1=ALU.subtract)


def s4_output(nc, w, d, m):
    powr, h_c, u_all, y_all = (m[k] for k in ("powr", "h_c", "u_all", "y_all"))
    NI = NG // GI
    CI = GI * CG
    with ExitStack() as ctx:
        sb = lambda n, s, t=F32: ctx.enter_context(nc.sbuf_tensor(n, s, t))
        ps = lambda n, s, t=F32: ctx.enter_context(nc.psum_tensor(n, s, t))
        sem = lambda n: semaphore_of(nc, ctx, n)
        wr = [sb(f"ywr{u}", [P, 2, GI, LW]) for u in range(2)]
        tz = [sb(f"tz{u}", [P, CI, P]) for u in range(2)]
        hd = [sb(f"hd{u}", [P, GI, 2, CG, NT]) for u in range(2)]
        py = ps("py", [P, 2, ST])
        w_in = [sem(f"yw_in{u}") for u in range(2)]
        z_set, hd_done, y_ps, y_out = sem("z_set"), sem("hd_done"), sem("y_ps"), sem("y_out4")
        with nc.Block() as block:
            @block.sync
            def _(sp):
                with sp.Fori(0, NI // 2) as i:
                    for u in range(2):
                        n = 2 * i + u
                        sp.wait_ge(y_ps, n)
                        sp.dma_start(wr[u][:], powr[:, :, bass.ds(n * GI, GI), :]).then_inc(w_in[u], 16)
                        src = bass.AP(d.kpad.tensor, n * (CI * 2 * P) + 1, [[1, P], [2 * P, CI], [1, P]])
                        sp.dma_start(tz[u][:], src).then_inc(w_in[u], 16)

            @block.vector
            def _(dve):
                for u in range(2):
                    ins = nc.vector.memset(hd[u][:], 0.0)
                ins.then_inc(z_set, 1)
                dve.wait_ge(z_set, 1)
                with dve.Fori(0, NI // 2) as i:
                    for u in range(2):
                        n = 2 * i + u
                        dve.wait_ge(y_ps, n)
                        for h in range(CG):
                            r = slice(h * NSTATE, (h + 1) * NSTATE)
                            ins = nc.vector.tensor_copy(hd[u][r, :, :, h, :], h_c[r, bass.ds(n * GI, GI), :, :])
                        ins.then_inc(hd_done, 1)

            @block.tensor
            def _(pe):
                with pe.Fori(0, NI // 2) as i:
                    for u in range(2):
                        n = 2 * i + u
                        pe.wait_ge(w_in[u], 32 * i + 32)
                        pe.wait_ge(hd_done, n + 1)
                        pe.wait_ge(y_out, n)
                        for g in range(GI):
                            for a in range(2):
                                nc.tensor.matmul(py[:, u, g * P:(g + 1) * P], wr[u][:, a, g, 1:LW],
                                                 hd[u][:, g, a].rearrange("p c t -> p (c t)"), start=a == 0, stop=False, skip_group_check=True)
                            for c in range(CG):
                                ch = g * CG + c
                                ins = nc.tensor.matmul(py[:, u, ch * NT:(ch + 1) * NT], tz[u][:, ch, :],
                                                       u_all[:, bass.ds(n * CI + ch, 1), :].rearrange("p o t -> p (o t)"),
                                                       start=False, stop=c == CG - 1, skip_group_check=True)
                        ins.then_inc(y_ps, 1)

            @block.scalar
            def _(act):
                count = act.alloc_register("gelu_count")
                with act.Fori(0, NI // 2) as i:
                    for u in range(2):
                        n = 2 * i + u
                        wait_before(act, count, y_ps, n + 1, hd_done)
                        dst = y_all[:].rearrange("p t c -> p c t")[:, bass.ds(n * CI, CI), :]
                        nc.scalar.activation(dst, py[:, u, :].rearrange("p (c t) -> p c t", c=CI), ACT.Gelu).then_inc(y_out, 1)


def s4_gate(nc, w, d, m):
    gluT, glub, outT, outb, y_all, h_keep = (m[k] for k in ("gluT", "glub", "outT", "outb", "y_all", "h_keep"))
    with ExitStack() as ctx:
        sb = lambda n, s, t=F32: ctx.enter_context(nc.sbuf_tensor(n, s, t))
        ps = lambda n, s, t=F32: ctx.enter_context(nc.psum_tensor(n, s, t))
        sem = lambda n: semaphore_of(nc, ctx, n)
        ys = [sb(f"gys{u}", [P, 4, C]) for u in range(2)]
        yT = [sb(f"gyT{u}", [P, ST]) for u in range(2)]
        sig = [sb(f"gsig{u}", [P, ST]) for u in range(2)]
        y2 = [sb(f"gy2{u}", [P, ST]) for u in range(2)]
        o = [sb(f"go{u}", [P, 4, C]) for u in range(2)]
        pT = ps("gpT", [P, 2, ST])
        pz = ps("gpz", [P, 2, ST])
        po = ps("gpo", [P, 2, ST])
        y_in, y_tr, y_T, z_ps, sg_done, y2_done, o_ps, o_step, x_done = (sem("g" + n) for n in (
            "y_in", "y_tr", "y_T", "z_ps", "sg_done", "y2_done", "o_ps", "o_step", "x_done"))
        with nc.Block() as block:
            @block.gpsimd
            def _(pool):
                with pool.Fori(0, NB) as b:
                    for u in range(2):
                        s = 2 * b + u
                        pool.wait_ge(y_tr, s)
                        nc.gpsimd.tensor_copy(ys[u][:], y_all[:, bass.ds(b * TPB + u * 4, 4), :]).then_inc(y_in, 1)

            @block.tensor
            def _(pe):
                with pe.Fori(0, NB) as b:
                    for u in range(2):
                        s = 2 * b + u
                        pe.wait_ge(y_in, s + 1)
                        pe.wait_ge(y_T, s)
                        for j in range(4):
                            ins = nc.tensor.transpose(pT[:, u, j * C:(j + 1) * C], ys[u][:, j, :], w.ident[:])
                        ins.then_inc(y_tr, 1)
                        pe.wait_ge(y_T, s + 1)
                        pe.wait_ge(y2_done, s)
                        for k in range(2):
                            ins = nc.tensor.matmul(pz[:, k, :], gluT[:, k, :], yT[u][:], start=True, stop=True)
                        ins.then_inc(z_ps, 1)
                        pe.wait_ge(y2_done, s + 1)
                        pe.wait_ge(x_done, s)
                        for j in range(4):
                            ins = nc.tensor.matmul(po[:, u, j * C:(j + 1) * C], y2[u][:, j * C:(j + 1) * C], outT[:], start=True, stop=True)
                        ins.then_inc(o_ps, 1)

            @block.scalar
            def _(act):
                with act.Fori(0, NB) as b:
                    for u in range(2):
                        s = 2 * b + u
                        act.wait_ge(z_ps, s + 1)
                        nc.scalar.activation(sig[u][:], pz[:, 1, :], ACT.Sigmoid, bias=glub[:, 1:2]).then_inc(sg_done, 1)

            @block.vector
            def _(dve):
                v = nc.vector
                with dve.Fori(0, NB) as b:
                    for u in range(2):
                        s = 2 * b + u
                        dve.wait_ge(y_tr, s + 1)
                        v.tensor_copy(yT[u][:], pT[:, u, :]).then_inc(y_T, 1)
                        dve.wait_ge(sg_done, s + 1)
                        v.scalar_tensor_tensor(out=y2[u][:], in0=pz[:, 0, :], scalar=glub[:, 0:1], in1=sig[u][:],
                                               op0=ALU.add, op1=ALU.mult).then_inc(y2_done, 1)
                        dve.wait_ge(o_ps, s + 1)
                        link = Chain(dve, o_step, 3 * s)
                        link(v.tensor_tensor(o[u][:], po[:, u, :].rearrange("p (j c) -> p j c", j=4),
                                             outb[:].rearrange("p (o c) -> p o c", o=1).to_broadcast([P, 4, C]), ALU.add))
                        link(v.tensor_tensor(o[u][:], o[u][:], h_keep[:, bass.ds(b * TPB + u * 4, 4), :], ALU.add))
                        link(v.tensor_tensor(o[u][:], o[u][:], w.gate[:, 2, bass.ds(b, 1), :].to_broadcast([P, 4, C]), ALU.mult))
                        xs = w.x[:, bass.ds(b * TPB + u * 4, 4), :]
                        v.tensor_tensor(xs, xs, o[u][:], ALU.add).then_inc(x_done, 1)


def program(nc, d):
    d.qk = [nc.dram_tensor(f"qk{s}", [NB * NH, TERMS, HD, T], BF16, kind="Internal").ap() for s in range(2)]
    d.xg = nc.dram_tensor("xg", [NSLOT * P, C], F32, kind="Internal").ap()
    d.coef = nc.dram_tensor("coef", [6, C * NSTATE], F32, kind="Internal").ap()
    d.kpad = nc.dram_tensor("kpad", [C, 2 * P], F32, kind="Internal").ap()
    d.yg = nc.dram_tensor("yg", [NSLOT * P, C], F32, kind="Internal").ap()

    w = Work()
    with ExitStack() as ctx:
        sb = lambda n, shape, t=F32: ctx.enter_context(nc.sbuf_tensor(n, shape, t))
        w.x = sb("x", [P, NT, C])
        w.y = sb("y", [P, NQUAD, TPB, 32])
        w.v = sb("v", [P, NQUAD, TPB, 32])
        w.ident, w.flip = sb("ident", [P, P]), sb("flip", [P, P])
        w.identb, w.trib, w.onesb = (sb(n, [P, P], BF16) for n in ("identb", "trib", "onesb"))
        w.iota = sb("iota", [P, P + 1])
        w.bnst = sb("bnst", [P, NT, 6])
        w.mean, w.rstd, w.t0, w.t1 = (sb(n, [P, NT]) for n in ("mean", "rstd", "t0", "t1"))
        w.mod = sb("mod", [P, 2, 6, NB])
        w.gate, w.modr = sb("gate", [P, 4, NB, C]), sb("modr", [P, 4, NB, C])
        w.moda = sb("moda", [P, 2, NB, C])
        w.wo, w.bo = sb("wo", [P, C]), sb("bo", [P, C])
        w.h = w.v[:].rearrange("p a b c -> p (a b c)").rearrange("p (t c) -> p t c", c=C)
        w.sh = w.y[:].rearrange("p a b c -> p (a b c)").rearrange("p (t c) -> p t c", c=C)
        with ExitStack() as first:
            sf = lambda n, shape, t=F32: first.enter_context(nc.sbuf_tensor(n, shape, t))
            w.wqkv, w.wrot = sf("wqkv", [P, 3 * C]), sf("wrot", [P, 2 * C])
            w.bqk, w.bv = sf("bqk", [P, 4]), sf("bv", [P, C])
            w.rope, w.rotsign = sf("rope", [P, 2, T]), sf("rotsign", [P, 1])
            w.maskb = sf("maskb", [P, P], BF16)
            setup_phase(nc, w, d)
            qkv_phase(nc, w, d)
            attention_phase(nc, w, d)
        project_phase(nc, w, d)
        w.wt, w.slot = [sb(f"wt{k}", [P, NT]) for k in range(2)], [sb(f"slot{k}", [P, NT], U32) for k in range(2)]
        w.shw = sb("shw", [P, NT])
        w.tile_expert = sb("tile_expert", [P, NSLOT], mybir.dt.int32)
        for layer in range(2):
            if layer == 1:
                stats_phase(nc, w, "c")
                s4_phase(nc, w, d)
            with ExitStack() as own:
                so = lambda n, shape: own.enter_context(nc.sbuf_tensor(f"{n}{layer}", shape, F32))
                w.up = so("up", [P, NE, layer + 1, 352])
                w.down = so("down", [P, NE, (2, 3)[layer], C])
                w.rt = so("rt", [P, (NE + 1, NE)[layer]])
                if layer == 0:
                    w.shgu, w.shd = so("shgu", [P, 2, SI]), so("shd", [P, 3, C])
                weights_phase(nc, w, d, layer)
                stats_phase(nc, w, "bd"[layer])
                route_phase(nc, w, d, layer)
                experts_phase(nc, w, d, layer)
                combine_phase(nc, w, d, layer)


_INPUTS = {
    "x": "L0_attn_x", "w_attn": "L0_attn_W_attn", "b_attn": "L0_attn_b_attn", "w_proj": "L0_attn_W_proj", "b_proj": "L0_attn_b_proj",
    "gate_w": "L0_ffn_gate_w", "gu0": "L0_ffn_experts_gate_up", "dn0": "L0_ffn_experts_down", "sg": "L0_ffn_shared_gate_w",
    "su": "L0_ffn_shared_up_w", "sd": "L0_ffn_shared_down_w", "seg": "L0_ffn_shared_expert_gate_w", "c0": "L0_c", "wmod0": "L0_wmod",
    "in_W": "L1_attn_in_W", "in_b": "L1_attn_in_b", "log_dt": "L1_attn_log_dt", "C": "L1_attn_C", "log_A_real": "L1_attn_log_A_real",
    "A_imag": "L1_attn_A_imag", "D_skip": "L1_attn_D_skip", "glu_W": "L1_attn_glu_W", "glu_b": "L1_attn_glu_b",
    "out_W": "L1_attn_out_W", "out_b": "L1_attn_out_b", "wg": "L1_ffn_Wg", "w1": "L1_ffn_W1", "w2": "L1_ffn_W2", "w3": "L1_ffn_W3",
    "c1": "L1_c", "wmod1": "L1_wmod",
}


def _constants():
    bf16 = mybir.dt.np(BF16)
    at = np.arange(P)
    pos = np.arange(T, dtype=np.float32)
    timescale = np.float32(1250) ** (2.0 * np.arange(HD // 2, dtype=np.float32) / HD)
    angle = (pos[None, :] / timescale[:, None]).astype(np.float32)[at % (HD // 2)]
    return {
        "rope": np.stack([np.cos(angle), np.sin(angle)], 1).astype(np.float32),
        "rotsign": np.where(at % HD < HD // 2, -1, 1).astype(np.float32)[:, None],
        "ident": np.eye(P, dtype=np.float32),
        "flip": np.ascontiguousarray(np.eye(P, dtype=np.float32)[::-1]),
        "identb": np.eye(P).astype(bf16),
        "maskb": np.where(at[None, :] > at[:, None], NEG, 0).astype(bf16),
        "trib": (at[:, None] < at[None, :]).astype(bf16),
        "onesb": np.ones((P, P), bf16),
        "iota": np.tile(np.arange(P + 1, dtype=np.float32), (P, 1)),
    }


def kernel(**inputs):
    from types import SimpleNamespace

    import concourse.bacc as bacc
    from concourse.bass_utils import run_bass_kernel_spmd

    nc = bacc.Bacc("TRN2", target_bir_lowering=False, num_devices=1)

    arrays, aps = {}, {}
    given = {short: inputs[name] for short, name in _INPUTS.items()}
    for short, a in {**given, **_constants()}.items():
        a = np.ascontiguousarray(a)
        arrays[f"in_{short}"] = a
        aps[short] = nc.dram_tensor(f"in_{short}", a.shape, mybir.dt.from_np(a.dtype), kind="ExternalInput").ap()
    d = SimpleNamespace(**aps)
    d.c, d.wmod = [d.c0, d.c1], [d.wmod0, d.wmod1]
    d.out = nc.dram_tensor("out", [NB, T, C], F32, kind="ExternalOutput").ap()
    program(nc, d)
    r = run_bass_kernel_spmd(nc, [arrays], core_ids=[0])
    return r.results[0]["out"]
```

```python
from contextlib import ExitStack

import numpy as np

import concourse.bass as bass
from concourse import mybir

F32 = mybir.dt.float32
BF16 = mybir.dt.bfloat16
U32 = mybir.dt.uint32
ALU = mybir.AluOpType
ACT = mybir.ActivationFunctionType
AX = mybir.AxisListType

P = 128
NB, T, C = 4, 1024, 128
TOK = NB * T
NT = TOK // P
TPB = T // P
ST = 512
NH, HD = 16, 8
HQ = 4
NQ = NH // HQ
NQUAD = NB * NQ
TERMS = 6
KR = TERMS * HD
MROW = 64
EPS = 1e-5
NEG = -1e30



def wait_before(eng, reg, sem, value, met):
    if isinstance(value, int):
        eng.wait_ge(sem, value)
        return
    eng.reg_mov(reg, value)
    eng.wait_ge(met, 1)
    eng.wait_ge(sem, reg)


def semaphore_of(nc, phase, name):
    s = phase.enter_context(nc.semaphore(name))
    phase.callback(nc.sync.sem_clear, s)
    return s


def after(eng, sem, n):
    if not (isinstance(n, int) and n <= 0):
        eng.wait_ge(sem, n)


def staged(eng, count, *stages, unroll=2):
    deep = max(delay for delay, f in stages)
    first = 1 + deep // unroll

    def tick(i, u):
        for delay, f in stages:
            j, v = i + (u - delay) // unroll, (u - delay) % unroll
            if not (isinstance(j, int) and not 0 <= unroll * j + v < count):
                f(j, v)
    for t in range(unroll * first):
        tick(t // unroll, t % unroll)
    with eng.Fori(first, count // unroll) as i:
        for u in range(unroll):
            tick(i, u)
    for t in range(count, count + deep):
        tick(t // unroll, t % unroll)


class Work:
    pass


class Chain:

    def __init__(self, eng, sem, base=0):
        self.eng, self.sem, self.base, self.n = eng, sem, base, 0

    def __call__(self, ins):
        self.n += 1
        ins.then_inc(self.sem, 1)
        self.eng.wait_ge(self.sem, self.base + self.n)


def layernorm_stats(nc, eng, link, x, w):
    st = w.bnst
    v = nc.vector
    for u in range(NT):
        ins = v.bn_stats(st[:, u, :], x[:, u, :])
    link(ins)
    link(v.tensor_tensor(w.mean[:], st[:, :, 1], st[:, :, 4], ALU.add))
    link(v.tensor_tensor(w.t0[:], st[:, :, 1], st[:, :, 4], ALU.subtract))
    link(v.tensor_tensor(w.t1[:], st[:, :, 2], st[:, :, 5], ALU.add))
    link(v.tensor_tensor(w.t0[:], w.t0[:], w.t0[:], ALU.mult))
    link(v.tensor_scalar(w.t1[:], w.t1[:], 1.0 / C, EPS, ALU.mult, ALU.add))
    link(v.tensor_scalar(w.mean[:], w.mean[:], 0.5, None, ALU.mult))
    return v.scalar_tensor_tensor(out=w.t1[:], in0=w.t0[:], scalar=0.25, in1=w.t1[:], op0=ALU.mult, op1=ALU.add)


def setup_phase(nc, w, d):
    with ExitStack() as ctx:
        sb = lambda n, s, t=F32: ctx.enter_context(nc.sbuf_tensor(n, s, t))
        ps = lambda n, s, t=F32: ctx.enter_context(nc.psum_tensor(n, s, t))
        sem = lambda n: semaphore_of(nc, ctx, n)
        root_done = sem("root_done")
        csT = sb("csT", [P, 2, NB])
        csS = sb("csS", [P, 2, NB])
        csB = sb("csB", [P, 2 * NB, P])
        wm = sb("wm", [P, 2, 6 * C])
        sgn = sb("sgn", [P, 4 * NB * C])
        mag = sb("mag", [P, 4 * NB * C])
        mps = ps("mps", [P, 2, 6, NB])
        gps = ps("gps", [P, 4, 4, C])
        c_in, x_in, attn_in, cst_in = sem("c_in"), sem("x_in"), sem("attn_in"), sem("cst_in")
        silu_done, cols_done, cols_ps, gate_ps = sem("silu_done"), sem("cols_done"), sem("cols_ps"), sem("gate_ps")
        vst, gate_out, zero_set = sem("vst"), sem("gate_out"), sem("zero_set")
        brow, bperm = sb("brow", [2, C]), sb("bperm", [2, 2, C])
        pb = ps("pb", [P, 4])
        perm_done, bias_ps = sem("perm_done"), sem("bias_ps")
        with nc.Block() as block:
            @block.sync
            def _(sp):
                for l in range(2):
                    with nc.allow_non_contiguous_dma(reason="4 conditioning rows as columns"):
                        sp.dma_start(csT[:, l, :], d.c[l].rearrange("b f -> f b")).then_inc(c_in, 16)
                    sp.dma_start(wm[:, l, :], d.wmod[l]).then_inc(c_in, 16)
                sp.dma_start(w.x[:], d.x.rearrange("b (n p) c -> p (b n) c", p=P)).then_inc(x_in, 16)
                sp.dma_start(w.wqkv[:], d.w_attn).then_inc(attn_in, 16)
                sp.dma_start(brow[:], d.b_attn[0:2 * C].rearrange("(j c) -> j c", j=2)).then_inc(attn_in, 16)
                sp.dma_start(w.ident[:], d.ident).then_inc(attn_in, 16)
                sp.dma_start(w.bv[:], d.b_attn[2 * C:].rearrange("(o c) -> o c", o=1).to_broadcast([P, C])).then_inc(cst_in, 16)
                sp.dma_start(w.bo[:], d.b_proj.rearrange("(o c) -> o c", o=1).to_broadcast([P, C])).then_inc(cst_in, 16)
                sp.dma_start(w.wo[:], d.w_proj).then_inc(cst_in, 16)
                sp.dma_start(w.rope[:], d.rope).then_inc(cst_in, 16)
                sp.dma_start(w.identb[:], d.identb).then_inc(cst_in, 16)
                sp.dma_start(w.maskb[:], d.maskb).then_inc(cst_in, 16)
                for src, dst in ((d.trib, w.trib), (d.onesb, w.onesb), (d.iota, w.iota), (d.flip, w.flip), (d.octal, w.octal)):
                    sp.dma_start(dst[:], src).then_inc(cst_in, 16)
                sp.wait_ge(zero_set, 2)
                for layer in range(2):
                    sp.dma_start(d.xg[layer].rearrange("(p n) c -> p n c", p=P), w.empty[:]).then_inc(w.empty_out, 16)
                sp.wait_ge(cst_in, 16 * 11)

            @block.gpsimd
            def _(pool):
                pool.memset(w.empty[:], 0.0).then_inc(zero_set, 1)
                pool.wait_ge(zero_set, 1)
                pool.iota(w.empty[:, :, C:C + 1].bitcast(U32), pattern=[[1, NSLOT], [0, 1]], base=2 * TOK,
                          channel_multiplier=NSLOT).then_inc(zero_set, 1)

            @block.scalar
            def _(act):
                act.wait_ge(c_in, 64)
                nc.scalar.activation(csS[:], csT[:], ACT.Silu).then_inc(silu_done, 1)
                act.wait_ge(vst, 8)
                nc.scalar.activation(w.t1[:], w.t1[:], ACT.Sqrt).then_inc(root_done, 1)

            @block.vector
            def _(dve):
                dve.wait_ge(x_in, 16)
                link = Chain(dve, vst)
                link(layernorm_stats(nc, dve, link, w.x, w))
                dve.wait_ge(root_done, 1)
                link(nc.vector.reciprocal(w.rstd[:], w.t1[:]))
                dve.wait_ge(silu_done, 1)
                for l in range(2):
                    for b in range(NB):
                        ins = nc.vector.tensor_copy(csB[:, l * NB + b, :], csS[:, l, b:b + 1].to_broadcast([P, P]))
                ins.then_inc(cols_done, 1)
                dve.wait_ge(attn_in, 16 * 3)
                for src, plain, rot in ((w.wqkv[:, 0:C], w.wqk[:, 0], w.wqk[:, 2]), (w.wqkv[:, C:2 * C], w.wqk[:, 1], w.wqk[:, 3]),
                                        (brow[:], bperm[:, 0], bperm[:, 1])):
                    by_head = src.rearrange("p (q h e) -> p q h e", q=NQ, e=HD)
                    plain, rot = (x.rearrange("p (q e h) -> p q h e", q=NQ, e=HD) for x in (plain, rot))
                    nc.vector.tensor_copy(plain, by_head)
                    nc.vector.tensor_scalar(rot[:, :, :, 0:4], by_head[:, :, :, 4:8], -1.0, None, ALU.mult)
                    ins = nc.vector.tensor_copy(rot[:, :, :, 4:8], by_head[:, :, :, 0:4])
                ins.then_inc(perm_done, 1)
                dve.wait_ge(bias_ps, 1)
                nc.vector.tensor_copy(w.bqk[:], pb[:])
                dve.wait_ge(cols_ps, 1)
                link(nc.vector.tensor_copy(w.mod[:], mps[:]))
                for j in (1, 4):
                    ins = nc.vector.tensor_scalar(w.mod[:, :, j, :], w.mod[:, :, j, :], 1.0, None, ALU.add)
                link(ins)
                gb = w.gate[:].rearrange("p a b c -> p (a b c)")
                g = gb
                dve.wait_ge(gate_ps, 1)
                nc.vector.tensor_copy(gb, gps[:].rearrange("p a b c -> p (a b c)")).then_inc(gate_out, 1)
                dve.wait_ge(gate_out, 1)
                link(nc.vector.tensor_scalar(sgn[:], g, 0.0, 2.0, ALU.is_ge, ALU.mult))
                link(nc.vector.tensor_scalar(mag[:], g, -1.0, None, ALU.mult))
                link(nc.vector.tensor_tensor(mag[:], mag[:], g, ALU.max))
                link(nc.vector.tensor_scalar(mag[:], mag[:], 0.25, None, ALU.max))
                link(nc.vector.scalar_tensor_tensor(out=gb, in0=sgn[:], scalar=-1.0, in1=mag[:], op0=ALU.add, op1=ALU.mult))
                dve.wait_ge(gate_ps, 2)
                for l in range(2):
                    nc.vector.tensor_copy(w.modr[:, 2 * l], gps[:, 2 * l])
                    ins = nc.vector.tensor_scalar(w.modr[:, 2 * l + 1], gps[:, 2 * l + 1], 1.0, None, ALU.add)
                ins.then_inc(gate_out, 1)
                dve.wait_ge(gate_ps, 3)
                nc.vector.tensor_copy(w.moda[:, 0], gps[:, 2])
                nc.vector.tensor_scalar(w.moda[:, 1], gps[:, 3], 1.0, None, ALU.add)

            @block.tensor
            def _(pe):
                pe.wait_ge(silu_done, 1)
                for l in range(2):
                    for j in range(6):
                        ins = nc.tensor.matmul(mps[:, l, j, :], wm[:, l, j * C:(j + 1) * C], csS[:, l, :], start=True, stop=True)
                ins.then_inc(cols_ps, 1)
                pe.wait_ge(perm_done, 1)
                for a in range(2):
                    ins = nc.tensor.transpose(pb[:, 2 * a:2 * a + 2], bperm[:, a, :], w.ident[0:2, 0:2])
                ins.then_inc(bias_ps, 1)
                pe.wait_ge(cols_done, 1)
                for rnd, comps in enumerate(((2, 5), (3, 4), (0, 1))):
                    pe.wait_ge(gate_out, rnd)
                    for l in range(2):
                        for a, j in enumerate(comps):
                            for b in range(NB):
                                ins = nc.tensor.matmul(gps[:, 2 * l + a, b, :], csB[:, l * NB + b, :], wm[:, l, j * C:(j + 1) * C],
                                                       start=True, stop=True)
                    ins.then_inc(gate_ps, 1)


def qkv_phase(nc, w, d):
    with ExitStack() as ctx:
        sb = lambda n, s, t=F32: ctx.enter_context(nc.sbuf_tensor(n, s, t))
        ps = lambda n, s, t=F32: ctx.enter_context(nc.psum_tensor(n, s, t))
        sem = lambda n: semaphore_of(nc, ctx, n)
        xn = [sb(f"xn{u}", [P, 4, C]) for u in range(2)]
        hT = [sb(f"hTq{u}", [P, ST]) for u in range(2)]
        raw = [sb(f"raw{u}", [P, 4, ST]) for u in range(2)]
        res = [sb(f"res{u}", [P, 2, ST]) for u in range(2)]
        term = [[sb(f"term{u}_{n}", [P, 2, ST], BF16) for n in range(3)] for u in range(2)]
        pT = ps("pT", [P, 2, ST])
        pq = ps("pq", [P, 4, ST])
        pv = ps("pv", [P, 2, ST])
        norm_done, tr_done, h_done, qk_ps, v_ps = sem("norm_done"), sem("tr_done"), sem("h_done"), sem("qk_ps"), sem("v_ps")
        qk_out, v_out, sin_done = sem("qk_out"), sem("v_out"), sem("sin_done")
        cos_done, rope_done, hi_done, r1_done, mid_done, lo_done = (sem("cos_done"), sem("rope_done"), sem("hi_done"),
                                                                   sem("r1_done"), sem("mid_done"), sem("lo_done"))
        stored = [sem(f"stored{u}") for u in range(2)]
        NS = 2 * NB
        with nc.Block() as block:
            @block.vector
            def _(dve):
                def norm(b, u):
                    s = 2 * b + u
                    after(dve, tr_done, s - 1)
                    for j in range(4):
                        t = b * TPB + u * 4 + j
                        ins = nc.vector.tensor_scalar(xn[u][:, j, :], w.x[:, t, :], w.mean[:, bass.ds(t, 1)],
                                                      w.rstd[:, bass.ds(t, 1)], ALU.subtract, ALU.mult)
                    ins.then_inc(norm_done, 1)

                def cos(b, u):
                    dve.wait_ge(qk_out, 4 * (2 * b + u) + 2)
                    cosb = w.rope[:, 0:1, u * ST:(u + 1) * ST].to_broadcast([P, 2, ST])
                    nc.vector.tensor_tensor(raw[u][:, 0:2, :], raw[u][:, 0:2, :], cosb, ALU.mult).then_inc(cos_done, 1)

                def value(b, u):
                    dve.wait_ge(v_ps, 2 * b + u + 1)
                    vt = w.v[:].rearrange("p (b q) k c -> p b k q c", q=NQ)[:, bass.ds(b, 1), u * 4:u * 4 + 4, :, :]
                    for j in range(4):
                        ins = nc.vector.tensor_tensor(vt[:, 0, j], pv[:, u, j * C:(j + 1) * C].rearrange("p (q c) -> p q c", q=NQ),
                                                      w.bv[:].rearrange("p (q c) -> p q c", q=NQ), ALU.add)
                    ins.then_inc(v_out, 1)

                def rotate(b, u):
                    s = 2 * b + u
                    dve.wait_ge(cos_done, s + 1)
                    dve.wait_ge(sin_done, s + 1)
                    q = raw[u][:, 0:2, :]
                    nc.vector.tensor_tensor(q, q, raw[u][:, 2:4, :], ALU.add).then_inc(rope_done, 1)

                def split(b, u):
                    s = 2 * b + u
                    dve.wait_ge(hi_done, s + 1)
                    nc.vector.tensor_tensor(res[u][:], raw[u][:, 0:2, :], term[u][0][:], ALU.subtract).then_inc(r1_done, 1)
                    dve.wait_ge(mid_done, s + 1)
                    nc.vector.tensor_tensor(term[u][2][:], res[u][:], term[u][1][:], ALU.subtract).then_inc(lo_done, 1)
                staged(dve, NS, (1, cos), (0, norm), (1, rotate), (1, value), (1, split))

            @block.gpsimd
            def _(pool):
                def sin(b, u):
                    pool.wait_ge(qk_out, 4 * (2 * b + u) + 4)
                    sinb = w.rope[:, 1:2, u * ST:(u + 1) * ST].to_broadcast([P, 2, ST])
                    nc.gpsimd.tensor_tensor(raw[u][:, 2:4, :], raw[u][:, 2:4, :], sinb, ALU.mult).then_inc(sin_done, 1)
                staged(pool, NS, (0, sin))

            @block.scalar
            def _(act):
                count = act.alloc_register("qkv_count")

                def bias(b, u):
                    s = 2 * b + u
                    after(act, lo_done, s - 1)
                    for n in range(4):
                        act.wait_ge(qk_ps, 4 * s + n + 1)
                        nc.scalar.activation(raw[u][:, n, :], pq[:, n, :], ACT.Identity,
                                             bias=w.bqk[:, n:n + 1]).then_inc(qk_out, 1)

                def modulate(b, u):
                    s = 2 * b + u
                    after(act, v_ps, s - 1)
                    wait_before(act, count, tr_done, s + 1, norm_done)
                    nc.scalar.activation(hT[u][:], pT[:, u, :], ACT.Identity, bias=w.mod[:, 0, 0, bass.ds(b, 1)],
                                         scale=w.mod[:, 0, 1, bass.ds(b, 1)]).then_inc(h_done, 1)

                def split(b, u):
                    s = 2 * b + u
                    act.wait_ge(rope_done, s + 1)
                    after(act, stored[u], b * 16 * 3)
                    nc.scalar.copy(term[u][0][:], raw[u][:, 0:2, :]).then_inc(hi_done, 1)
                    act.wait_ge(r1_done, s + 1)
                    nc.scalar.copy(term[u][1][:], res[u][:]).then_inc(mid_done, 1)
                staged(act, NS, (1, bias), (0, modulate), (1, split))

            @block.tensor
            def _(pe):
                def project(b, u):
                    s = 2 * b + u
                    pe.wait_ge(h_done, s + 1)
                    for n in range(4):
                        after(pe, qk_out, 4 * (s - 1) + n + 1)
                        nc.tensor.matmul(pq[:, n, :], w.wqk[:, n, :], hT[u][:], start=True, stop=True).then_inc(qk_ps, 1)
                    after(pe, v_out, s - 1)
                    for j in range(4):
                        ins = nc.tensor.matmul(pv[:, u, j * C:(j + 1) * C], hT[u][:, j * C:(j + 1) * C],
                                               w.wqkv[:, 2 * C:3 * C], start=True, stop=True)
                    ins.then_inc(v_ps, 1)

                def transpose(b, u):
                    s = 2 * b + u
                    pe.wait_ge(norm_done, s + 1)
                    after(pe, h_done, s - 1)
                    for j in range(4):
                        ins = nc.tensor.transpose(pT[:, u, j * C:(j + 1) * C], xn[u][:, j, :], w.ident[:])
                    ins.then_inc(tr_done, 1)
                staged(pe, NS, (1, project), (0, transpose))

            @block.sync
            def _(sp):
                def store(b, u):
                    s = 2 * b + u
                    for n, ready in enumerate((hi_done, mid_done, lo_done)):
                        sp.wait_ge(ready, s + 1)
                        dst = d.qk[:, :, n].rearrange("s b c t -> b c s t")[bass.ds(b, 1), :, :, u * ST:(u + 1) * ST][0]
                        sp.dma_start(dst, term[u][n][:]).then_inc(stored[u], 16)
                staged(sp, NS, (0, store))
                for u in range(2):
                    sp.wait_ge(stored[u], NB * 16 * 3)
                sp.wait_ge(w.empty_out, 32)


CHUNKS = [
    (0, [(0, 0, 512, 0)]),
    (0, [(1, 128, 384, 0), (3, 384, 128, 384)]),
    (0, [(2, 256, 256, 0)]),
    (1, [(0, 512, 512, 0)]), (1, [(1, 512, 512, 0)]), (1, [(2, 512, 512, 0)]), (1, [(3, 512, 512, 0)]),
    (1, [(4, 512, 512, 0)]),
    (1, [(5, 640, 384, 0), (7, 896, 128, 384)]),
    (1, [(6, 768, 256, 0)]),
]
NCH = len(CHUNKS)
HALF_END = [2, 9]
SITEMS = ([(0, [0, 1, 2, 3], 128), (1, [0, 1, 2, 3], 256), (2, [0, 1], 512), (2, [2, 3], 512), (3, [0, 1], 512), (3, [2, 3], 512)]
          + [(i, [h], 1024) for i in range(4, 8) for h in range(4)])
PLAN = {c: [] for c in range(NCH)}
for _n, _it in enumerate(sorted(range(len(SITEMS)), key=lambda n: SITEMS[n][0])):
    PLAN[min(_n * 8 // len(SITEMS), 7)].append(_it)
MAXT, O0, O1 = "max", "o0", "o1"


def items_of(first, nxt):
    out = []
    for c in range(NCH):
        here = [("s", n) for n in PLAN[c]] if nxt else []
        if c == 2 and not first:
            here.append((O1, None))
        if c == 6:
            here.append((O0, None))
        if c == 8 and nxt:
            here.append((MAXT, None))
        out.append(here)
    return out


def attention_phase(nc, w, d):
    with ExitStack() as ctx:
        sb = lambda n, s, t=F32: ctx.enter_context(nc.sbuf_tensor(n, s, t))
        ps = lambda n, s, t=F32: ctx.enter_context(nc.psum_tensor(n, s, t))
        sem = lambda n: semaphore_of(nc, ctx, n)
        qa = [sb(f"qa{p}", [P, HQ, T], BF16) for p in range(2)]
        ka = [sb(f"ka{p}", [P, HQ, T], BF16) for p in range(2)]
        qb = [sb(f"qb{p}", [P, HQ, T], BF16) for p in range(2)]
        kb = [sb(f"kb{p}", [P, HQ, T], BF16) for p in range(2)]
        vs = [sb(f"vs{p}", [P, TPB, HQ, 32]) for p in range(2)]
        prob = [sb(f"prob{p}", [P, HQ, ST]) for p in range(2)]
        osb = [sb(f"osb{p}", [P, ST]) for p in range(2)]
        part = [sb(f"part{p}", [P, HQ, TPB]) for p in range(2)]
        mrow = [sb(f"mrow{p}", [HQ * TPB, 2, P], BF16) for p in range(2)]
        rec = [sb(f"rec{p}", [P, 4, HQ]) for p in range(2)]
        sps = [ps(f"sps{p}", [P, 2 * ST]) for p in range(2)]
        tps = ps("tps", [P, 3, ST])
        ops = ps("ops", [P, ST])
        s_ready, s_free, t_ready, exp_done, masked = sem("s_ready"), sem("s_free"), sem("t_ready"), sem("exp_done"), sem("masked")
        pv_done, o_out, v_copied, rec_done, zeroed = (sem("pv_done"), sem("o_out"), sem("v_copied"),
                                                     sem("rec_done"), sem("zeroed"))
        max_hi, ones_set = sem("max_hi"), sem("ones_set")
        a_in = [sem(f"a_in{p}") for p in range(2)]
        b_in = [sem(f"b_in{p}") for p in range(2)]
        m_in = [sem(f"m_in{p}") for p in range(2)]

        NS = len(SITEMS)
        LOADED = 6 * 16
        first_items = sum(len(x) for x in items_of(True, True))
        body_items = sum(len(x) for x in items_of(False, True))

        def item_base(t):
            return (NS + 1) if isinstance(t, int) and t == 0 else (NS + 1 + first_items - body_items) + body_items * t

        def sched(t, p, first, nxt):
            return items_of(first, nxt)

        mask_count = [0]
        for half, parts in CHUNKS:
            mask_count.append(mask_count[-1] + sum(1 for j, q0, n, col in parts if q0 == j * P))
        NM = mask_count[-1]

        def bodies(eng, body):
            body(0, 0, True, True)
            with eng.Fori(0, (NQUAD - 2) // 2) as i:
                body(2 * i + 1, 1, False, True)
                body(2 * i + 2, 0, False, True)
            body(NQUAD - 1, 1, False, False)

        with nc.Block() as block:
            @block.gpsimd
            def _(pool):
                for p in range(2):
                    for z in (qa[p], ka[p], qb[p], kb[p]):
                        pool.memset(z[:].rearrange("p h t -> p (h t)").bitcast(F32), 0.0)
                    ins = pool.memset(vs[p][:], 0.0)
                ins.then_inc(zeroed, 1)
                pool.wait_ge(zeroed, 1)
                for p in range(2):
                    ins = pool.memset(vs[p][:, :, :, HD:HD + 1], 1.0)
                ins.then_inc(zeroed, 1)
                pool.wait_ge(zeroed, 2)

                def copy_v(t, p):
                    src = w.v[:, t] if isinstance(t, int) else w.v[:, bass.ds(t, 1)][:, 0]
                    nc.gpsimd.tensor_copy(vs[p][:, :, :, 0:HD], src.rearrange("p k (h e) -> p k h e", h=HQ)).then_inc(v_copied, 1)

                def body(t, p, first, nxt):
                    for c, (half, parts) in enumerate(CHUNKS):
                        if mask_count[c + 1] > mask_count[c]:
                            wait_before(pool, count, exp_done, 4 * NCH * t + 4 * (c + 1), t_ready)
                        for j, q0, n, col in parts:
                            if q0 == j * P:
                                blk = prob[c % 2][:, :, col:col + P]
                                nc.gpsimd.affine_select(out=blk, in_=blk, pattern=[[0, HQ], [1, P]], compare_op=ALU.is_ge,
                                                        fill=0.0, base=0, channel_multiplier=-1).then_inc(masked, 1)
                        if c == 2 and nxt:
                            if not (isinstance(t, int) and t == 0):
                                pool.wait_ge(pv_done, NCH * t)
                            copy_v(t + 1, 1 - p)
                count = pool.alloc_register("exp_count")
                copy_v(0, 0)
                bodies(pool, body)

            @block.sync
            def _(sp):
                def load(t, p, s_in, qq, kk):
                    b, quad = (t // NQ, t % NQ) if isinstance(t, int) else (t >> 2, t & (NQ - 1))
                    row = 0
                    for n, rows in enumerate((3, 2, 1)):
                        for side, buf, term, step in ((0, qq, n, 0), (1, kk, 0, C * T)):
                            at = b * (3 * C * T) + quad * (HD * HQ * T) + (side * NB * 3 + term) * (C * T)
                            src = bass.AP(d.qk.tensor, at, [[step, rows], [HQ * T, HD], [1, HQ * T]])
                            sp.dma_start(buf[row * HD:(row + rows) * HD, :, :].rearrange("p h t -> p (h t)"), src).then_inc(s_in, 16)
                        row += rows

                sp.wait_ge(zeroed, 1)
                sp.wait_ge(ones_set, 1)
                load(0, 0, a_in[0], qa[0], ka[0])
                load(0, 0, b_in[0], qb[0], kb[0])
                load(1, 1, a_in[1], qa[1], ka[1])
                load(1, 1, b_in[1], qb[1], kb[1])

                def max_to_rows(n, p):
                    sp.wait_ge(s_free, item_base(n))
                    for r in range(2):
                        sp.dma_start(qb[p][MROW + r:MROW + r + 1, :, :].rearrange("o h (k q) -> o (h k) q", k=TPB),
                                     mrow[p][:, r, :]).then_inc(m_in[p], 16)
                max_to_rows(0, 0)

                def body(t, p, first, nxt):
                    if nxt:
                        tn = t + 2
                        if not isinstance(t, int):
                            tn = (t + 2) & (NQUAD - 1)
                        load(tn, p, a_in[p], qa[p], ka[p])
                    if nxt:
                        max_to_rows(t + 1, 1 - p)
                        sp.wait_ge(t_ready, 4 * NCH * (t + 1))
                        load(tn, p, b_in[p], qb[p], kb[p])
                bodies(sp, body)
                for p in range(2):
                    sp.wait_ge(a_in[p], LOADED * (NQUAD // 2 + (1 if p == 0 else 0)))
                    sp.wait_ge(b_in[p], LOADED * (NQUAD // 2 + (1 if p == 0 else 0)))

            @block.tensor
            def _(pe):
                item = [0, 0]

                def slot():
                    return sps[(item[1] + par[0]) % 2]

                par = [0]

                def acquire():
                    n = item[0] + item[1]
                    if not (isinstance(n, int) and n < 2):
                        pe.wait_ge(s_free, n - 1)

                def filled(ins):
                    ins.then_inc(s_ready, 1)
                    item[1] += 1

                def s_item(n, p):
                    i, heads, step = SITEMS[n]
                    acquire()
                    out = slot()
                    for x, h in enumerate(heads):
                        for c0 in range(0, (i + 1) * P, ST):
                            n1 = min(ST, (i + 1) * P - c0)
                            diag = c0 + n1 == (i + 1) * P
                            ins = nc.tensor.matmul(out[:, x * step + c0:x * step + c0 + n1], qa[p][:, h, i * P:(i + 1) * P],
                                                   ka[p][:, h, c0:c0 + n1], start=True, stop=not diag, skip_group_check=True)
                        e = x * step + i * P
                        ins = nc.tensor.matmul(out[:, e:e + P], w.identb[:], w.maskb[:], start=False, stop=True, skip_group_check=True)
                    filled(ins)

                def max_item(n, p, last):
                    pe.wait_ge(s_free, last)
                    acquire()
                    filled(nc.tensor.transpose(slot()[0:HQ * TPB, 0:P], part[p][:].rearrange("p h k -> p (h k)"), w.ident[:]))

                def o_item(half, count):
                    pe.wait_ge(o_out, count)
                    acquire()
                    out = slot()
                    for x in range(4):
                        ins = nc.tensor.transpose(out[:, x * P:(x + 1) * P], osb[half][:, x * P:(x + 1) * P], w.ident[:])
                    filled(ins)

                def pv(t, p, c):
                    half, parts = CHUNKS[c]
                    if mask_count[c + 1] > mask_count[c]:
                        pe.wait_ge(masked, NM * t + mask_count[c + 1])
                    else:
                        pe.wait_ge(exp_done, 4 * NCH * t + 4 * (c + 1))
                    if c == 0:
                        pe.wait_ge(v_copied, t + 1)
                    new = c == 0 or c == HALF_END[0] + 1
                    if new:
                        n = 2 * t + half
                        if not (isinstance(n, int) and n == 0):
                            pe.wait_ge(o_out, n)
                    for j, q0, n, col in parts:
                        o0 = q0 - half * ST
                        for h in range(HQ):
                            ins = nc.tensor.matmul(ops[32 * h:32 * h + 32, o0:o0 + n], vs[p][:, j, h, :],
                                                   prob[c % 2][:, h, col:col + n], start=new, stop=c in HALF_END,
                                                   skip_group_check=True, tile_position=(0, 32 * h))
                    ins.then_inc(pv_done, 1)

                def body(t, p, first, nxt):
                    base = item_base(t)
                    item[0], item[1] = base, 0
                    par[0] = (NS + 1 + (0 if first else first_items) + (0 if first or p == 1 else body_items)) % 2
                    todo = items_of(first, nxt)
                    done = 0
                    for c, (half, parts) in enumerate(CHUNKS):
                        if c == 0:
                            pe.wait_ge(b_in[p], quads(t, p, LOADED))
                            pe.wait_ge(m_in[p], quads(t, p, 2 * 16))
                        todo_c = list(todo[c])
                        for h in range(HQ):
                            k = 4 * c + h
                            prev = 4 * NCH * t + k - 2 if k >= 3 else 4 * NCH * (t - 1) + {0: 40, 1: 38, 2: 39}[k]
                            if not (isinstance(prev, int) and prev <= 0):
                                pe.wait_ge(exp_done, prev)
                            for j, q0, n, col in parts:
                                ins = nc.tensor.matmul(tps[:, k % 3, col:col + n], kb[p][:, h, j * P:(j + 1) * P],
                                                       qb[p][:, h, q0:q0 + n], start=True, stop=True)
                            ins.then_inc(t_ready, 1)
                            if h in (1, 2) and todo_c and todo_c[0][0] == "s":
                                if done == 0:
                                    pe.wait_ge(a_in[1 - p], quads(t + 1, 1 - p, LOADED))
                                s_item(todo_c.pop(0)[1], 1 - p)
                                done = item[1]
                        if c > 0:
                            pv(t, p, c - 1)
                        elif not first:
                            pv(t - 1, 1 - p, NCH - 1)
                        for kind, n in todo_c:
                            if kind == "s":
                                s_item(n, 1 - p)
                                done = item[1]
                            elif kind == O1:
                                o_item(1, 2 * t)
                            elif kind == O0:
                                o_item(0, 2 * t + 1)
                            else:
                                max_item(t + 1, 1 - p, base + done)

                def quads(t, p, signals):
                    return signals * (t // 2 + 1) if isinstance(t, int) else signals // 2 * (t - p) + signals

                pe.wait_ge(a_in[0], LOADED)
                for n in range(NS):
                    s_item(n, 0)
                max_item(0, 0, NS)
                bodies(pe, body)
                t = NQUAD - 1
                pv(t, 1, NCH - 1)
                o_item(1, 2 * NQUAD)

            @block.scalar
            def _(act):
                def o_copy(half):
                    nc.scalar.copy(osb[half][:], ops[:]).then_inc(o_out, 1)

                def body(t, p, first, nxt):
                    for c, (half, parts) in enumerate(CHUNKS):
                        n = sum(x[2] for x in parts)
                        for h in range(HQ):
                            k = 4 * c + h
                            act.wait_ge(t_ready, 4 * NCH * t + k + 1)
                            if h == 0:
                                v = NCH * t + c - 1
                                if not (isinstance(v, int) and v <= 0):
                                    act.wait_ge(pv_done, v)
                            nc.scalar.activation(prob[c % 2][:, h, 0:n], tps[:, k % 3, 0:n], ACT.Exp,
                                                 scale=float(HD) ** -0.5).then_inc(exp_done, 1)
                        if c == 0 and not first:
                            act.wait_ge(pv_done, NCH * t)
                            o_copy(1)
                        if c == 3:
                            act.wait_ge(pv_done, NCH * t + 3)
                            o_copy(0)
                bodies(act, body)
                act.wait_ge(pv_done, NCH * NQUAD)
                o_copy(1)

            @block.vector
            def _(dve):
                item = [0, 0]
                par = [0]

                def ready():
                    dve.wait_ge(s_ready, item[0] + item[1] + 1)
                    return sps[(item[1] + par[0]) % 2]

                def freed(ins):
                    ins.then_inc(s_free, 1)
                    item[1] += 1

                def s_item(n, p):
                    i, heads, step = SITEMS[n]
                    src = ready()
                    wd = (i + 1) * P
                    if len(heads) > 1:
                        src = src[:, 0:len(heads) * step].rearrange("p (h k) -> p h k", h=len(heads))[:, :, 0:wd]
                    else:
                        src = src[:, 0:wd].rearrange("p (h k) -> p h k", h=1)
                    freed(nc.vector.tensor_reduce(part[p][:, heads[0]:heads[-1] + 1, i:i + 1].rearrange("p h o -> p (h o)"),
                                                  src, AX.X, ALU.max, negate=True))

                def max_item(n, p):
                    src = ready()
                    nc.vector.tensor_copy(mrow[p][:, 0, :], src[0:HQ * TPB, 0:P]).then_inc(max_hi, 1)
                    dve.wait_ge(max_hi, n + 1)
                    ins = nc.vector.tensor_tensor(mrow[p][:, 1, :], src[0:HQ * TPB, 0:P], mrow[p][:, 0, :], ALU.subtract)
                    freed(ins)

                def o_item(t, half):
                    src = ready()[:, 0:ST].rearrange("p (x h e) -> p x h e", x=4, h=HQ)
                    nc.vector.reciprocal(rec[half][:], src[:, :, :, HD]).then_inc(rec_done, 1)
                    dve.wait_ge(rec_done, 2 * t + half + 1)
                    dst = (w.y[:, t] if isinstance(t, int) else w.y[:, bass.ds(t, 1)][:, 0])[:, half * 4:half * 4 + 4, :]
                    recb = rec[half][:].rearrange("p x (h o) -> p x h o", o=1).to_broadcast([P, 4, HQ, HD])
                    freed(nc.vector.tensor_tensor(dst.rearrange("p x (h e) -> p x h e", h=HQ), src[:, :, :, 0:HD], recb, ALU.mult))

                def body(t, p, first, nxt):
                    item[0], item[1] = item_base(t), 0
                    par[0] = (NS + 1 + (0 if first else first_items) + (0 if first or p == 1 else body_items)) % 2
                    for here in items_of(first, nxt):
                        for kind, n in here:
                            if kind == "s":
                                s_item(n, 1 - p)
                            elif kind == O1:
                                o_item(t - 1, 1)
                            elif kind == O0:
                                o_item(t, 0)
                            else:
                                max_item(t + 1, 1 - p)
                dve.wait_ge(zeroed, 1)
                for p in range(2):
                    ins = nc.vector.memset(kb[p][MROW:MROW + 2, :, :], 1.0)
                ins.then_inc(ones_set, 1)
                for n in range(NS):
                    s_item(n, 0)
                max_item(0, 0)
                bodies(dve, body)
                o_item(NQUAD - 1, 1)


def project_phase(nc, w, d):
    with ExitStack() as ctx:
        sb = lambda n, s, t=F32: ctx.enter_context(nc.sbuf_tensor(n, s, t))
        ps = lambda n, s, t=F32: ctx.enter_context(nc.psum_tensor(n, s, t))
        sem = lambda n: semaphore_of(nc, ctx, n)
        ys = [sb(f"ys{u}", [P, 4, C]) for u in range(2)]
        yT = [sb(f"yT{u}", [P, ST]) for u in range(2)]
        o = [sb(f"o{u}", [P, 4, C]) for u in range(2)]
        pT = ps("pTo", [P, 2, ST])
        po = ps("po", [P, 2, ST])
        y_in, y_tr, y_T, o_ps, o_step, x_done = sem("y_in"), sem("y_tr"), sem("y_T"), sem("o_ps"), sem("o_step"), sem("x_done")
        with nc.Block() as block:
            @block.scalar
            def _(act):
                def rows(b, u):
                    after(act, y_tr, 2 * b + u - 1)
                    yb = w.y[:].rearrange("p (b q) k c -> p b k q c", q=NQ)[:, bass.ds(b, 1), u * 4:u * 4 + 4, :, :]
                    for j in range(4):
                        ins = nc.scalar.copy(ys[u][:, j, :].rearrange("p (q c) -> p q c", q=NQ), yb[:, 0, j])
                    ins.then_inc(y_in, 1)
                staged(act, 2 * NB, (0, rows))

            @block.tensor
            def _(pe):
                def transpose(b, u):
                    s = 2 * b + u
                    pe.wait_ge(y_in, s + 1)
                    after(pe, y_T, s - 1)
                    for j in range(4):
                        ins = nc.tensor.transpose(pT[:, u, j * C:(j + 1) * C], ys[u][:, j, :], w.ident[:])
                    ins.then_inc(y_tr, 1)

                def project(b, u):
                    s = 2 * b + u
                    pe.wait_ge(y_T, s + 1)
                    after(pe, x_done, s - 1)
                    for j in range(4):
                        ins = nc.tensor.matmul(po[:, u, j * C:(j + 1) * C], yT[u][:, j * C:(j + 1) * C], w.wo[:], start=True, stop=True)
                    ins.then_inc(o_ps, 1)
                staged(pe, 2 * NB, (0, transpose), (1, project))

            @block.vector
            def _(dve):
                def transposed(b, u):
                    s = 2 * b + u
                    dve.wait_ge(y_tr, s + 1)
                    after(dve, o_ps, s - 1)
                    nc.vector.tensor_copy(yT[u][:], pT[:, u, :]).then_inc(y_T, 1)

                def residual(b, u):
                    s = 2 * b + u
                    dve.wait_ge(o_ps, s + 1)
                    link = Chain(dve, o_step, 2 * s)
                    bo4 = w.bo[:].rearrange("p (o c) -> p o c", o=1).to_broadcast([P, 4, C])
                    link(nc.vector.tensor_tensor(o[u][:], po[:, u, :].rearrange("p (j c) -> p j c", j=4), bo4, ALU.add))
                    g4 = w.gate[:, 0, bass.ds(b, 1), :].to_broadcast([P, 4, C])
                    link(nc.vector.tensor_tensor(o[u][:], o[u][:], g4, ALU.mult))
                    xs = w.x[:, bass.ds(b * TPB + u * 4, 4), :]
                    nc.vector.tensor_tensor(xs, xs, o[u][:], ALU.add).then_inc(x_done, 1)
                staged(dve, 2 * NB, (0, transposed), (1, residual))


def stats_phase(nc, w, name, d=None, layer=None):
    with ExitStack() as ctx:
        sem = lambda n: semaphore_of(nc, ctx, n + name)
        st_step, root, r_in, r_tr = sem("st_step"), sem("root"), sem("r_in"), sem("r_tr")
        if layer is not None:
            rows = ctx.enter_context(nc.sbuf_tensor(f"router_rows{layer}", [NE + 1, C], F32))
            rt_ps = ctx.enter_context(nc.psum_tensor(f"router_ps{layer}", [P, NE + 1], F32))
            NR = NE + 1 - layer
        with nc.Block() as block:
            @block.sync
            def _(sp):
                if layer is not None:
                    sp.dma_start(rows[0:NE, :], (d.gate_w, d.wg)[layer]).then_inc(r_in, 16)
                    if layer == 0:
                        sp.dma_start(rows[NE:NE + 1, :], d.seg).then_inc(r_in, 16)

            @block.tensor
            def _(pe):
                if layer is not None:
                    pe.wait_ge(r_in, 16 * (2 - layer))
                    nc.tensor.transpose(rt_ps[:, 0:NR], rows[0:NR, :], w.ident[0:NR, 0:NR]).then_inc(r_tr, 1)

            @block.vector
            def _(dve):
                link = Chain(dve, st_step)
                link(layernorm_stats(nc, dve, link, w.x, w))
                if layer is not None:
                    dve.wait_ge(r_tr, 1)
                    nc.vector.tensor_copy(w.rt[:], rt_ps[:, 0:NR])
                dve.wait_ge(root, 1)
                nc.vector.reciprocal(w.rstd[:], w.t1[:])

            @block.scalar
            def _(act):
                act.wait_ge(st_step, 8)
                nc.scalar.activation(w.t1[:], w.t1[:], ACT.Sqrt).then_inc(root, 1)


NE = 8
SI = 352
XW = C + 2
NSLOT = 2 * NT + NE
UN = 8
LAG = 2


def chunks_of(width):
    return {176: [88, 88], 352: [128, 128, 96]}[width]


def weights_parts(nc, w, d, layer, ctx, up_banks, down_banks):
    I = (176, 352)[layer]
    NK = layer + 1
    R = 88
    WB = 4
    sb = lambda n, s, t=F32: ctx.enter_context(nc.sbuf_tensor(f"{n}_w{layer}", s, t))
    sem = lambda n: semaphore_of(nc, ctx, f"{n}_w{layer}")
    rows = [sb(f"rows{u}", [R, 2, 4, C]) for u in range(WB)]
    dn = [sb(f"dn{u}", [P, 352]) for u in range(WB)]
    w_in = [sem(f"w_in{u}") for u in range(WB)]
    w_tr, w_out = sem("w_tr"), sem("w_out")
    ups, down = ((d.gu0,), d.dn0) if layer == 0 else ((d.w1, d.w2), d.w3)
    at = lambda a, e: a[:, e] if isinstance(e, int) else a[:, bass.ds(e, 1)][:, 0]

    def loads(sp):
        def load(i, u):
            e = WB * i + u
            after(sp, w_tr, e - WB + 1)
            pick = lambda a: a[e] if isinstance(e, int) else a[bass.ds(e, 1)][0]
            for k, src in enumerate(ups):
                sp.dma_start(rows[u][:, k], pick(src).rearrange("(n p) c -> p n c", p=R)).then_inc(w_in[u], 16)
            sp.dma_start(dn[u][:, 0:I], pick(down)).then_inc(w_in[u], 16)
        staged(sp, NE, (0, load), unroll=WB)
        if layer == 0:
            sp.wait_ge(w_tr, NE - WB + 1)
            for k, src in enumerate((d.sg, d.su)):
                sp.dma_start(rows[0][:, k], src.rearrange("(n p) c -> p n c", p=R)).then_inc(w_in[0], 16)
            sp.dma_start(dn[0][:], d.sd).then_inc(w_in[0], 16)

    def transposes(pe):
        def up_tr(bank, u, k):
            for m in range(4):
                ins = nc.tensor.transpose(bank[:, m * R:(m + 1) * R], rows[u][:, k, m, :], w.ident[0:R, 0:R])
            return ins

        def down_tr(bank, u, width):
            c0 = 0
            for m, cw in enumerate(chunks_of(width)):
                ins = nc.tensor.transpose(bank[0:cw, m * C:(m + 1) * C], dn[u][:, c0:c0 + cw], w.ident[:])
                c0 += cw
            return ins

        def turn(i, u):
            pe.wait_ge(w_in[u], 16 * (NK + 1) * (i + 1))
            after(pe, w_out, WB * i + u - 1)
            for k in range(NK):
                up_tr(up_banks[u % 2][k], u, k)
            down_tr(down_banks[u % 2], u, I).then_inc(w_tr, 1)
        staged(pe, NE, (0, turn), unroll=WB)
        if layer == 0:
            pe.wait_ge(w_in[0], 16 * (NK + 1) * (NE // WB) + 16 * 3)
            pe.wait_ge(w_out, NE)
            for k in range(2):
                up_tr((up_banks[0] + up_banks[1])[k], 0, k)
            down_tr(down_banks[0], 0, SI).then_inc(w_tr, 1)
            pe.wait_ge(w_out, NE + 1)

    def copies(act):
        def down_out(dst, bank, width):
            cs = chunks_of(width)
            full = [m for m, cw in enumerate(cs) if cw == cs[0]]
            ins = nc.scalar.copy(dst[0:cs[0], 0:len(full), :], bank[0:cs[0], 0:len(full) * C].rearrange("p (m c) -> p m c", c=C))
            if len(full) < len(cs):
                ins = nc.scalar.copy(dst[0:cs[-1], len(full), :], bank[0:cs[-1], len(full) * C:len(cs) * C])
            return ins

        def turn(i, u):
            e = WB * i + u
            act.wait_ge(w_tr, e + 1)
            for k in range(NK):
                nc.scalar.copy(at(w.up, e)[:, k, :], up_banks[u % 2][k][:, 0:352])
            down_out(at(w.down, e), down_banks[u % 2], I).then_inc(w_out, 1)
        staged(act, NE, (0, turn), unroll=WB)
        if layer == 0:
            act.wait_ge(w_tr, NE + 1)
            for k in range(2):
                nc.scalar.copy(w.shgu[:, k, :], (up_banks[0] + up_banks[1])[k][:, 0:352])
            down_out(w.shd, down_banks[0], SI).then_inc(w_out, 1)
    return loads, transposes, copies


def route_phase(nc, w, d, layer):
    NR = NE + 1 if layer == 0 else NE
    cols = chunks_of(SI)
    with ExitStack() as ctx:
        sb = lambda n, s, t=F32: ctx.enter_context(nc.sbuf_tensor(f"{n}_{layer}", s, t))
        sem = lambda n: semaphore_of(nc, ctx, f"{n}_{layer}")
        hs = [sb(f"hs{u}", [P, 4, C]) for u in range(2)]
        hT = sb("hTr", [P, 2 * NB, ST])
        lg = sb("lg", [P, NT, NR])
        r_step, h_done, h_kept, tr_done, hT_done, lg_ps, lg_out = (sem("r_step"), sem("h_done"), sem("h_kept"), sem("tr_done"),
                                                                  sem("hT_done"), sem("lg_ps"), sem("lg_out"))
        with ExitStack() as banks:
            ps = lambda n, s, t=F32: banks.enter_context(nc.psum_tensor(f"{n}_{layer}", s, t))
            hr = [sb(f"hr{u}", [P, ST]) for u in range(2)]
            pT = ps("pTr", [P, 2, ST])
            pl = ps("pl", [P, 2, ST])
            with nc.Block() as block:
                @block.vector
                def _(dve):
                    def rows(b, u):
                        s = 2 * b + u
                        after(dve, tr_done, s - 1)
                        after(dve, h_kept, s - 1)
                        link = Chain(dve, r_step, 2 * s)
                        for j in range(4):
                            t = b * TPB + u * 4 + j
                            ins = nc.vector.tensor_scalar(hs[u][:, j, :], w.x[:, t, :], w.mean[:, bass.ds(t, 1)],
                                                          w.rstd[:, bass.ds(t, 1)], ALU.subtract, ALU.mult)
                        link(ins)
                        link(nc.vector.tensor_tensor(hs[u][:], hs[u][:], w.modr[:, 2 * layer + 1, bass.ds(b, 1), :].to_broadcast([P, 4, C]), ALU.mult))
                        nc.vector.tensor_tensor(hs[u][:], hs[u][:], w.modr[:, 2 * layer, bass.ds(b, 1), :].to_broadcast([P, 4, C]), ALU.add).then_inc(h_done, 1)

                    def logits(b, u):
                        dve.wait_ge(lg_ps, 2 * b + u + 1)
                        nc.vector.tensor_copy(lg[:, bass.ds(b * TPB + u * 4, 4), :],
                                              pl[:, u, 0:4 * NR].rearrange("p (j r) -> p j r", j=4)).then_inc(lg_out, 1)
                    staged(dve, 2 * NB, (0, rows), (1, logits))

                @block.gpsimd
                def _(pool):
                    def keep(b, u):
                        pool.wait_ge(h_done, 2 * b + u + 1)
                        nc.gpsimd.tensor_copy(w.h[:, bass.ds(b * TPB + u * 4, 4), 0:C], hs[u][:]).then_inc(h_kept, 1)
                    nc.gpsimd.iota(w.h[:, :, C:C + 1].bitcast(U32), pattern=[[P, NT], [0, 1]], base=0, channel_multiplier=1)
                    staged(pool, 2 * NB, (0, keep))

                @block.scalar
                def _(act):
                    def transposed(b, u):
                        s = 2 * b + u
                        act.wait_ge(tr_done, s + 1)
                        after(act, lg_ps, s - 1)
                        ins = nc.scalar.copy(hr[u][:], pT[:, u, :])
                        if layer == 0:
                            ins = nc.scalar.copy(hT[:, bass.ds(s, 1), :].rearrange("p o t -> p (o t)"), pT[:, u, :])
                        ins.then_inc(hT_done, 1)
                    staged(act, 2 * NB, (0, transposed))

                @block.tensor
                def _(pe):
                    def transpose(b, u):
                        s = 2 * b + u
                        pe.wait_ge(h_done, s + 1)
                        after(pe, hT_done, s - 1)
                        for j in range(4):
                            ins = nc.tensor.transpose(pT[:, u, j * C:(j + 1) * C], hs[u][:, j, :], w.ident[:])
                        ins.then_inc(tr_done, 1)

                    def logits(b, u):
                        s = 2 * b + u
                        pe.wait_ge(hT_done, s + 1)
                        after(pe, lg_out, s - 1)
                        for j in range(4):
                            ins = nc.tensor.matmul(pl[:, u, j * NR:(j + 1) * NR], hr[u][:, j * C:(j + 1) * C], w.rt[:],
                                                   start=True, stop=True)
                        ins.then_inc(lg_ps, 1)
                    staged(pe, 2 * NB, (1, logits), (0, transpose))

        sc = sb("sc", [P, NT, NE])
        m1 = sb("m1", [P, NT])
        top = sb("top", [P, NT, 8])
        idx = sb("idx", [P, NT, 8], U32)
        idf = sb("idf", [P, NT, 2])
        hot = [sb(f"hot{k}", [P, NE, NT]) for k in range(2)]
        both = sb("both", [P, NE, NT], BF16)
        bsum = sb("bsum", [P, NE * NT])
        ones = sb("ones", [P, NE * NT])
        excl = sb("excl", [P, NE, NT])
        base = sb("base", [P, NE])
        nt = sb("nt", [P, NE])
        off = sb("off", [P, NE])
        tmp = sb("tmp", [P, NE, NT])
        slf = sb("slf", [P, NT])
        ge = sb("ge", [P, NSLOT, NE])
        te = sb("te", [P, NSLOT + UN])
        word = sb("word", [P, NSLOT // UN + 1])
        ps = lambda n, s, t=F32: ctx.enter_context(nc.psum_tensor(f"{n}_{layer}", s, t))
        pp = ps("pp", [P, 2, NE * NT])
        if layer == 0:
            sg = [sb(f"sg{u}", [P, ST]) for u in range(2)]
            hid = [sb(f"hid{u}", [P, ST]) for u in range(2)]
            pg = ps("pg", [P, 2, 2, ST])
            pd = ps("pd", [P, 2, ST])
        g_ps, s_done, hid_done, d_ps, sh_out = sem("g_ps"), sem("s_done"), sem("hid_done"), sem("d_ps"), sem("sh_out")
        q_step, ex_done, both_done, pre_ps = sem("q_step"), sem("ex_done"), sem("both_done"), sem("pre_ps")
        slots_done, scattered, second = sem("slots_done"), w.scattered[layer], sem("second")
        if layer == 0:
            up_banks, down_banks = [[pg[:, 0, 0]], [pg[:, 0, 1]]], [pg[:, 1, 0], pg[:, 1, 1]]
        else:
            gp, dp = ps("gp", [P, 4, ST]), ps("dp", [P, 2, ST])
            up_banks, down_banks = [[gp[:, 2 * u + k] for k in range(2)] for u in range(2)], [dp[:, u] for u in range(2)]
        load_weights, transpose_weights, copy_weights = weights_parts(nc, w, d, layer, ctx, up_banks, down_banks)
        M = len(cols)
        NC = 2 * NB * M
        turn = lambda i, u: 2 * M * i + u
        with nc.Block() as block:
            @block.vector
            def _(dve):
                link = Chain(dve, q_step)
                v = nc.vector
                if layer == 0:
                    link(v.tensor_reduce(m1[:], lg[:, :, 0:NE], AX.X, ALU.max))
                    link(v.tensor_tensor(sc[:], lg[:, :, 0:NE], m1[:].rearrange("p (t o) -> p t o", o=1).to_broadcast([P, NT, NE]), ALU.subtract))
                    dve.wait_ge(ex_done, 2)
                    link(v.tensor_scalar(w.shw[:], w.shw[:], 1.0, None, ALU.add))
                    link(v.reciprocal(w.shw[:], w.shw[:]))
                    link(v.tensor_reduce(m1[:], sc[:], AX.X, ALU.add))
                    link(v.reciprocal(m1[:], m1[:]))
                    link(v.tensor_tensor(sc[:], sc[:], m1[:].rearrange("p (t o) -> p t o", o=1).to_broadcast([P, NT, NE]), ALU.mult))
                else:
                    link(v.tensor_copy(sc[:], lg[:]))
                for t in range(NT):
                    ins = v.max(top[:, t, :], sc[:, t, :])
                link(ins)
                for t in range(NT):
                    ins = v.max_index(idx[:, t, :], top[:, t, :], sc[:, t, :])
                link(ins)
                link(v.tensor_copy(idf[:], idx[:, :, 0:2]))
                eb = w.iota[:, 0:NE].rearrange("p (e o) -> p e o", o=1).to_broadcast([P, NE, NT])
                for k in range(2):
                    ins = v.tensor_tensor(hot[k][:], eb, idf[:, :, k:k + 1].rearrange("p t o -> p o t").to_broadcast([P, NE, NT]), ALU.is_equal)
                link(ins)
                v.tensor_tensor(both[:], hot[0][:], hot[1][:], ALU.add).then_inc(both_done, 1)
                for k in range(2):
                    link(v.tensor_tensor(tmp[:], hot[k][:], sc[:].rearrange("p t e -> p e t"), ALU.mult))
                    link(v.tensor_reduce(w.wt[k][:], tmp[:].rearrange("p e t -> p t e"), AX.X, ALU.add))
                link(v.memset(ones[:], 1.0))
                dve.wait_ge(pre_ps, 1)
                link(v.tensor_copy(bsum[:], pp[:, 1, 0:NE * NT]))
                link(v.tensor_tensor_scan(out=excl[:].rearrange("p e t -> p (e t)"), data0=ones[:], data1=bsum[:], initial=0.0,
                                          op0=ALU.mult, op1=ALU.add))
                link(v.tensor_tensor(excl[:], excl[:], bsum[:].rearrange("p (e t) -> p e t", e=NE), ALU.subtract))
                link(v.tensor_copy(base[:], excl[:, :, 0]))
                link(v.tensor_reduce(nt[:], bsum[:].rearrange("p (e t) -> p e t", e=NE), AX.X, ALU.add))
                link(v.tensor_scalar(nt[:], nt[:], 63.5, 1.0 / P, ALU.add, ALU.mult))
                link(v.tensor_scalar(nt[:], nt[:], 12582912.0, 12582912.0, ALU.add, ALU.subtract))
                link(v.tensor_tensor_scan(out=off[:], data0=ones[:, 0:NE], data1=nt[:], initial=0.0, op0=ALU.mult, op1=ALU.add))
                link(v.tensor_tensor(ge[:], w.iota[:, 0:NSLOT].rearrange("p (i o) -> p i o", o=1).to_broadcast([P, NSLOT, NE]),
                                     off[:].rearrange("p (o e) -> p o e", o=1).to_broadcast([P, NSLOT, NE]), ALU.is_ge))
                link(v.memset(te[:], 0.0))
                link(v.tensor_reduce(te[:, LAG:LAG + NSLOT], ge[:], AX.X, ALU.add))
                link(v.tensor_scalar(te[:, LAG:LAG + NSLOT], te[:, LAG:LAG + NSLOT], float(NE - 1), None, ALU.min))
                digits = te[:].rearrange("p (g j) -> p g j", j=UN)
                link(v.tensor_tensor(digits, digits, w.octal[:].rearrange("p (o j) -> p o j", o=1).to_broadcast([P, NSLOT // UN + 1, UN]), ALU.mult))
                link(v.tensor_reduce(word[:], digits, AX.X, ALU.add))
                link(v.tensor_copy(w.tile_expert[:], word[:]))
                link(v.tensor_tensor(off[:], off[:], nt[:], ALU.subtract))
                link(v.scalar_tensor_tensor(out=off[:], in0=off[:], scalar=float(P), in1=base[:], op0=ALU.mult, op1=ALU.subtract))
                link(v.tensor_tensor(excl[:], excl[:], off[:].rearrange("p (e o) -> p e o", o=1).to_broadcast([P, NE, NT]), ALU.add))
                link(v.tensor_tensor(excl[:], excl[:], pp[:, 0, 0:NE * NT].rearrange("p (e t) -> p e t", e=NE), ALU.add))
                for k in range(2):
                    link(v.tensor_tensor(tmp[:], hot[k][:], excl[:], ALU.mult))
                    link(v.tensor_reduce(slf[:], tmp[:].rearrange("p e t -> p t e"), AX.X, ALU.add))
                    link(v.tensor_copy(w.slot[k][:], slf[:]))
                dve.sem_inc(slots_done, 1)

                def product(i, u):
                    n = turn(i, u)
                    cw = cols[u % M]
                    dve.wait_ge(s_done, n + 1)
                    after(dve, d_ps, n - 1)
                    v.tensor_tensor(hid[u % 2][0:cw, :], sg[u % 2][0:cw, :], pg[0:cw, u % 2, 1, :], ALU.mult).then_inc(hid_done, 1)
                if layer == 0:
                    staged(dve, NC, (0, product), unroll=2 * M)

            @block.scalar
            def _(act):
                def silu(i, u):
                    n = turn(i, u)
                    cw = cols[u % M]
                    act.wait_ge(g_ps, n + 1)
                    after(act, hid_done, n - 1)
                    nc.scalar.activation(sg[u % 2][0:cw, :], pg[0:cw, u % 2, 0, :], ACT.Silu).then_inc(s_done, 1)

                def out(i, u):
                    if u % M == M - 1:
                        wait_before(act, count, d_ps, turn(i, u) + 1, g_ps)
                        for j in range(4):
                            t = i * TPB + u // M * 4 + j
                            ins = nc.scalar.activation(w.sh[:, bass.ds(t, 1), :].rearrange("p o c -> p (o c)"), pd[:, u // M, j * C:(j + 1) * C],
                                                       ACT.Copy, scale=w.shw[:, bass.ds(t, 1)])
                        ins.then_inc(sh_out, 1)
                count = act.alloc_register(f"shared_count_{layer}")
                if layer == 0:
                    act.wait_ge(q_step, 2)
                    nc.scalar.activation(sc[:], sc[:], ACT.Exp).then_inc(ex_done, 1)
                    nc.scalar.activation(w.shw[:], lg[:, :, NE], ACT.Exp, scale=-1.0).then_inc(ex_done, 1)
                copy_weights(act)
                if layer == 0:
                    staged(act, NC, (0, silu), (2, out), unroll=2 * M)

            @block.tensor
            def _(pe):
                def up(i, u):
                    n, m = turn(i, u), u % M
                    after(pe, hid_done, n - 1)
                    rhs = hT[:, bass.ds(2 * i + u // M, 1), :].rearrange("p o t -> p (o t)")
                    for k in range(2):
                        ins = nc.tensor.matmul(pg[0:cols[m], u % 2, k, :], w.shgu[:, k, m * P:m * P + cols[m]], rhs, start=True, stop=True)
                    ins.then_inc(g_ps, 1)

                def down(i, u):
                    n, m, h = turn(i, u), u % M, u // M
                    pe.wait_ge(hid_done, n + 1)
                    if m == 0:
                        after(pe, sh_out, 2 * i + h - 1)
                    for j in range(4):
                        ins = nc.tensor.matmul(pd[:, h, j * C:(j + 1) * C], hid[u % 2][0:cols[m], j * P:(j + 1) * P],
                                               w.shd[0:cols[m], m, :], start=m == 0 and j == 0, stop=m == M - 1, skip_group_check=True)
                    ins.then_inc(d_ps, 1)
                pe.wait_ge(both_done, 1)
                nc.tensor.matmul(pp[:, 0, 0:NE * NT], w.trib[:], both[:].rearrange("p e t -> p (e t)"), start=True, stop=True)
                nc.tensor.matmul(pp[:, 1, 0:NE * NT], w.onesb[:], both[:].rearrange("p e t -> p (e t)"), start=True, stop=True).then_inc(pre_ps, 1)
                transpose_weights(pe)
                if layer == 0:
                    staged(pe, NC, (0, up), (1, down), unroll=2 * M)

            @block.sync
            def _(sp):
                load_weights(sp)

            @block.gpsimd
            def _(pool):
                pool.wait_ge(slots_done, 1)
                weight = w.h[:, :, C + 1:C + 2].rearrange("p t o -> p (t o)")
                nc.gpsimd.tensor_copy(weight, w.wt[0][:]).then_inc(second, 1)
                pool.wait_ge(second, 1)
                for k in range(2):
                    if k == 1:
                        pool.wait_ge(scattered[0], 16 * NT)
                        index = w.h[:, :, C:C + 1].bitcast(U32)
                        nc.gpsimd.tensor_copy(weight, w.wt[1][:])
                        nc.gpsimd.iota(index, pattern=[[P, NT], [0, 1]], base=TOK, channel_multiplier=1).then_inc(second, 1)
                        pool.wait_ge(second, 2)
                    for t in range(NT):
                        nc.gpsimd.indirect_dma_start(out=d.xg[layer], out_offset=bass.IndirectOffsetOnAxis(ap=w.slot[k][:, t:t + 1], axis=0),
                                                     in_=w.h[:, t, :], in_offset=None).then_inc(scattered[k], 16)
                pool.wait_ge(scattered[1], 16 * NT)


def experts_phase(nc, w, d, layer):
    I = (176, 352)[layer]
    cols = chunks_of(I)
    M = len(cols)
    with ExitStack() as ctx:
        sb = lambda n, s, t=F32: ctx.enter_context(nc.sbuf_tensor(f"{n}_{layer}", s, t))
        ps = lambda n, s, t=F32: ctx.enter_context(nc.psum_tensor(f"{n}_{layer}", s, t))
        sem = lambda n: semaphore_of(nc, ctx, f"{n}_{layer}")
        xt = [sb(f"xt{u}", [P, XW]) for u in range(UN)]
        xT = [sb(f"xT{u}", [P, P]) for u in range(UN)]
        sg = [sb(f"esg{u}", [P, I]) for u in range(2)]
        hid = [sb(f"ehid{u}", [P, I]) for u in range(4)]
        hidT = [sb(f"ehidT{u}", [P, M, P]) for u in range(2)]
        yo = [sb(f"yo{u}", [P, C]) for u in range(UN)]
        pT = ps("epT", [P, ST])
        pg = ps("epg", [P, 2, 2, ST])
        ph = ps("eph", [P, 2, ST])
        pd = ps("epd", [P, ST])
        g_of = lambda u: pg[:, u, 0, 0:I]
        u_of = lambda u: pg[:, u, 1, 0:I]
        x_in = [sem(f"xin{u}") for u in range(UN)]
        y_out = w.y_out[layer]
        in_ps, in_T, up_ps, s_done, hid_done, hid_ps, hid_T, dn_ps, y_done = (
            sem("in_ps"), sem("in_T"), sem("up_ps"), sem("s_done"), sem("ehid_done"), sem("hid_ps"), sem("hid_T"), sem("dn_ps"), sem("y_done"))
        const = lambda n: isinstance(n, int)

        def rows_of(a, n):
            v = a.rearrange("(i p) c -> i p c", p=P)
            return v[n] if const(n) else v[bass.ds(n, 1)][0]

        def loop(eng, step):
            for u in range(UN):
                step(u, u)
            with eng.Fori(1, NSLOT // UN) as i:
                for u in range(UN):
                    step(UN * i + u, u)

        def skewed(eng, *stages, begin=lambda i: None, tick=lambda u: None):
            def step(n, u, at):
                tick(at)
                for k, f in stages:
                    if not (const(n) and not 0 <= n + k < NSLOT):
                        f(n + k, (u + k) % UN)
            begin(0)
            for n in range(UN):
                step(n, n, n)
            with eng.Fori(1, NSLOT // UN - 1) as i:
                begin(i)
                for u in range(UN):
                    step(UN * i + u, u, u)
            begin(NSLOT // UN - 1)
            for u in range(UN + LAG):
                step(NSLOT - UN + u, u % UN, u)

        with nc.Block() as block:
            @block.sync
            def _(sp):
                def step(n, u):
                    if not (const(n) and n < UN):
                        sp.wait_ge(y_out[u], (16 // UN) * (n - u))
                    sp.dma_start(xt[u][:], rows_of(d.xg[layer], n)).then_inc(x_in[u], 16)
                loop(sp, step)

            @block.gpsimd
            def _(pool):
                count = pool.alloc_register(f"y_count_{layer}")

                def step(n, u):
                    wait_before(pool, count, y_done, n + 1, in_ps)
                    nc.gpsimd.indirect_dma_start(out=d.yk, out_offset=bass.IndirectOffsetOnAxis(ap=xt[u][:, C:C + 1].bitcast(U32), axis=0),
                                                 in_=yo[u][:], in_offset=None).then_inc(y_out[u], 16)
                loop(pool, step)
                for u in range(UN):
                    pool.wait_ge(y_out[u], 16 * (NSLOT // UN))

            @block.scalar
            def _(act):
                def x_copy(n, u):
                    act.wait_ge(in_ps, n + 1)
                    nc.scalar.copy(xT[u][:], pT[:, 0:P]).then_inc(in_T, 1)

                def silu(n, u):
                    act.wait_ge(up_ps, n + 1)
                    nc.scalar.activation(sg[u % 2][:], g_of(u % 2), ACT.Silu).then_inc(s_done, 1)

                def y_copy(n, u):
                    act.wait_ge(dn_ps, n + 1)
                    if not (const(n) and n < UN):
                        act.wait_ge(y_out[u], (16 // UN) * (n - u))
                    nc.scalar.activation(yo[u][:], pd[:, 0:C], ACT.Copy, scale=xt[u][:, C + 1:C + 2]).then_inc(y_done, 1)

                x_copy(0, 0)
                x_copy(1, 1)
                silu(0, 0)
                skewed(act, (2, x_copy), (1, silu), (-LAG, y_copy))

            @block.vector
            def _(dve):
                def product(n, u):
                    dve.wait_ge(s_done, n + 1)
                    nc.vector.tensor_tensor(hid[u % 4][:], sg[u % 2][:], u_of(u % 2), ALU.mult).then_inc(hid_done, 1)

                def hid_copy(n, u):
                    dve.wait_ge(hid_ps, n + 1)
                    if I == 176:
                        ins = nc.vector.tensor_copy(hidT[u % 2][0:88, :, :], ph[0:88, u % 2, 0:M * P].rearrange("p (m c) -> p m c", m=M))
                    else:
                        nc.vector.tensor_copy(hidT[u % 2][:, 0:2, :], ph[:, u % 2, 0:2 * P].rearrange("p (m c) -> p m c", m=2))
                        ins = nc.vector.tensor_copy(hidT[u % 2][0:96, 2, :], ph[0:96, u % 2, 2 * P:3 * P])
                    ins.then_inc(hid_T, 1)

                product(0, 0)
                skewed(dve, (1, product), (-1, hid_copy))

            @block.tensor
            def _(pe):
                def t_in(n, u):
                    if const(n):
                        pe.wait_ge(x_in[u], 16 * (n // UN + 1))
                    else:
                        pe.wait_ge(x_in[u], (16 // UN) * (n - u) + 16)
                    after(pe, in_T, n)
                    nc.tensor.transpose(pT[:, 0:P], xt[u][:, 0:C], w.ident[:]).then_inc(in_ps, 1)

                def up(n, u):
                    e = expert(1)
                    pe.wait_ge(in_T, n + 1)
                    after(pe, hid_done, n - 1)
                    wt = w.up[:, bass.ds(e, 1)][:, 0]
                    for k in range(2):
                        rhs = wt[:, 0, k * I:(k + 1) * I] if layer == 0 else wt[:, k, :]
                        ins = nc.tensor.matmul((g_of, u_of)[k](u % 2), xT[u][:], rhs, start=True, stop=True)
                    ins.then_inc(up_ps, 1)
                    return e

                def t_hid(n, u):
                    pe.wait_ge(hid_done, n + 1)
                    after(pe, hid_T, n - 1)
                    c0 = 0
                    for m, cw in enumerate(cols):
                        ins = nc.tensor.transpose(ph[0:cw, u % 2, m * P:(m + 1) * P], hid[u % 4][:, c0:c0 + cw], w.ident[:])
                        c0 += cw
                    ins.then_inc(hid_ps, 1)

                def down(n, u):
                    e = expert(-LAG)
                    pe.wait_ge(hid_T, n + 1)
                    after(pe, y_done, n)
                    wt = w.down[:, bass.ds(e, 1)][:, 0]
                    for m, cw in enumerate(cols):
                        ins = nc.tensor.matmul(pd[:, 0:C], hidT[u % 2][0:cw, m, :], wt[0:cw, m, :], start=m == 0, stop=m == M - 1)
                    ins.then_inc(dn_ps, 1)

                place, words = [0], [None, None]

                def begin(i):
                    for k in range(2):
                        at = w.tile_expert[0:1, i + k:i + k + 1] if const(i) else w.tile_expert[0:1, bass.ds(i + k, 1)]
                        words[k] = pe.value_load(at, min_val=0, max_val=8 ** UN - 1)

                def tick(u):
                    place[0] = u

                def expert(k):
                    at = place[0] + LAG + k
                    return (words[at // UN] >> (3 * (at % UN))) & (NE - 1)
                t_in(0, 0)
                t_in(1, 1)
                begin(0)
                tick(-1)
                up(0, 0)
                skewed(pe, (2, t_in), (1, up), (-1, t_hid), (-LAG, down), begin=begin, tick=tick)


def combine_phase(nc, w, d, layer):
    with ExitStack() as ctx:
        sb = lambda n, s, t=F32: ctx.enter_context(nc.sbuf_tensor(f"{n}_{layer}", s, t))
        sem = lambda n: semaphore_of(nc, ctx, f"{n}_{layer}")
        gat = [[sb(f"gat{k}_{u}", [P, 4, C]) for u in range(4)] for k in range(2)]
        got = [sem(f"got{u}") for u in range(4)]
        c_step, x_done, stored = sem("c_step"), sem("x_done"), sem("stored")
        NSTEP = 4 if layer == 0 else 3
        with nc.Block() as block:
            @block.scalar
            def _(act):
                for s in range(2 * NB):
                    u = s % 4
                    if s >= 4:
                        act.wait_ge(x_done, s - 3)
                    for k in range(2):
                        at = k * TOK + s * ST
                        act.dma_start(gat[k][u][:], d.yk[at:at + ST, :].rearrange("(j p) c -> p j c", p=P)).then_inc(got[u], 16)

            @block.vector
            def _(dve):
                v = nc.vector
                for s in range(2 * NB):
                    u, b = s % 4, s // 2
                    dve.wait_ge(got[u], 16 * 2 * (s // 4 + 1))
                    link = Chain(dve, c_step, NSTEP * s)
                    a0, a1 = gat[0][u][:], gat[1][u][:]
                    link(v.tensor_tensor(a0, a0, a1, ALU.add))
                    if layer == 0:
                        link(v.tensor_tensor(a0, a0, w.sh[:, 4 * s:4 * s + 4, :], ALU.add))
                    link(v.tensor_tensor(a0, a0, w.gate[:, 2 * layer + 1, b:b + 1, :].to_broadcast([P, 4, C]), ALU.mult))
                    link(v.tensor_tensor(w.x[:, 4 * s:4 * s + 4, :], w.x[:, 4 * s:4 * s + 4, :], a0, ALU.add))
                    dve.sem_inc(x_done, 1)

            @block.sync
            def _(sp):
                if layer == 1:
                    xo = d.out.rearrange("b (n p) c -> p (b n) c", p=P)
                    for s in range(2 * NB):
                        sp.wait_ge(x_done, s + 1)
                        sp.dma_start(xo[:, 4 * s:4 * s + 4, :], w.x[:, 4 * s:4 * s + 4, :]).then_inc(stored, 16)
                    sp.wait_ge(stored, 16 * 2 * NB)


NSTATE = 32
CG = P // NSTATE
NG = C // CG
LW = P + 1
GI = 4
TWO_PI = 6.283185
ROUND = 12582912.0


def s4_phase(nc, w, d):
    with ExitStack() as whole:
        sbw = lambda n, s, t=F32: whole.enter_context(nc.sbuf_tensor(n, s, t))
        inT = sbw("inT", [P, C])
        gluT = sbw("gluT", [P, 2, C])
        outT = sbw("outT", [P, C])
        glub = sbw("glub", [P, 2])
        inb = sbw("inb", [P, C])
        outb = sbw("outb", [P, C])
        cols = sbw("cols", [P, 6, NG])
        powr = sbw("powr", [P, 2, NG, LW])
        s_all = sbw("s_all", [P, NG, 2, NB, TPB])
        h_all = sbw("h_all", [P, NG, 2, NB, TPB])
        h_c = sbw("h_c", [P, NG, 2, NT])
        cdiag = sbw("cdiag", [P, NG, 2, CG])
        k_lh = sbw("k_lh", [P, C])
        k_hl = sbw("k_hl", [P, P])
        dskip = sbw("dskip", [P, 1])
        R_, PH_, CR_, CI_, DR_, DI_ = range(6)
        u_all = w.v[:].rearrange("p a b c -> p (a b c)").rearrange("p (c t) -> p c t", t=NT)
        h_keep = w.sh
        s4_coefficients(nc, w, d, locals())
        s4_input(nc, w, d, locals())
        s4_states(nc, w, d, locals())
        y_all = sbw("y_all", [P, NT, C])
        s4_output(nc, w, d, locals())
        s4_gate(nc, w, d, locals())


def s4_coefficients(nc, w, d, m):
    inT, gluT, outT, glub, inb, outb, cols, powr, cdiag, dskip = (m[k] for k in (
        "inT", "gluT", "outT", "glub", "inb", "outb", "cols", "powr", "cdiag", "dskip"))
    R_, PH_, CR_, CI_, DR_, DI_ = range(6)
    with ExitStack() as ctx:
        sb = lambda n, s, t=F32: ctx.enter_context(nc.sbuf_tensor(n, s, t))
        ps = lambda n, s, t=F32: ctx.enter_context(nc.psum_tensor(n, s, t))
        sem = lambda n: semaphore_of(nc, ctx, n)
        wsrc = sb("wsrc", [P, 4, C])
        raw = sb("sraw", [P, 3, NSTATE])
        cc = sb("cc", [P, NSTATE, 2])
        ldt = sb("ldt", [P, 1])
        co = sb("co", [P, 6, NSTATE])
        ea = sb("ea", [P, NSTATE])
        tt = sb("tt", [P, 4, NSTATE])
        rn = sb("rn", [P, 4, NSTATE])
        ex = sb("ex", [P, 2, NSTATE])
        zz = sb("zz", [P, 4, NSTATE])
        q = sb("qtmp", [P, 4, NSTATE])
        den = sb("den", [P, NSTATE])
        rowsg = sb("rowsg", [NG, 6, P])
        rnd = sb("rnd", [P, NG, LW])
        mag = sb("smag", [P, NG, LW])
        pw = ps("pw", [P, ST])
        pc = ps("pc", [P, ST])
        s_in, w_tr, w_out, c_step, e_done, z_done, co_out, rows_in, cols_ps, m_done, sin_done = (sem(n) for n in (
            "s_in", "sw_tr", "sw_out", "c_step", "e_done", "z_done", "co_out", "rows_in", "cols_ps4", "m_done", "ssin_done"))
        p_step = sem("p_step")
        with nc.Block() as block:
            @block.sync
            def _(sp):
                srcs = [d.in_W, d.glu_W[0:C], d.glu_W[C:2 * C], d.out_W]
                for k, src in enumerate(srcs):
                    sp.dma_start(wsrc[:, k, :], src).then_inc(s_in, 16)
                sp.dma_start(raw[:, 0, :], d.log_A_real).then_inc(s_in, 16)
                sp.dma_start(raw[:, 1, :], d.A_imag).then_inc(s_in, 16)
                sp.dma_start(cc[:], d.C).then_inc(s_in, 16)
                col = lambda a: a.rearrange("(p o) -> p o", o=1)
                with nc.allow_non_contiguous_dma(reason="vectors as columns"):
                    sp.dma_start(ldt[:], col(d.log_dt)).then_inc(s_in, 16)
                    sp.dma_start(dskip[:], col(d.D_skip)).then_inc(s_in, 16)
                    for k in range(2):
                        sp.dma_start(glub[:, k:k + 1], col(d.glu_b[k * C:(k + 1) * C])).then_inc(s_in, 16)
                sp.dma_start(inb[:], d.in_b.rearrange("(o c) -> o c", o=1).to_broadcast([P, C])).then_inc(s_in, 16)
                sp.dma_start(outb[:], d.out_b.rearrange("(o c) -> o c", o=1).to_broadcast([P, C])).then_inc(s_in, 16)
                sp.wait_ge(z_done, 1)
                sp.dma_start(d.coef.rearrange("a (h n) -> h a n", n=NSTATE), co[:]).then_inc(co_out, 16)
                sp.wait_ge(co_out, 16)
                sp.dma_start(rowsg[:], d.coef.rearrange("a (g p) -> g a p", p=P)).then_inc(rows_in, 16)

            @block.tensor
            def _(pe):
                pe.wait_ge(s_in, 16 * 13)
                for k in range(4):
                    ins = nc.tensor.transpose(pw[:, k * C:(k + 1) * C], wsrc[:, k, :], w.ident[:])
                ins.then_inc(w_tr, 1)
                pe.wait_ge(rows_in, 16)
                for a in range(6):
                    ins = nc.tensor.transpose(pc[:, a * NG:(a + 1) * NG], rowsg[:, a, :], w.ident[0:NG, 0:NG])
                ins.then_inc(cols_ps, 1)

            @block.scalar
            def _(act):
                act.wait_ge(s_in, 16 * 13)
                nc.scalar.activation(ldt[:], ldt[:], ACT.Exp).then_inc(e_done, 1)
                nc.scalar.activation(ea[:], raw[:, 0, :], ACT.Exp).then_inc(e_done, 1)
                act.wait_ge(c_step, 1)
                nc.scalar.activation(ex[:, 0, :], co[:, R_, :], ACT.Exp)
                nc.scalar.activation(ex[:, 1, :], co[:, R_, :], ACT.Exp, scale=float(P)).then_inc(e_done, 1)
                act.wait_ge(c_step, 5)
                nc.scalar.activation(zz[:], tt[:], ACT.Sin, scale=TWO_PI).then_inc(e_done, 1)
                act.wait_ge(p_step, 1)
                nc.scalar.activation(mag[:], mag[:], ACT.Exp).then_inc(m_done, 1)
                for k in range(2):
                    act.wait_ge(p_step, 4 + 2 * k)
                    nc.scalar.activation(powr[:, 1 - k], powr[:, 1 - k], ACT.Sin, scale=TWO_PI).then_inc(sin_done, 1)

            @block.vector
            def _(dve):
                v = nc.vector
                link = Chain(dve, c_step)
                dve.wait_ge(e_done, 2)
                link(v.tensor_scalar(co[:, R_, :], ea[:], ldt[:], -1.0, ALU.mult, ALU.mult))
                link(v.tensor_scalar(co[:, PH_, :], raw[:, 1, :], ldt[:], 1.0 / (2.0 * np.pi), ALU.mult, ALU.mult))
                v.tensor_copy(tt[:, 0, :], co[:, PH_, :])
                v.tensor_scalar(tt[:, 1, :], co[:, PH_, :], 0.25, None, ALU.add)
                v.tensor_scalar(tt[:, 2, :], co[:, PH_, :], float(P), None, ALU.mult)
                link(v.tensor_scalar(tt[:, 3, :], co[:, PH_, :], float(P), 0.25, ALU.mult, ALU.add))
                link(v.tensor_scalar(rn[:], tt[:], ROUND, ROUND, ALU.add, ALU.subtract))
                link(v.tensor_tensor(tt[:], tt[:], rn[:], ALU.subtract))
                dve.wait_ge(e_done, 4)
                v.tensor_tensor(zz[:, 0:2, :], zz[:, 0:2, :], ex[:, 0:1, :].to_broadcast([P, 2, NSTATE]), ALU.mult)
                v.tensor_tensor(co[:, DI_, :], zz[:, 2, :], ex[:, 1, :], ALU.mult)
                v.tensor_tensor(co[:, DR_, :], zz[:, 3, :], ex[:, 1, :], ALU.mult)
                v.tensor_tensor(den[:], ea[:], ea[:], ALU.mult)
                link(v.tensor_tensor(q[:, 0, :], raw[:, 1, :], raw[:, 1, :], ALU.mult))
                link(v.tensor_tensor(den[:], den[:], q[:, 0, :], ALU.add))
                v.reciprocal(den[:], den[:])
                link(v.tensor_scalar(zz[:, 1, :], zz[:, 1, :], -1.0, None, ALU.add))

                def cmul(o_r, o_i, a_r, a_i, b_r, b_i):
                    v.tensor_tensor(q[:, 0, :], a_r, b_r, ALU.mult)
                    v.tensor_tensor(q[:, 1, :], a_i, b_i, ALU.mult)
                    v.tensor_tensor(q[:, 2, :], a_r, b_i, ALU.mult)
                    link(v.tensor_tensor(q[:, 3, :], a_i, b_r, ALU.mult))
                    v.tensor_tensor(o_r, q[:, 0, :], q[:, 1, :], ALU.subtract)
                    link(v.tensor_tensor(o_i, q[:, 2, :], q[:, 3, :], ALU.add))
                cmul(co[:, CR_, :], co[:, CI_, :], cc[:, :, 0], cc[:, :, 1], zz[:, 1, :], zz[:, 0, :])
                v.tensor_scalar(zz[:, 2, :], ea[:], -1.0, None, ALU.mult)
                link(v.tensor_scalar(zz[:, 3, :], raw[:, 1, :], -1.0, None, ALU.mult))
                cmul(zz[:, 0, :], zz[:, 1, :], co[:, CR_, :], co[:, CI_, :], zz[:, 2, :], zz[:, 3, :])
                link(v.tensor_scalar(den[:], den[:], 2.0, None, ALU.mult))
                v.tensor_tensor(co[:, CR_, :], zz[:, 0, :], den[:], ALU.mult)
                v.tensor_tensor(co[:, CI_, :], zz[:, 1, :], den[:], ALU.mult).then_inc(z_done, 1)
                dve.wait_ge(w_tr, 1)
                v.tensor_copy(inT[:], pw[:, 0:C])
                v.tensor_copy(gluT[:], pw[:, C:3 * C].rearrange("p (a c) -> p a c", a=2))
                v.tensor_copy(outT[:], pw[:, 3 * C:4 * C])
                dve.wait_ge(cols_ps, 1)
                link(v.tensor_copy(cols[:], pc[:, 0:6 * NG].rearrange("p (a g) -> p a g", a=6)))
                pl = Chain(dve, p_step)
                ib = w.iota[:, 0:LW].rearrange("p (o l) -> p o l", o=1).to_broadcast([P, NG, LW])
                cb = lambda a: cols[:, a, :].rearrange("p (g o) -> p g o", o=1).to_broadcast([P, NG, LW])
                pl(v.tensor_tensor(mag[:], ib, cb(R_), ALU.mult))
                pl(v.tensor_tensor(powr[:, 1], ib, cb(PH_), ALU.mult))
                v.tensor_scalar(powr[:, 0], powr[:, 1], 0.25, None, ALU.add)
                for k in range(2):
                    pl(v.tensor_scalar(rnd[:], powr[:, 1 - k], ROUND, ROUND, ALU.add, ALU.subtract))
                    pl(v.tensor_tensor(powr[:, 1 - k], powr[:, 1 - k], rnd[:], ALU.subtract))
                link(v.memset(cdiag[:], 0.0))
                for h in range(CG):
                    r = slice(h * NSTATE, (h + 1) * NSTATE)
                    v.tensor_copy(cdiag[r, :, 0, h], cols[r, CR_, :])
                    v.tensor_scalar(cdiag[r, :, 1, h], cols[r, CI_, :], -1.0, None, ALU.mult)
                dve.wait_ge(m_done, 1)
                for k in range(2):
                    dve.wait_ge(sin_done, k + 1)
                    v.tensor_tensor(powr[:, 1 - k], powr[:, 1 - k], mag[:], ALU.mult)


def s4_input(nc, w, d, m):
    inT, inb, u_all, h_keep = (m[k] for k in ("inT", "inb", "u_all", "h_keep"))
    with ExitStack() as ctx:
        sb = lambda n, s, t=F32: ctx.enter_context(nc.sbuf_tensor(n, s, t))
        ps = lambda n, s, t=F32: ctx.enter_context(nc.psum_tensor(n, s, t))
        sem = lambda n: semaphore_of(nc, ctx, n)
        hs = [sb(f"shs{u}", [P, 4, C]) for u in range(2)]
        hT = [sb(f"shT{u}", [P, ST]) for u in range(2)]
        pT = ps("spT", [P, 2, ST])
        pu = ps("spu", [P, 2, ST])
        i_step, h_done, h_kept, tr_done, hT_done, u_ps, u_out = (sem(n) for n in (
            "i_step", "sh_done", "sh_kept", "str_done", "shT_done", "u_ps", "u_out"))
        with nc.Block() as block:
            @block.vector
            def _(dve):
                def rows(b, u):
                    s = 2 * b + u
                    after(dve, tr_done, s - 1)
                    after(dve, h_kept, s - 1)
                    link = Chain(dve, i_step, 2 * s)
                    for j in range(4):
                        t = b * TPB + u * 4 + j
                        ins = nc.vector.tensor_scalar(hs[u][:, j, :], w.x[:, t, :], w.mean[:, bass.ds(t, 1)],
                                                      w.rstd[:, bass.ds(t, 1)], ALU.subtract, ALU.mult)
                    link(ins)
                    link(nc.vector.tensor_tensor(hs[u][:], hs[u][:], w.moda[:, 1, bass.ds(b, 1), :].to_broadcast([P, 4, C]), ALU.mult))
                    nc.vector.tensor_tensor(hs[u][:], hs[u][:], w.moda[:, 0, bass.ds(b, 1), :].to_broadcast([P, 4, C]), ALU.add).then_inc(h_done, 1)

                def project(b, u):
                    dve.wait_ge(u_ps, 2 * b + u + 1)
                    dst = u_all.rearrange("p c t -> p t c")[:, bass.ds(b * TPB + u * 4, 4), :]
                    nc.vector.tensor_tensor(dst, pu[:, u, :].rearrange("p (j c) -> p j c", j=4),
                                            inb[:].rearrange("p (o c) -> p o c", o=1).to_broadcast([P, 4, C]), ALU.add).then_inc(u_out, 1)
                staged(dve, 2 * NB, (0, rows), (1, project))

            @block.gpsimd
            def _(pool):
                def keep(b, u):
                    pool.wait_ge(h_done, 2 * b + u + 1)
                    nc.gpsimd.tensor_copy(h_keep[:, bass.ds(b * TPB + u * 4, 4), :], hs[u][:]).then_inc(h_kept, 1)
                staged(pool, 2 * NB, (0, keep))

            @block.scalar
            def _(act):
                def transposed(b, u):
                    s = 2 * b + u
                    act.wait_ge(tr_done, s + 1)
                    after(act, u_ps, s - 1)
                    nc.scalar.copy(hT[u][:], pT[:, u, :]).then_inc(hT_done, 1)
                staged(act, 2 * NB, (0, transposed))

            @block.tensor
            def _(pe):
                def transpose(b, u):
                    s = 2 * b + u
                    pe.wait_ge(h_done, s + 1)
                    after(pe, hT_done, s - 1)
                    for j in range(4):
                        ins = nc.tensor.matmul(pT[:, u, j * C:(j + 1) * C], hs[u][:, j, :], w.flip[:], start=True, stop=True)
                    ins.then_inc(tr_done, 1)

                def project(b, u):
                    s = 2 * b + u
                    pe.wait_ge(hT_done, s + 1)
                    after(pe, u_out, s - 1)
                    for j in range(4):
                        ins = nc.tensor.matmul(pu[:, u, j * C:(j + 1) * C], hT[u][:, j * C:(j + 1) * C], inT[:], start=True, stop=True)
                    ins.then_inc(u_ps, 1)
                staged(pe, 2 * NB, (1, project), (0, transpose))


def s4_states(nc, w, d, m):
    powr, s_all, h_all, h_c, cdiag, k_lh, k_hl, u_all, cols, dskip = (m[k] for k in (
        "powr", "s_all", "h_all", "h_c", "cdiag", "k_lh", "k_hl", "u_all", "cols", "dskip"))
    R_, PH_, CR_, CI_, DR_, DI_ = range(6)
    with ExitStack() as ctx:
        sb = lambda n, s, t=F32: ctx.enter_context(nc.sbuf_tensor(n, s, t))
        ps = lambda n, s, t=F32: ctx.enter_context(nc.psum_tensor(n, s, t))
        sem = lambda n: semaphore_of(nc, ctx, n)
        wr = [sb(f"wr{u}", [P, 2, GI, LW]) for u in range(2)]
        vr = [sb(f"vr{u}", [P, 2, GI, P]) for u in range(2)]
        zk = sb("zk", [P, P])
        q = sb("hq", [P, 2, NG, 2, NB])
        qc = sb("hqc", [P, 4, NG, NT])
        pv = ps("spv", [P, 4, ST])
        pS = ps("sps4", [P, 2, ST])
        pk = ps("spk", [P, ST])
        w_in = [sem(f"sw_in{u}") for u in range(2)]
        v_ps, v_out, s_ps, s_out, r_step, k_tr, k_done, k_stored, k_ps = (sem(n) for n in (
            "v_ps4", "v_out4", "s_ps4", "s_out4", "r_step4", "k_tr", "k_done", "k_stored", "k_ps"))
        NI = NG // GI
        with nc.Block() as block:
            @block.sync
            def _(sp):
                def powers(i, u):
                    n = 2 * i + u
                    after(sp, k_ps, n - 1)
                    sp.dma_start(wr[u][:], powr[:, :, bass.ds(n * GI, GI), :]).then_inc(w_in[u], 16)
                staged(sp, NI, (0, powers))
                sp.wait_ge(k_done, 1)
                sp.dma_start(d.kpad[:, 0:P], zk[:]).then_inc(k_stored, 16)
                sp.dma_start(d.kpad[:, P:2 * P], k_hl[:]).then_inc(k_stored, 16)
                sp.wait_ge(k_stored, 32)

            @block.scalar
            def _(act):
                def powers_out(i, u):
                    n = 2 * i + u
                    act.wait_ge(v_ps, n + 1)
                    after(act, s_ps, n - 1)
                    for a in range(2):
                        ins = nc.scalar.copy(vr[u][:, a], pv[:, 2 * u + a, :].rearrange("p (g l) -> p g l", g=GI))
                    ins.then_inc(v_out, 1)
                staged(act, NI, (0, powers_out))

            @block.tensor
            def _(pe):
                def transpose(i, u):
                    n = 2 * i + u
                    pe.wait_ge(w_in[u], 16 * i + 16)
                    after(pe, v_out, n - 1)
                    for a in range(2):
                        for g in range(GI):
                            ins = nc.tensor.transpose(pv[:, 2 * u + a, g * P:(g + 1) * P], wr[u][:, a, g, 0:P], w.ident[:])
                    ins.then_inc(v_ps, 1)

                def states(i, u):
                    n = 2 * i + u
                    after(pe, s_out, n)
                    for g in range(GI):
                        for a in range(2):
                            ins = nc.tensor.matmul(pk[:, g * CG:(g + 1) * CG], wr[u][:, a, g, 0:P],
                                                   cdiag[:, bass.ds(n * GI + g, 1), a, :].rearrange("p o c -> p (o c)"),
                                                   start=a == 0, stop=a == 1)
                    ins.then_inc(k_ps, 1)
                    pe.wait_ge(v_out, n + 1)
                    for a in range(2):
                        for g in range(GI):
                            ins = nc.tensor.matmul(pS[:, a, g * P:(g + 1) * P], vr[u][:, a, g, :],
                                                   u_all[:, bass.ds((n * GI + g) * CG, CG), :].rearrange("p c t -> p (c t)"),
                                                   start=True, stop=True)
                    ins.then_inc(s_ps, 1)
                staged(pe, NI, (0, transpose), (1, states))
                pe.wait_ge(s_out, NI)
                nc.tensor.transpose(pk[:, 0:P], k_lh[:], w.ident[:]).then_inc(k_tr, 1)

            @block.vector
            def _(dve):
                v = nc.vector
                def states_out(i, u):
                    n = 2 * i + u
                    dve.wait_ge(s_ps, n + 1)
                    v.tensor_copy(k_lh[:, bass.ds(n * GI * CG, GI * CG)], pk[:, 0:GI * CG])
                    for h in range(CG):
                        r = slice(h * NSTATE, (h + 1) * NSTATE)
                        src = pS[r, :, :].rearrange("p a (g c t) -> p a g c t", g=GI, c=CG)[:, :, :, h, :]
                        dst = s_all[:].rearrange("p g a b t -> p a g (b t)")[r, :, bass.ds(n * GI, GI), :]
                        ins = v.tensor_copy(dst, src)
                    ins.then_inc(s_out, 1)
                staged(dve, NI, (0, states_out))
                dve.wait_ge(k_tr, 1)
                link = Chain(dve, r_step)
                link(v.tensor_copy(k_hl[:], pk[:, 0:P]))
                v.memset(zk[:], 0.0)
                v.tensor_tensor(k_hl[:, 0:1], k_hl[:, 0:1], dskip[:], ALU.add).then_inc(k_done, 1)
                link(v.memset(h_all[:, :, :, :, 0], 0.0))
                for t in range(1, TPB):
                    hp = h_all[:, :, :, :, t - 1]
                    for k, a in enumerate((DR_, DI_)):
                        cb = cols[:, a, :].rearrange("p (g o) -> p g o", o=1).to_broadcast([P, NG, 2 * NB])
                        ins = v.tensor_tensor(q[:, k].rearrange("p g a b -> p g (a b)"), hp.rearrange("p g a b -> p g (a b)"), cb, ALU.mult)
                    link(ins)
                    link(v.tensor_tensor(q[:, 0], q[:, 0], s_all[:, :, :, :, t - 1], ALU.add))
                    v.tensor_tensor(h_all[:, :, 0, :, t], q[:, 0, :, 0, :], q[:, 1, :, 1, :], ALU.subtract)
                    link(v.tensor_tensor(h_all[:, :, 1, :, t], q[:, 0, :, 1, :], q[:, 1, :, 0, :], ALU.add))
                hr, hi = (h_all[:, :, a, :, :].rearrange("p g b t -> p g (b t)") for a in range(2))
                cb = lambda a: cols[:, a, :].rearrange("p (g o) -> p g o", o=1).to_broadcast([P, NG, NT])
                v.tensor_tensor(qc[:, 0], hr, cb(CR_), ALU.mult)
                v.tensor_tensor(qc[:, 1], hi, cb(CI_), ALU.mult)
                v.tensor_tensor(qc[:, 2], hr, cb(CI_), ALU.mult)
                link(v.tensor_tensor(qc[:, 3], hi, cb(CR_), ALU.mult))
                v.tensor_tensor(h_c[:, :, 0, :], qc[:, 0], qc[:, 1], ALU.subtract)
                v.scalar_tensor_tensor(out=h_c[:, :, 1, :], in0=qc[:, 2], scalar=-1.0, in1=qc[:, 3], op0=ALU.mult, op1=ALU.subtract)


def s4_output(nc, w, d, m):
    powr, h_c, u_all, y_all = (m[k] for k in ("powr", "h_c", "u_all", "y_all"))
    NI = NG // GI
    CI = GI * CG
    with ExitStack() as ctx:
        sb = lambda n, s, t=F32: ctx.enter_context(nc.sbuf_tensor(n, s, t))
        ps = lambda n, s, t=F32: ctx.enter_context(nc.psum_tensor(n, s, t))
        sem = lambda n: semaphore_of(nc, ctx, n)
        wr = [sb(f"ywr{u}", [P, 2, GI, LW]) for u in range(2)]
        tz = [sb(f"tz{u}", [P, CI, P]) for u in range(2)]
        hd = [sb(f"hd{u}", [P, GI, 2, CG, NT]) for u in range(2)]
        py = ps("py", [P, 2, ST])
        w_in = [sem(f"yw_in{u}") for u in range(2)]
        z_set, hd_done, y_ps, y_out = sem("z_set"), sem("hd_done"), sem("y_ps"), sem("y_out4")
        with nc.Block() as block:
            @block.sync
            def _(sp):
                def load(i, u):
                    n = 2 * i + u
                    after(sp, y_ps, n - 1)
                    sp.dma_start(wr[u][:], powr[:, :, bass.ds(n * GI, GI), :]).then_inc(w_in[u], 16)
                    src = bass.AP(d.kpad.tensor, n * (CI * 2 * P) + 1, [[1, P], [2 * P, CI], [1, P]])
                    sp.dma_start(tz[u][:], src).then_inc(w_in[u], 16)
                staged(sp, NI, (0, load))

            @block.vector
            def _(dve):
                for u in range(2):
                    ins = nc.vector.memset(hd[u][:], 0.0)
                ins.then_inc(z_set, 1)
                dve.wait_ge(z_set, 1)
                def states(i, u):
                    n = 2 * i + u
                    after(dve, y_ps, n - 1)
                    for h in range(CG):
                        r = slice(h * NSTATE, (h + 1) * NSTATE)
                        ins = nc.vector.tensor_copy(hd[u][r, :, :, h, :], h_c[r, bass.ds(n * GI, GI), :, :])
                    ins.then_inc(hd_done, 1)
                staged(dve, NI, (0, states))

            @block.tensor
            def _(pe):
                def convolve(i, u):
                    n = 2 * i + u
                    pe.wait_ge(w_in[u], 32 * i + 32)
                    pe.wait_ge(hd_done, n + 1)
                    after(pe, y_out, n - 1)
                    for g in range(GI):
                        for a in range(2):
                            nc.tensor.matmul(py[:, u, g * P:(g + 1) * P], wr[u][:, a, g, 1:LW],
                                             hd[u][:, g, a].rearrange("p c t -> p (c t)"), start=a == 0, stop=False, skip_group_check=True)
                        for c in range(CG):
                            ch = g * CG + c
                            ins = nc.tensor.matmul(py[:, u, ch * NT:(ch + 1) * NT], tz[u][:, ch, :],
                                                   u_all[:, bass.ds(n * CI + ch, 1), :].rearrange("p o t -> p (o t)"),
                                                   start=False, stop=c == CG - 1, skip_group_check=True)
                    ins.then_inc(y_ps, 1)
                staged(pe, NI, (0, convolve))

            @block.scalar
            def _(act):
                count = act.alloc_register("gelu_count")
                def gelu(i, u):
                    n = 2 * i + u
                    wait_before(act, count, y_ps, n + 1, hd_done)
                    dst = y_all[:].rearrange("p t c -> p c t")[:, bass.ds(n * CI, CI), :]
                    nc.scalar.activation(dst, py[:, u, :].rearrange("p (c t) -> p c t", c=CI), ACT.Gelu).then_inc(y_out, 1)
                staged(act, NI, (0, gelu))


def s4_gate(nc, w, d, m):
    gluT, glub, outT, outb, y_all, h_keep = (m[k] for k in ("gluT", "glub", "outT", "outb", "y_all", "h_keep"))
    with ExitStack() as ctx:
        sb = lambda n, s, t=F32: ctx.enter_context(nc.sbuf_tensor(n, s, t))
        ps = lambda n, s, t=F32: ctx.enter_context(nc.psum_tensor(n, s, t))
        sem = lambda n: semaphore_of(nc, ctx, n)
        ys = [sb(f"gys{u}", [P, 4, C]) for u in range(2)]
        yT = [sb(f"gyT{u}", [P, ST]) for u in range(2)]
        sig = [sb(f"gsig{u}", [P, ST]) for u in range(2)]
        y2 = [sb(f"gy2{u}", [P, ST]) for u in range(2)]
        o = [sb(f"go{u}", [P, 4, C]) for u in range(2)]
        pT = ps("gpT", [P, 2, ST])
        pz = ps("gpz", [P, 4, ST])
        po = ps("gpo", [P, ST])
        y_in, y_tr, y_T, z_ps, sg_done, y2_done, o_ps, o_step, x_done = (sem("g" + n) for n in (
            "y_in", "y_tr", "y_T", "z_ps", "sg_done", "y2_done", "o_ps", "o_step", "x_done"))
        with nc.Block() as block:
            @block.gpsimd
            def _(pool):
                def rows(b, u):
                    after(pool, y_tr, 2 * b + u - 1)
                    nc.gpsimd.tensor_copy(ys[u][:], y_all[:, bass.ds(b * TPB + u * 4, 4), :]).then_inc(y_in, 1)
                staged(pool, 2 * NB, (0, rows))

            @block.tensor
            def _(pe):
                def transpose(b, u):
                    s = 2 * b + u
                    pe.wait_ge(y_in, s + 1)
                    after(pe, y_T, s - 1)
                    for j in range(4):
                        ins = nc.tensor.transpose(pT[:, u, j * C:(j + 1) * C], ys[u][:, j, :], w.ident[:])
                    ins.then_inc(y_tr, 1)

                def gates(b, u):
                    s = 2 * b + u
                    pe.wait_ge(y_T, s + 1)
                    after(pe, y2_done, s - 1)
                    for k in range(2):
                        ins = nc.tensor.matmul(pz[:, 2 * u + k, :], gluT[:, k, :], yT[u][:], start=True, stop=True)
                    ins.then_inc(z_ps, 1)

                def project(b, u):
                    s = 2 * b + u
                    pe.wait_ge(y2_done, s + 1)
                    after(pe, o_step, 3 * s)
                    for j in range(4):
                        ins = nc.tensor.matmul(po[:, j * C:(j + 1) * C], y2[u][:, j * C:(j + 1) * C], outT[:], start=True, stop=True)
                    ins.then_inc(o_ps, 1)
                staged(pe, 2 * NB, (0, transpose), (1, gates), (2, project))

            @block.scalar
            def _(act):
                def sigmoid(b, u):
                    s = 2 * b + u
                    act.wait_ge(z_ps, s + 1)
                    after(act, y2_done, s - 1)
                    nc.scalar.activation(sig[u][:], pz[:, 2 * u + 1, :], ACT.Sigmoid, bias=glub[:, 1:2]).then_inc(sg_done, 1)
                staged(act, 2 * NB, (0, sigmoid))

            @block.vector
            def _(dve):
                v = nc.vector

                def transposed(b, u):
                    s = 2 * b + u
                    dve.wait_ge(y_tr, s + 1)
                    after(dve, z_ps, s - 1)
                    v.tensor_copy(yT[u][:], pT[:, u, :]).then_inc(y_T, 1)

                def gated(b, u):
                    s = 2 * b + u
                    dve.wait_ge(sg_done, s + 1)
                    after(dve, o_ps, s - 1)
                    v.scalar_tensor_tensor(out=y2[u][:], in0=pz[:, 2 * u, :], scalar=glub[:, 0:1], in1=sig[u][:],
                                           op0=ALU.add, op1=ALU.mult).then_inc(y2_done, 1)

                def residual(b, u):
                    s = 2 * b + u
                    dve.wait_ge(o_ps, s + 1)
                    link = Chain(dve, o_step, 3 * s)
                    link(v.tensor_tensor(o[u][:], po[:].rearrange("p (j c) -> p j c", j=4),
                                         outb[:].rearrange("p (o c) -> p o c", o=1).to_broadcast([P, 4, C]), ALU.add))
                    link(v.tensor_tensor(o[u][:], o[u][:], h_keep[:, bass.ds(b * TPB + u * 4, 4), :], ALU.add))
                    link(v.tensor_tensor(o[u][:], o[u][:], w.gate[:, 2, bass.ds(b, 1), :].to_broadcast([P, 4, C]), ALU.mult))
                    xs = w.x[:, bass.ds(b * TPB + u * 4, 4), :]
                    v.tensor_tensor(xs, xs, o[u][:], ALU.add).then_inc(x_done, 1)
                staged(dve, 2 * NB, (0, transposed), (1, gated), (2, residual))


def program(nc, d):
    d.qk = nc.dram_tensor("qk", [2, NB, 3, C, T], BF16, kind="Internal").ap()
    d.xg = [nc.dram_tensor(f"xg{layer}", [NSLOT * P, XW], F32, kind="Internal").ap() for layer in range(2)]
    d.yk = nc.dram_tensor("yk", [2 * TOK + NSLOT * P, C], F32, kind="Internal").ap()
    d.coef = nc.dram_tensor("coef", [6, C * NSTATE], F32, kind="Internal").ap()
    d.kpad = nc.dram_tensor("kpad", [C, 2 * P], F32, kind="Internal").ap()

    w = Work()
    with ExitStack() as ctx:
        sb = lambda n, shape, t=F32: ctx.enter_context(nc.sbuf_tensor(n, shape, t))
        w.x = sb("x", [P, NT, C])
        w.y = sb("y", [P, NQUAD, TPB, 32])
        w.v = sb("v", [P, NQUAD, TPB, 32])
        w.ident, w.flip = sb("ident", [P, P]), sb("flip", [P, P])
        w.identb, w.trib, w.onesb = (sb(n, [P, P], BF16) for n in ("identb", "trib", "onesb"))
        w.iota, w.octal = sb("iota", [P, P + 1]), sb("octal", [P, UN])
        w.bnst = sb("bnst", [P, NT, 6])
        w.mean, w.rstd, w.t0, w.t1 = (sb(n, [P, NT]) for n in ("mean", "rstd", "t0", "t1"))
        w.mod = sb("mod", [P, 2, 6, NB])
        w.gate, w.modr = sb("gate", [P, 4, NB, C]), sb("modr", [P, 4, NB, C])
        w.moda = sb("moda", [P, 2, NB, C])
        w.wo, w.bo = sb("wo", [P, C]), sb("bo", [P, C])
        w.maskb = sb("maskb", [P, P], BF16)
        w.scattered = [[ctx.enter_context(nc.semaphore(f"scattered{k}_{layer}")) for k in range(2)] for layer in range(2)]
        w.y_out = [[ctx.enter_context(nc.semaphore(f"tile_out{u}_{layer}")) for u in range(UN)] for layer in range(2)]
        w.sh = w.y[:].rearrange("p a b c -> p (a b c)").rearrange("p (t c) -> p t c", c=C)
        with ExitStack() as first:
            sf = lambda n, shape, t=F32: first.enter_context(nc.sbuf_tensor(n, shape, t))
            w.wqkv, w.wqk = sf("wqkv", [P, 3 * C]), sf("wqk", [P, 4, C])
            w.bqk, w.bv = sf("bqk", [P, 4]), sf("bv", [P, C])
            w.rope = sf("rope", [P, 2, T])
            w.empty, w.empty_out = sf("empty", [P, NSLOT, XW]), semaphore_of(nc, first, "empty_out")
            setup_phase(nc, w, d)
            qkv_phase(nc, w, d)
        attention_phase(nc, w, d)
        project_phase(nc, w, d)
        w.wt, w.slot = [sb(f"wt{k}", [P, NT]) for k in range(2)], [sb(f"slot{k}", [P, NT], U32) for k in range(2)]
        w.shw = sb("shw", [P, NT])
        w.tile_expert = sb("tile_expert", [P, NSLOT // UN + 1], mybir.dt.int32)
        for layer in range(2):
            if layer == 1:
                stats_phase(nc, w, "c")
                s4_phase(nc, w, d)
            with ExitStack() as own:
                so = lambda n, shape: own.enter_context(nc.sbuf_tensor(f"{n}{layer}", shape, F32))
                w.up = so("up", [P, NE, layer + 1, 352])
                w.down = so("down", [P, NE, (2, 3)[layer], C])
                w.h = so("h", [P, NT, XW])
                w.rt = so("rt", [P, (NE + 1, NE)[layer]])
                if layer == 0:
                    w.shgu, w.shd = so("shgu", [P, 2, SI]), so("shd", [P, 3, C])
                stats_phase(nc, w, "bd"[layer], d, layer)
                route_phase(nc, w, d, layer)
                experts_phase(nc, w, d, layer)
                combine_phase(nc, w, d, layer)


_INPUTS = {
    "x": "L0_attn_x", "w_attn": "L0_attn_W_attn", "b_attn": "L0_attn_b_attn", "w_proj": "L0_attn_W_proj", "b_proj": "L0_attn_b_proj",
    "gate_w": "L0_ffn_gate_w", "gu0": "L0_ffn_experts_gate_up", "dn0": "L0_ffn_experts_down", "sg": "L0_ffn_shared_gate_w",
    "su": "L0_ffn_shared_up_w", "sd": "L0_ffn_shared_down_w", "seg": "L0_ffn_shared_expert_gate_w", "c0": "L0_c", "wmod0": "L0_wmod",
    "in_W": "L1_attn_in_W", "in_b": "L1_attn_in_b", "log_dt": "L1_attn_log_dt", "C": "L1_attn_C", "log_A_real": "L1_attn_log_A_real",
    "A_imag": "L1_attn_A_imag", "D_skip": "L1_attn_D_skip", "glu_W": "L1_attn_glu_W", "glu_b": "L1_attn_glu_b",
    "out_W": "L1_attn_out_W", "out_b": "L1_attn_out_b", "wg": "L1_ffn_Wg", "w1": "L1_ffn_W1", "w2": "L1_ffn_W2", "w3": "L1_ffn_W3",
    "c1": "L1_c", "wmod1": "L1_wmod",
}


def _constants():
    bf16 = mybir.dt.np(BF16)
    at = np.arange(P)
    pos = np.arange(T, dtype=np.float32)
    timescale = np.float32(1250) ** (2.0 * np.arange(HD // 2, dtype=np.float32) / HD)
    angle = (pos[None, :] / timescale[:, None]).astype(np.float32)[at // HQ % (HD // 2)]
    return {
        "rope": np.stack([np.cos(angle), np.sin(angle)], 1).astype(np.float32),
        "ident": np.eye(P, dtype=np.float32),
        "flip": np.ascontiguousarray(np.eye(P, dtype=np.float32)[::-1]),
        "identb": np.eye(P).astype(bf16),
        "maskb": np.where(at[None, :] > at[:, None], NEG, 0).astype(bf16),
        "trib": (at[:, None] < at[None, :]).astype(bf16),
        "onesb": np.ones((P, P), bf16),
        "octal": np.tile(8.0 ** np.arange(UN, dtype=np.float32), (P, 1)).astype(np.float32),
        "iota": np.tile(np.arange(P + 1, dtype=np.float32), (P, 1)),
    }


def kernel(**inputs):
    from types import SimpleNamespace

    import concourse.bacc as bacc
    from concourse.bass_utils import run_bass_kernel_spmd

    nc = bacc.Bacc("TRN2", target_bir_lowering=False, num_devices=1)

    arrays, aps = {}, {}
    given = {short: inputs[name] for short, name in _INPUTS.items()}
    for short, a in {**given, **_constants()}.items():
        a = np.ascontiguousarray(a)
        arrays[f"in_{short}"] = a
        aps[short] = nc.dram_tensor(f"in_{short}", a.shape, mybir.dt.from_np(a.dtype), kind="ExternalInput").ap()
    d = SimpleNamespace(**aps)
    d.c, d.wmod = [d.c0, d.c1], [d.wmod0, d.wmod1]
    d.out = nc.dram_tensor("out", [NB, T, C], F32, kind="ExternalOutput").ap()
    program(nc, d)
    r = run_bass_kernel_spmd(nc, [arrays], core_ids=[0])
    return r.results[0]["out"]
```

```python
from contextlib import ExitStack

import numpy as np

import concourse.bass as bass
from concourse import mybir

F32 = mybir.dt.float32
BF16 = mybir.dt.bfloat16
U32 = mybir.dt.uint32
ALU = mybir.AluOpType
ACT = mybir.ActivationFunctionType
AX = mybir.AxisListType

P = 128
NB, T, C = 4, 1024, 128
TOK = NB * T
NT = TOK // P
TPB = T // P
ST = 512
NH, HD = 16, 8
HQ = 4
NQ = NH // HQ
NQUAD = NB * NQ
TERMS = 6
KR = TERMS * HD
MROW = 64
EPS = 1e-5
NEG = -1e30
TWO_BF16_ONES = float(np.array([0x3F803F80], np.uint32).view(np.float32)[0])



def wait_before(eng, reg, sem, value, met):
    if isinstance(value, int):
        eng.wait_ge(sem, value)
        return
    eng.reg_mov(reg, value)
    eng.wait_ge(met, 1)
    eng.wait_ge(sem, reg)


def semaphore_of(nc, phase, name):
    s = phase.enter_context(nc.semaphore(name))
    phase.callback(nc.sync.sem_clear, s)
    return s


def after(eng, sem, n):
    if not (isinstance(n, int) and n <= 0):
        eng.wait_ge(sem, n)


def staged(eng, count, *stages, unroll=2):
    deep = max(delay for delay, f in stages)
    first = 1 + deep // unroll

    def tick(i, u):
        for delay, f in stages:
            j, v = i + (u - delay) // unroll, (u - delay) % unroll
            if not (isinstance(j, int) and not 0 <= unroll * j + v < count):
                f(j, v)
    for t in range(unroll * first):
        tick(t // unroll, t % unroll)
    with eng.Fori(first, count // unroll) as i:
        for u in range(unroll):
            tick(i, u)
    for t in range(count, count + deep):
        tick(t // unroll, t % unroll)


class Work:
    pass


class Chain:

    def __init__(self, eng, sem, base=0):
        self.eng, self.sem, self.base, self.n = eng, sem, base, 0

    def __call__(self, ins):
        self.n += 1
        ins.then_inc(self.sem, 1)
        self.eng.wait_ge(self.sem, self.base + self.n)


def layernorm_stats(nc, eng, link, x, w):
    st = w.bnst
    v = nc.vector
    for u in range(NT):
        ins = v.bn_stats(st[:, u, :], x[:, u, :])
    link(ins)
    link(v.tensor_tensor(w.mean[:], st[:, :, 1], st[:, :, 4], ALU.add))
    link(v.tensor_tensor(w.t0[:], st[:, :, 1], st[:, :, 4], ALU.subtract))
    link(v.tensor_tensor(w.t1[:], st[:, :, 2], st[:, :, 5], ALU.add))
    link(v.tensor_tensor(w.t0[:], w.t0[:], w.t0[:], ALU.mult))
    link(v.tensor_scalar(w.t1[:], w.t1[:], 1.0 / C, EPS, ALU.mult, ALU.add))
    link(v.tensor_scalar(w.mean[:], w.mean[:], 0.5, None, ALU.mult))
    return v.scalar_tensor_tensor(out=w.t1[:], in0=w.t0[:], scalar=0.25, in1=w.t1[:], op0=ALU.mult, op1=ALU.add)


def setup_phase(nc, w, d, m):
    with ExitStack() as ctx:
        sb = lambda n, s, t=F32: ctx.enter_context(nc.sbuf_tensor(n, s, t))
        ps = lambda n, s, t=F32: ctx.enter_context(nc.psum_tensor(n, s, t))
        sem = lambda n: semaphore_of(nc, ctx, n)
        root_done, st_step = sem("root_done"), sem("st_step")
        csT = sb("csT", [P, 2, NB])
        csS = sb("csS", [P, 2, NB])
        csB = sb("csB", [P, 2 * NB, P])
        wm = sb("wm", [P, 2, 6 * C])
        sgn = sb("sgn", [P, 4 * NB * C])
        mag = sb("mag", [P, 4 * NB * C])
        mps = ps("mps", [P, 2, 6, NB])
        gps = ps("gps", [P, 4, 4, C])
        c_in, x_in, attn_in, cst_in = sem("c_in"), sem("x_in"), sem("attn_in"), sem("cst_in")
        silu_done, cols_done, cols_ps, gate_ps = sem("silu_done"), sem("cols_done"), sem("cols_ps"), sem("gate_ps")
        vst, gate_out, zero_set = sem("vst"), sem("gate_out"), sem("zero_set")
        brow, bperm = sb("brow", [2, C]), sb("bperm", [2, 2, C])
        pb = ps("pb", [P, 4])
        perm_done, bias_ps = sem("perm_done"), sem("bias_ps")
        s4_loads, s4_transposes, s4_exponentials, s4_coefficients, s4_results = s4_coefficient_parts(nc, d, m, ctx)
        with nc.Block() as block:
            @block.sync
            def _(sp):
                for l in range(2):
                    with nc.allow_non_contiguous_dma(reason="4 conditioning rows as columns"):
                        sp.dma_start(csT[:, l, :], d.c[l].rearrange("b f -> f b")).then_inc(c_in, 16)
                    sp.dma_start(wm[:, l, :], d.wmod[l]).then_inc(c_in, 16)
                sp.dma_start(w.x[:], d.x.rearrange("b (n p) c -> p (b n) c", p=P)).then_inc(x_in, 16)
                sp.dma_start(w.wqkv[:], d.w_attn).then_inc(attn_in, 16)
                sp.dma_start(brow[:], d.b_attn[0:2 * C].rearrange("(j c) -> j c", j=2)).then_inc(attn_in, 16)
                sp.dma_start(w.ident[:], d.ident).then_inc(attn_in, 16)
                sp.dma_start(w.bv[:], d.b_attn[2 * C:].rearrange("(o c) -> o c", o=1).to_broadcast([P, C])).then_inc(cst_in, 16)
                sp.dma_start(w.bo[:], d.b_proj.rearrange("(o c) -> o c", o=1).to_broadcast([P, C])).then_inc(cst_in, 16)
                sp.dma_start(w.wo[:], d.w_proj).then_inc(cst_in, 16)
                sp.dma_start(w.rope[:], d.rope).then_inc(cst_in, 16)
                sp.dma_start(w.identb[:], d.identb).then_inc(cst_in, 16)
                sp.dma_start(w.maskb[:], d.maskb).then_inc(cst_in, 16)
                for src, dst in ((d.trib, w.trib), (d.onesb, w.onesb), (d.iota, w.iota), (d.flip, w.flip), (d.octal, w.octal)):
                    sp.dma_start(dst[:], src).then_inc(cst_in, 16)
                s4_loads(sp)
                sp.wait_ge(zero_set, 2)
                for layer in range(2):
                    sp.dma_start(d.xg[layer].rearrange("(p n) c -> p n c", p=P), w.empty[:]).then_inc(w.empty_out, 16)
                sp.wait_ge(cst_in, 16 * 11)

            @block.gpsimd
            def _(pool):
                pool.memset(w.empty[:], 0.0).then_inc(zero_set, 1)
                pool.wait_ge(zero_set, 1)
                pool.iota(w.empty[:, :, C:C + 1].bitcast(U32), pattern=[[1, NSLOT], [0, 1]], base=2 * TOK,
                          channel_multiplier=NSLOT).then_inc(zero_set, 1)

            @block.scalar
            def _(act):
                act.wait_ge(c_in, 64)
                nc.scalar.activation(csS[:], csT[:], ACT.Silu).then_inc(silu_done, 1)
                act.wait_ge(st_step, 8)
                nc.scalar.activation(w.t1[:], w.t1[:], ACT.Sqrt).then_inc(root_done, 1)
                s4_exponentials(act)

            @block.vector
            def _(dve):
                link = Chain(dve, vst)
                dve.wait_ge(silu_done, 1)
                for l in range(2):
                    for b in range(NB):
                        ins = nc.vector.tensor_copy(csB[:, l * NB + b, :], csS[:, l, b:b + 1].to_broadcast([P, P]))
                ins.then_inc(cols_done, 1)
                dve.wait_ge(x_in, 16)
                stats_link = Chain(dve, st_step)
                stats_link(layernorm_stats(nc, dve, stats_link, w.x, w))
                dve.wait_ge(root_done, 1)
                nc.vector.reciprocal(w.rstd[:], w.t1[:])
                dve.wait_ge(attn_in, 16 * 3)
                for src, plain, rot in ((w.wqkv[:, 0:C], w.wqk[:, 0], w.wqk[:, 2]), (w.wqkv[:, C:2 * C], w.wqk[:, 1], w.wqk[:, 3]),
                                        (brow[:], bperm[:, 0], bperm[:, 1])):
                    by_head = src.rearrange("p (q h e) -> p q h e", q=NQ, e=HD)
                    plain, rot = (x.rearrange("p (q e h) -> p q h e", q=NQ, e=HD) for x in (plain, rot))
                    nc.vector.tensor_copy(plain, by_head)
                    nc.vector.tensor_scalar(rot[:, :, :, 0:4], by_head[:, :, :, 4:8], -1.0, None, ALU.mult)
                    ins = nc.vector.tensor_copy(rot[:, :, :, 4:8], by_head[:, :, :, 0:4])
                ins.then_inc(perm_done, 1)
                dve.wait_ge(cols_ps, 1)
                link(nc.vector.tensor_copy(w.mod[:], mps[:]))
                for j in (1, 4):
                    ins = nc.vector.tensor_scalar(w.mod[:, :, j, :], w.mod[:, :, j, :], 1.0, None, ALU.add)
                link(ins)
                gb = w.gate[:].rearrange("p a b c -> p (a b c)")
                dve.wait_ge(gate_ps, 1)
                nc.vector.tensor_copy(gb, gps[:].rearrange("p a b c -> p (a b c)")).then_inc(gate_out, 1)
                dve.wait_ge(gate_out, 1)
                link(nc.vector.tensor_scalar(sgn[:], gb, 0.0, 2.0, ALU.is_ge, ALU.mult))
                link(nc.vector.tensor_scalar(mag[:], gb, -1.0, None, ALU.mult))
                dve.wait_ge(gate_ps, 2)
                for l in range(2):
                    nc.vector.tensor_copy(w.modr[:, 2 * l], gps[:, 2 * l])
                    ins = nc.vector.tensor_scalar(w.modr[:, 2 * l + 1], gps[:, 2 * l + 1], 1.0, None, ALU.add)
                ins.then_inc(gate_out, 1)
                link(nc.vector.tensor_tensor(mag[:], mag[:], gb, ALU.max))
                link(nc.vector.tensor_scalar(mag[:], mag[:], 0.25, None, ALU.max))
                link(nc.vector.scalar_tensor_tensor(out=gb, in0=sgn[:], scalar=-1.0, in1=mag[:], op0=ALU.add, op1=ALU.mult))
                s4_coefficients(dve)
                dve.wait_ge(bias_ps, 1)
                nc.vector.tensor_copy(w.bqk[:], pb[:])
                s4_results(dve)
                dve.wait_ge(gate_ps, 3)
                nc.vector.tensor_copy(w.moda[:, 0], gps[:, 2])
                nc.vector.tensor_scalar(w.moda[:, 1], gps[:, 3], 1.0, None, ALU.add)

            @block.tensor
            def _(pe):
                pe.wait_ge(silu_done, 1)
                for l in range(2):
                    for j in range(6):
                        ins = nc.tensor.matmul(mps[:, l, j, :], wm[:, l, j * C:(j + 1) * C], csS[:, l, :], start=True, stop=True)
                ins.then_inc(cols_ps, 1)
                pe.wait_ge(cols_done, 1)
                for rnd, comps in enumerate(((2, 5), (3, 4), (0, 1))):
                    pe.wait_ge(gate_out, rnd)
                    for l in range(2):
                        for a, j in enumerate(comps):
                            for b in range(NB):
                                ins = nc.tensor.matmul(gps[:, 2 * l + a, b, :], csB[:, l * NB + b, :], wm[:, l, j * C:(j + 1) * C],
                                                       start=True, stop=True)
                    ins.then_inc(gate_ps, 1)
                pe.wait_ge(perm_done, 1)
                for a in range(2):
                    ins = nc.tensor.transpose(pb[:, 2 * a:2 * a + 2], bperm[:, a, :], w.ident[0:2, 0:2])
                ins.then_inc(bias_ps, 1)
                s4_transposes(pe)


def qkv_phase(nc, w, d):
    with ExitStack() as ctx:
        sb = lambda n, s, t=F32: ctx.enter_context(nc.sbuf_tensor(n, s, t))
        ps = lambda n, s, t=F32: ctx.enter_context(nc.psum_tensor(n, s, t))
        sem = lambda n: semaphore_of(nc, ctx, n)
        xn = [sb(f"xn{u}", [P, 4, C]) for u in range(2)]
        hT = [sb(f"hTq{u}", [P, ST]) for u in range(2)]
        raw = [sb(f"raw{u}", [P, 4, ST]) for u in range(2)]
        res = [sb(f"res{u}", [P, 2, ST]) for u in range(2)]
        term = [[sb(f"term{u}_{n}", [P, 2, ST], BF16) for n in range(3)] for u in range(2)]
        pT = ps("pT", [P, 2, ST])
        pq = ps("pq", [P, 4, ST])
        pv = ps("pv", [P, 2, ST])
        norm_done, tr_done, h_done, qk_ps, v_ps = sem("norm_done"), sem("tr_done"), sem("h_done"), sem("qk_ps"), sem("v_ps")
        qk_out, v_out, sin_done = sem("qk_out"), sem("v_out"), sem("sin_done")
        cos_done, rope_done, hi_done, r1_done, mid_done, lo_done = (sem("cos_done"), sem("rope_done"), sem("hi_done"),
                                                                   sem("r1_done"), sem("mid_done"), sem("lo_done"))
        zeroed = sem("operands_zeroed")
        stored = [sem(f"stored{u}") for u in range(2)]
        NS = 2 * NB
        with nc.Block() as block:
            @block.vector
            def _(dve):
                def norm(b, u):
                    s = 2 * b + u
                    after(dve, tr_done, s - 1)
                    for j in range(4):
                        t = b * TPB + u * 4 + j
                        ins = nc.vector.tensor_scalar(xn[u][:, j, :], w.x[:, t, :], w.mean[:, bass.ds(t, 1)],
                                                      w.rstd[:, bass.ds(t, 1)], ALU.subtract, ALU.mult)
                    ins.then_inc(norm_done, 1)

                def cos(b, u):
                    dve.wait_ge(qk_out, 4 * (2 * b + u) + 2)
                    cosb = w.rope[:, 0:1, u * ST:(u + 1) * ST].to_broadcast([P, 2, ST])
                    nc.vector.tensor_tensor(raw[u][:, 0:2, :], raw[u][:, 0:2, :], cosb, ALU.mult).then_inc(cos_done, 1)

                def value(b, u):
                    dve.wait_ge(v_ps, 2 * b + u + 1)
                    vt = w.v[:].rearrange("p (b q) k c -> p b k q c", q=NQ)[:, bass.ds(b, 1), u * 4:u * 4 + 4, :, :]
                    for j in range(4):
                        ins = nc.vector.tensor_tensor(vt[:, 0, j], pv[:, u, j * C:(j + 1) * C].rearrange("p (q c) -> p q c", q=NQ),
                                                      w.bv[:].rearrange("p (q c) -> p q c", q=NQ), ALU.add)
                    ins.then_inc(v_out, 1)

                def rotate(b, u):
                    s = 2 * b + u
                    dve.wait_ge(cos_done, s + 1)
                    dve.wait_ge(sin_done, s + 1)
                    q = raw[u][:, 0:2, :]
                    nc.vector.tensor_tensor(q, q, raw[u][:, 2:4, :], ALU.add).then_inc(rope_done, 1)

                def residual(b, u):
                    dve.wait_ge(hi_done, 2 * b + u + 1)
                    nc.vector.tensor_tensor(res[u][:], raw[u][:, 0:2, :], term[u][0][:], ALU.subtract).then_inc(r1_done, 1)

                def low(b, u):
                    dve.wait_ge(mid_done, 2 * b + u + 1)
                    nc.vector.tensor_tensor(term[u][2][:], res[u][:], term[u][1][:], ALU.subtract).then_inc(lo_done, 1)
                staged(dve, NS, (0, norm), (2, residual), (1, cos), (2, low), (1, rotate), (1, value))

            @block.gpsimd
            def _(pool):
                def sin(b, u):
                    pool.wait_ge(qk_out, 4 * (2 * b + u) + 4)
                    sinb = w.rope[:, 1:2, u * ST:(u + 1) * ST].to_broadcast([P, 2, ST])
                    nc.gpsimd.tensor_tensor(raw[u][:, 2:4, :], raw[u][:, 2:4, :], sinb, ALU.mult).then_inc(sin_done, 1)
                pool.memset(w.operands[:].rearrange("p n h t -> p (n h t)").bitcast(F32), 0.0).then_inc(zeroed, 1)
                staged(pool, NS, (0, sin))
                pool.wait_ge(zeroed, 1)
                pool.wait_ge(sin_done, NS)
                pool.memset(w.operands[MROW:MROW + 2, 3].rearrange("p h t -> p (h t)").bitcast(F32), TWO_BF16_ONES)

            @block.scalar
            def _(act):
                count = act.alloc_register("qkv_count")

                def bias(b, u):
                    s = 2 * b + u
                    after(act, lo_done, s - 1)
                    for n in range(4):
                        act.wait_ge(qk_ps, 4 * s + n + 1)
                        nc.scalar.activation(raw[u][:, n, :], pq[:, n, :], ACT.Identity,
                                             bias=w.bqk[:, n:n + 1]).then_inc(qk_out, 1)

                def modulate(b, u):
                    s = 2 * b + u
                    after(act, v_ps, s - 1)
                    wait_before(act, count, tr_done, s + 1, norm_done)
                    nc.scalar.activation(hT[u][:], pT[:, u, :], ACT.Identity, bias=w.mod[:, 0, 0, bass.ds(b, 1)],
                                         scale=w.mod[:, 0, 1, bass.ds(b, 1)]).then_inc(h_done, 1)

                def high(b, u):
                    act.wait_ge(rope_done, 2 * b + u + 1)
                    after(act, stored[u], b * 16 * 3)
                    nc.scalar.copy(term[u][0][:], raw[u][:, 0:2, :]).then_inc(hi_done, 1)

                def middle(b, u):
                    act.wait_ge(r1_done, 2 * b + u + 1)
                    nc.scalar.copy(term[u][1][:], res[u][:]).then_inc(mid_done, 1)
                staged(act, NS, (2, high), (1, bias), (0, modulate), (2, middle))

            @block.tensor
            def _(pe):
                def project(b, u):
                    s = 2 * b + u
                    pe.wait_ge(h_done, s + 1)
                    for n in range(4):
                        after(pe, qk_out, 4 * (s - 1) + n + 1)
                        nc.tensor.matmul(pq[:, n, :], w.wqk[:, n, :], hT[u][:], start=True, stop=True).then_inc(qk_ps, 1)
                    after(pe, v_out, s - 1)
                    for j in range(4):
                        ins = nc.tensor.matmul(pv[:, u, j * C:(j + 1) * C], hT[u][:, j * C:(j + 1) * C],
                                               w.wqkv[:, 2 * C:3 * C], start=True, stop=True)
                    ins.then_inc(v_ps, 1)

                def transpose(b, u):
                    s = 2 * b + u
                    pe.wait_ge(norm_done, s + 1)
                    after(pe, h_done, s - 1)
                    for j in range(4):
                        ins = nc.tensor.transpose(pT[:, u, j * C:(j + 1) * C], xn[u][:, j, :], w.ident[:])
                    ins.then_inc(tr_done, 1)
                staged(pe, NS, (1, project), (0, transpose))

            @block.sync
            def _(sp):
                def store(b, u):
                    s = 2 * b + u
                    for n, ready in enumerate((hi_done, mid_done, lo_done)):
                        sp.wait_ge(ready, s + 1)
                        dst = d.qk[:, :, n].rearrange("s b c t -> b c s t")[bass.ds(b, 1), :, :, u * ST:(u + 1) * ST][0]
                        sp.dma_start(dst, term[u][n][:]).then_inc(stored[u], 16)
                staged(sp, NS, (0, store))
                for u in range(2):
                    sp.wait_ge(stored[u], NB * 16 * 3)
                sp.wait_ge(w.empty_out, 32)


CHUNKS = [
    (0, [(0, 0, 512, 0)]),
    (0, [(1, 128, 384, 0), (3, 384, 128, 384)]),
    (0, [(2, 256, 256, 0)]),
    (1, [(0, 512, 512, 0)]), (1, [(1, 512, 512, 0)]), (1, [(2, 512, 512, 0)]), (1, [(3, 512, 512, 0)]),
    (1, [(4, 512, 512, 0)]),
    (1, [(5, 640, 384, 0), (7, 896, 128, 384)]),
    (1, [(6, 768, 256, 0)]),
]
NCH = len(CHUNKS)
HALF_END = [2, 9]
SITEMS = ([(0, [0, 1, 2, 3], 128), (1, [0, 1, 2, 3], 256), (2, [0, 1], 512), (2, [2, 3], 512), (3, [0, 1], 512), (3, [2, 3], 512)]
          + [(i, [h], 1024) for i in range(4, 8) for h in range(4)])
PLAN = {c: [] for c in range(NCH)}
for _n, _it in enumerate(sorted(range(len(SITEMS)), key=lambda n: SITEMS[n][0])):
    PLAN[min(_n * 8 // len(SITEMS), 7)].append(_it)
MAXT, O0, O1 = "max", "o0", "o1"


def items_of(first, nxt):
    out = []
    for c in range(NCH):
        here = [("s", n) for n in PLAN[c]] if nxt else []
        if c == 2 and not first:
            here.append((O1, None))
        if c == 6:
            here.append((O0, None))
        if c == 8 and nxt:
            here.append((MAXT, None))
        out.append(here)
    return out


def attention_phase(nc, w, d):
    with ExitStack() as ctx:
        sb = lambda n, s, t=F32: ctx.enter_context(nc.sbuf_tensor(n, s, t))
        ps = lambda n, s, t=F32: ctx.enter_context(nc.psum_tensor(n, s, t))
        sem = lambda n: semaphore_of(nc, ctx, n)
        odd = sb("odd_operands", [P, 4, HQ, T], BF16)
        qa, ka, qb, kb = ([x[:, n] for x in (w.operands, odd)] for n in range(4))
        vs = [sb(f"vs{p}", [P, TPB, HQ, 32]) for p in range(2)]
        prob = [sb(f"prob{p}", [P, HQ, ST]) for p in range(2)]
        osb = [sb(f"osb{p}", [P, ST]) for p in range(2)]
        part = [sb(f"part{p}", [P, HQ, TPB]) for p in range(2)]
        mrow = [sb(f"mrow{p}", [HQ * TPB, 2, P], BF16) for p in range(2)]
        rec = [sb(f"rec{p}", [P, 4, HQ]) for p in range(2)]
        sps = [ps(f"sps{p}", [P, 2 * ST]) for p in range(2)]
        tps = ps("tps", [P, 3, ST])
        ops = ps("ops", [P, ST])
        s_ready, s_free, t_ready, exp_done, masked = sem("s_ready"), sem("s_free"), sem("t_ready"), sem("exp_done"), sem("masked")
        pv_done, o_out, v_copied, rec_done, zeroed = (sem("pv_done"), sem("o_out"), sem("v_copied"),
                                                     sem("rec_done"), sem("zeroed"))
        max_hi, odd_set, bias_gated = sem("max_hi"), sem("odd_set"), sem("bias_gated")
        gated_bias = sb("gated_bias", [P, NB, C])
        a_in = [sem(f"a_in{p}") for p in range(2)]
        b_in = [sem(f"b_in{p}") for p in range(2)]
        m_in = [sem(f"m_in{p}") for p in range(2)]

        NS = len(SITEMS)
        LOADED = 6 * 16
        first_items = sum(len(x) for x in items_of(True, True))
        body_items = sum(len(x) for x in items_of(False, True))

        def item_base(t):
            return (NS + 1) if isinstance(t, int) and t == 0 else (NS + 1 + first_items - body_items) + body_items * t

        mask_count = [0]
        for half, parts in CHUNKS:
            mask_count.append(mask_count[-1] + sum(1 for j, q0, n, col in parts if q0 == j * P))
        NM = mask_count[-1]

        def bodies(eng, body):
            body(0, 0, True, True)
            with eng.Fori(0, (NQUAD - 2) // 2) as i:
                body(2 * i + 1, 1, False, True)
                body(2 * i + 2, 0, False, True)
            body(NQUAD - 1, 1, False, False)

        with nc.Block() as block:
            @block.gpsimd
            def _(pool):
                pool.memset(odd[:].rearrange("p n h t -> p (n h t)").bitcast(F32), 0.0).then_inc(zeroed, 1)
                pool.wait_ge(zeroed, 1)
                pool.memset(kb[1][MROW:MROW + 2].rearrange("p h t -> p (h t)").bitcast(F32), TWO_BF16_ONES).then_inc(odd_set, 1)
                pool.wait_ge(odd_set, 1)
                for p in range(2):
                    ins = pool.memset(vs[p][:], 0.0)
                ins.then_inc(zeroed, 1)
                pool.wait_ge(zeroed, 2)
                for p in range(2):
                    ins = pool.memset(vs[p][:, :, :, HD:HD + 1], 1.0)
                ins.then_inc(zeroed, 1)
                pool.wait_ge(zeroed, 3)

                def copy_v(t, p):
                    src = w.v[:, t] if isinstance(t, int) else w.v[:, bass.ds(t, 1)][:, 0]
                    nc.gpsimd.tensor_copy(vs[p][:, :, :, 0:HD], src.rearrange("p k (h e) -> p k h e", h=HQ)).then_inc(v_copied, 1)

                def body(t, p, first, nxt):
                    for c, (half, parts) in enumerate(CHUNKS):
                        if mask_count[c + 1] > mask_count[c]:
                            wait_before(pool, count, exp_done, 4 * NCH * t + 4 * (c + 1), t_ready)
                        for j, q0, n, col in parts:
                            if q0 == j * P:
                                blk = prob[c % 2][:, :, col:col + P]
                                nc.gpsimd.affine_select(out=blk, in_=blk, pattern=[[0, HQ], [1, P]], compare_op=ALU.is_ge,
                                                        fill=0.0, base=0, channel_multiplier=-1).then_inc(masked, 1)
                        if c == 2 and nxt:
                            if not (isinstance(t, int) and t == 0):
                                pool.wait_ge(pv_done, NCH * t)
                            copy_v(t + 1, 1 - p)
                count = pool.alloc_register("exp_count")
                copy_v(0, 0)
                for b in range(NB):
                    ins = nc.gpsimd.tensor_tensor(gated_bias[:, b], w.gate[:, 0, b], w.bo[:], ALU.mult)
                ins.then_inc(bias_gated, 1)
                pool.wait_ge(bias_gated, 1)
                for b in range(NB):
                    xb = w.x[:, b * TPB:(b + 1) * TPB, :]
                    nc.gpsimd.tensor_tensor(xb, xb, gated_bias[:, b:b + 1].to_broadcast([P, TPB, C]), ALU.add)
                bodies(pool, body)

            @block.sync
            def _(sp):
                def load(t, p, s_in, qq, kk):
                    b, quad = (t // NQ, t % NQ) if isinstance(t, int) else (t >> 2, t & (NQ - 1))
                    row = 0
                    for n, rows in enumerate((3, 2, 1)):
                        for side, buf, term, step in ((0, qq, n, 0), (1, kk, 0, C * T)):
                            at = b * (3 * C * T) + quad * (HD * HQ * T) + (side * NB * 3 + term) * (C * T)
                            src = bass.AP(d.qk.tensor, at, [[step, rows], [HQ * T, HD], [1, HQ * T]])
                            sp.dma_start(buf[row * HD:(row + rows) * HD, :, :].rearrange("p h t -> p (h t)"), src).then_inc(s_in, 16)
                        row += rows

                load(0, 0, a_in[0], qa[0], ka[0])
                load(0, 0, b_in[0], qb[0], kb[0])
                sp.wait_ge(odd_set, 1)
                load(1, 1, a_in[1], qa[1], ka[1])
                load(1, 1, b_in[1], qb[1], kb[1])

                def max_to_rows(n, p):
                    sp.wait_ge(s_free, item_base(n))
                    for r in range(2):
                        sp.dma_start(qb[p][MROW + r:MROW + r + 1, :, :].rearrange("o h (k q) -> o (h k) q", k=TPB),
                                     mrow[p][:, r, :]).then_inc(m_in[p], 16)
                max_to_rows(0, 0)

                def body(t, p, first, nxt):
                    if nxt:
                        tn = t + 2
                        if not isinstance(t, int):
                            tn = (t + 2) & (NQUAD - 1)
                        load(tn, p, a_in[p], qa[p], ka[p])
                    if nxt:
                        max_to_rows(t + 1, 1 - p)
                        sp.wait_ge(t_ready, 4 * NCH * (t + 1))
                        load(tn, p, b_in[p], qb[p], kb[p])
                bodies(sp, body)
                for p in range(2):
                    sp.wait_ge(a_in[p], LOADED * (NQUAD // 2 + (1 if p == 0 else 0)))
                    sp.wait_ge(b_in[p], LOADED * (NQUAD // 2 + (1 if p == 0 else 0)))

            @block.tensor
            def _(pe):
                item = [0, 0]

                def slot():
                    return sps[(item[1] + par[0]) % 2]

                par = [0]

                def acquire():
                    n = item[0] + item[1]
                    if not (isinstance(n, int) and n < 2):
                        pe.wait_ge(s_free, n - 1)

                def filled(ins):
                    ins.then_inc(s_ready, 1)
                    item[1] += 1

                def s_item(n, p):
                    i, heads, step = SITEMS[n]
                    acquire()
                    out = slot()
                    for x, h in enumerate(heads):
                        for c0 in range(0, (i + 1) * P, ST):
                            n1 = min(ST, (i + 1) * P - c0)
                            diag = c0 + n1 == (i + 1) * P
                            ins = nc.tensor.matmul(out[:, x * step + c0:x * step + c0 + n1], qa[p][:, h, i * P:(i + 1) * P],
                                                   ka[p][:, h, c0:c0 + n1], start=True, stop=not diag, skip_group_check=True)
                        e = x * step + i * P
                        ins = nc.tensor.matmul(out[:, e:e + P], w.identb[:], w.maskb[:], start=False, stop=True, skip_group_check=True)
                    filled(ins)

                def max_item(n, p, last):
                    pe.wait_ge(s_free, last)
                    acquire()
                    filled(nc.tensor.transpose(slot()[0:HQ * TPB, 0:P], part[p][:].rearrange("p h k -> p (h k)"), w.ident[:]))

                def o_item(half, count):
                    pe.wait_ge(o_out, count)
                    acquire()
                    out = slot()
                    for x in range(4):
                        ins = nc.tensor.transpose(out[:, x * P:(x + 1) * P], osb[half][:, x * P:(x + 1) * P], w.ident[:])
                    filled(ins)

                def pv(t, p, c):
                    half, parts = CHUNKS[c]
                    if mask_count[c + 1] > mask_count[c]:
                        pe.wait_ge(masked, NM * t + mask_count[c + 1])
                    else:
                        pe.wait_ge(exp_done, 4 * NCH * t + 4 * (c + 1))
                    if c == 0:
                        pe.wait_ge(v_copied, t + 1)
                    new = c == 0 or c == HALF_END[0] + 1
                    if new:
                        n = 2 * t + half
                        if not (isinstance(n, int) and n == 0):
                            pe.wait_ge(o_out, n)
                    for j, q0, n, col in parts:
                        o0 = q0 - half * ST
                        for h in range(HQ):
                            ins = nc.tensor.matmul(ops[32 * h:32 * h + 32, o0:o0 + n], vs[p][:, j, h, :],
                                                   prob[c % 2][:, h, col:col + n], start=new, stop=c in HALF_END,
                                                   skip_group_check=True, tile_position=(0, 32 * h))
                    ins.then_inc(pv_done, 1)

                def body(t, p, first, nxt):
                    base = item_base(t)
                    item[0], item[1] = base, 0
                    par[0] = (NS + 1 + (0 if first else first_items) + (0 if first or p == 1 else body_items)) % 2
                    todo = items_of(first, nxt)
                    done = 0
                    for c, (half, parts) in enumerate(CHUNKS):
                        if c == 0:
                            pe.wait_ge(b_in[p], quads(t, p, LOADED))
                            pe.wait_ge(m_in[p], quads(t, p, 2 * 16))
                        todo_c = list(todo[c])
                        for h in range(HQ):
                            k = 4 * c + h
                            prev = 4 * NCH * t + k - 2 if k >= 3 else 4 * NCH * (t - 1) + {0: 40, 1: 38, 2: 39}[k]
                            if not (isinstance(prev, int) and prev <= 0):
                                pe.wait_ge(exp_done, prev)
                            for j, q0, n, col in parts:
                                ins = nc.tensor.matmul(tps[:, k % 3, col:col + n], kb[p][:, h, j * P:(j + 1) * P],
                                                       qb[p][:, h, q0:q0 + n], start=True, stop=True)
                            ins.then_inc(t_ready, 1)
                            if h in (1, 2) and todo_c and todo_c[0][0] == "s":
                                if done == 0:
                                    pe.wait_ge(a_in[1 - p], quads(t + 1, 1 - p, LOADED))
                                s_item(todo_c.pop(0)[1], 1 - p)
                                done = item[1]
                        if c > 0:
                            pv(t, p, c - 1)
                        elif not first:
                            pv(t - 1, 1 - p, NCH - 1)
                        for kind, n in todo_c:
                            if kind == "s":
                                s_item(n, 1 - p)
                                done = item[1]
                            elif kind == O1:
                                o_item(1, 2 * t)
                            elif kind == O0:
                                o_item(0, 2 * t + 1)
                            else:
                                max_item(t + 1, 1 - p, base + done)

                def quads(t, p, signals):
                    return signals * (t // 2 + 1) if isinstance(t, int) else signals // 2 * (t - p) + signals

                pe.wait_ge(a_in[0], LOADED)
                for n in range(NS):
                    s_item(n, 0)
                max_item(0, 0, NS)
                bodies(pe, body)
                t = NQUAD - 1
                pv(t, 1, NCH - 1)
                o_item(1, 2 * NQUAD)

            @block.scalar
            def _(act):
                def o_copy(half):
                    nc.scalar.copy(osb[half][:], ops[:]).then_inc(o_out, 1)

                def body(t, p, first, nxt):
                    for c, (half, parts) in enumerate(CHUNKS):
                        n = sum(x[2] for x in parts)
                        for h in range(HQ):
                            k = 4 * c + h
                            act.wait_ge(t_ready, 4 * NCH * t + k + 1)
                            if h == 0:
                                v = NCH * t + c - 1
                                if not (isinstance(v, int) and v <= 0):
                                    act.wait_ge(pv_done, v)
                            nc.scalar.activation(prob[c % 2][:, h, 0:n], tps[:, k % 3, 0:n], ACT.Exp,
                                                 scale=float(HD) ** -0.5).then_inc(exp_done, 1)
                        if c == 0 and not first:
                            act.wait_ge(pv_done, NCH * t)
                            o_copy(1)
                        if c == 3:
                            act.wait_ge(pv_done, NCH * t + 3)
                            o_copy(0)
                bodies(act, body)
                act.wait_ge(pv_done, NCH * NQUAD)
                o_copy(1)

            @block.vector
            def _(dve):
                item = [0, 0]
                par = [0]

                def ready():
                    dve.wait_ge(s_ready, item[0] + item[1] + 1)
                    return sps[(item[1] + par[0]) % 2]

                def freed(ins):
                    ins.then_inc(s_free, 1)
                    item[1] += 1

                def s_item(n, p):
                    i, heads, step = SITEMS[n]
                    src = ready()
                    wd = (i + 1) * P
                    if len(heads) > 1:
                        src = src[:, 0:len(heads) * step].rearrange("p (h k) -> p h k", h=len(heads))[:, :, 0:wd]
                    else:
                        src = src[:, 0:wd].rearrange("p (h k) -> p h k", h=1)
                    freed(nc.vector.tensor_reduce(part[p][:, heads[0]:heads[-1] + 1, i:i + 1].rearrange("p h o -> p (h o)"),
                                                  src, AX.X, ALU.max, negate=True))

                def max_item(n, p):
                    src = ready()
                    nc.vector.tensor_copy(mrow[p][:, 0, :], src[0:HQ * TPB, 0:P]).then_inc(max_hi, 1)
                    dve.wait_ge(max_hi, n + 1)
                    ins = nc.vector.tensor_tensor(mrow[p][:, 1, :], src[0:HQ * TPB, 0:P], mrow[p][:, 0, :], ALU.subtract)
                    freed(ins)

                def o_item(t, half):
                    src = ready()[:, 0:ST].rearrange("p (x h e) -> p x h e", x=4, h=HQ)
                    nc.vector.reciprocal(rec[half][:], src[:, :, :, HD]).then_inc(rec_done, 1)
                    dve.wait_ge(rec_done, 2 * t + half + 1)
                    dst = (w.y[:, t] if isinstance(t, int) else w.y[:, bass.ds(t, 1)][:, 0])[:, half * 4:half * 4 + 4, :]
                    recb = rec[half][:].rearrange("p x (h o) -> p x h o", o=1).to_broadcast([P, 4, HQ, HD])
                    freed(nc.vector.tensor_tensor(dst.rearrange("p x (h e) -> p x h e", h=HQ), src[:, :, :, 0:HD], recb, ALU.mult))

                def body(t, p, first, nxt):
                    item[0], item[1] = item_base(t), 0
                    par[0] = (NS + 1 + (0 if first else first_items) + (0 if first or p == 1 else body_items)) % 2
                    for here in items_of(first, nxt):
                        for kind, n in here:
                            if kind == "s":
                                s_item(n, 1 - p)
                            elif kind == O1:
                                o_item(t - 1, 1)
                            elif kind == O0:
                                o_item(t, 0)
                            else:
                                max_item(t + 1, 1 - p)
                for n in range(NS):
                    s_item(n, 0)
                max_item(0, 0)
                bodies(dve, body)
                o_item(NQUAD - 1, 1)


def project_phase(nc, w, d):
    with ExitStack() as ctx:
        sb = lambda n, s, t=F32: ctx.enter_context(nc.sbuf_tensor(n, s, t))
        ps = lambda n, s, t=F32: ctx.enter_context(nc.psum_tensor(n, s, t))
        sem = lambda n: semaphore_of(nc, ctx, n)
        ys = [sb(f"ys{u}", [P, 4, C]) for u in range(2)]
        yT = [sb(f"yT{u}", [P, ST]) for u in range(2)]
        o = [sb(f"o{u}", [P, 4, C]) for u in range(2)]
        pT = ps("pTo", [P, 2, ST])
        po = ps("po", [P, 2, ST])
        y_in, y_tr, y_T, o_ps, o_step, x_done = sem("y_in"), sem("y_tr"), sem("y_T"), sem("o_ps"), sem("o_step"), sem("x_done")
        with nc.Block() as block:
            @block.scalar
            def _(act):
                def rows(b, u):
                    after(act, y_tr, 2 * b + u - 1)
                    yb = w.y[:].rearrange("p (b q) k c -> p b k q c", q=NQ)[:, bass.ds(b, 1), u * 4:u * 4 + 4, :, :]
                    for j in range(4):
                        ins = nc.scalar.copy(ys[u][:, j, :].rearrange("p (q c) -> p q c", q=NQ), yb[:, 0, j])
                    ins.then_inc(y_in, 1)
                staged(act, 2 * NB, (0, rows))

            @block.tensor
            def _(pe):
                def transpose(b, u):
                    s = 2 * b + u
                    pe.wait_ge(y_in, s + 1)
                    after(pe, y_T, s - 1)
                    for j in range(4):
                        ins = nc.tensor.transpose(pT[:, u, j * C:(j + 1) * C], ys[u][:, j, :], w.ident[:])
                    ins.then_inc(y_tr, 1)

                def project(b, u):
                    s = 2 * b + u
                    pe.wait_ge(y_T, s + 1)
                    after(pe, x_done, s - 1)
                    for j in range(4):
                        ins = nc.tensor.matmul(po[:, u, j * C:(j + 1) * C], yT[u][:, j * C:(j + 1) * C], w.wo[:], start=True, stop=True)
                    ins.then_inc(o_ps, 1)
                staged(pe, 2 * NB, (0, transpose), (1, project))

            @block.vector
            def _(dve):
                def transposed(b, u):
                    s = 2 * b + u
                    dve.wait_ge(y_tr, s + 1)
                    after(dve, o_ps, s - 1)
                    nc.vector.tensor_copy(yT[u][:], pT[:, u, :]).then_inc(y_T, 1)

                def residual(b, u):
                    s = 2 * b + u
                    dve.wait_ge(o_ps, s + 1)
                    link = Chain(dve, o_step, s)
                    g4 = w.gate[:, 0, bass.ds(b, 1), :].to_broadcast([P, 4, C])
                    link(nc.vector.tensor_tensor(o[u][:], po[:, u, :].rearrange("p (j c) -> p j c", j=4), g4, ALU.mult))
                    xs = w.x[:, bass.ds(b * TPB + u * 4, 4), :]
                    nc.vector.tensor_tensor(xs, xs, o[u][:], ALU.add).then_inc(x_done, 1)
                staged(dve, 2 * NB, (0, transposed), (1, residual))


def stats_phase(nc, w, name, d=None, layer=None):
    with ExitStack() as ctx:
        sem = lambda n: semaphore_of(nc, ctx, n + name)
        st_step, root, r_in, r_tr = sem("st_step"), sem("root"), sem("r_in"), sem("r_tr")
        if layer is not None:
            rows = ctx.enter_context(nc.sbuf_tensor(f"router_rows{layer}", [NE + 1, C], F32))
            rt_ps = ctx.enter_context(nc.psum_tensor(f"router_ps{layer}", [P, NE + 1], F32))
            NR = NE + 1 - layer
        with nc.Block() as block:
            @block.sync
            def _(sp):
                if layer is not None:
                    sp.dma_start(rows[0:NE, :], (d.gate_w, d.wg)[layer]).then_inc(r_in, 16)
                    if layer == 0:
                        sp.dma_start(rows[NE:NE + 1, :], d.seg).then_inc(r_in, 16)

            @block.tensor
            def _(pe):
                if layer is not None:
                    pe.wait_ge(r_in, 16 * (2 - layer))
                    nc.tensor.transpose(rt_ps[:, 0:NR], rows[0:NR, :], w.ident[0:NR, 0:NR]).then_inc(r_tr, 1)

            @block.vector
            def _(dve):
                link = Chain(dve, st_step)
                link(layernorm_stats(nc, dve, link, w.x, w))
                if layer is not None:
                    dve.wait_ge(r_tr, 1)
                    nc.vector.tensor_copy(w.rt[:], rt_ps[:, 0:NR])
                dve.wait_ge(root, 1)
                nc.vector.reciprocal(w.rstd[:], w.t1[:])

            @block.scalar
            def _(act):
                act.wait_ge(st_step, 8)
                nc.scalar.activation(w.t1[:], w.t1[:], ACT.Sqrt).then_inc(root, 1)


NE = 8
SI = 352
XW = C + 2
NSLOT = 2 * NT + NE
UN = 8
LAG = 2


def chunks_of(width):
    return {176: [88, 88], 352: [128, 128, 96]}[width]


def weights_parts(nc, w, d, layer, ctx, up_banks, down_banks):
    I = (176, 352)[layer]
    NK = layer + 1
    R = 88
    WB = 4
    sb = lambda n, s, t=F32: ctx.enter_context(nc.sbuf_tensor(f"{n}_w{layer}", s, t))
    sem = lambda n: semaphore_of(nc, ctx, f"{n}_w{layer}")
    rows = [sb(f"rows{u}", [R, 2, 4, C]) for u in range(WB)]
    dn = [sb(f"dn{u}", [P, 352]) for u in range(WB)]
    w_in = [sem(f"w_in{u}") for u in range(WB)]
    w_tr, w_out = sem("w_tr"), sem("w_out")
    ups, down = ((d.gu0,), d.dn0) if layer == 0 else ((d.w1, d.w2), d.w3)
    at = lambda a, e: a[:, e] if isinstance(e, int) else a[:, bass.ds(e, 1)][:, 0]

    def loads(sp):
        def load(i, u):
            e = WB * i + u
            after(sp, w_tr, e - WB + 1)
            pick = lambda a: a[e] if isinstance(e, int) else a[bass.ds(e, 1)][0]
            for k, src in enumerate(ups):
                sp.dma_start(rows[u][:, k], pick(src).rearrange("(n p) c -> p n c", p=R)).then_inc(w_in[u], 16)
            sp.dma_start(dn[u][:, 0:I], pick(down)).then_inc(w_in[u], 16)
        staged(sp, NE, (0, load), unroll=WB)
        if layer == 0:
            sp.wait_ge(w_tr, NE - WB + 1)
            for k, src in enumerate((d.sg, d.su)):
                sp.dma_start(rows[0][:, k], src.rearrange("(n p) c -> p n c", p=R)).then_inc(w_in[0], 16)
            sp.dma_start(dn[0][:], d.sd).then_inc(w_in[0], 16)

    def transposes(pe):
        def up_tr(bank, u, k):
            for m in range(4):
                ins = nc.tensor.transpose(bank[:, m * R:(m + 1) * R], rows[u][:, k, m, :], w.ident[0:R, 0:R])
            return ins

        def down_tr(bank, u, width):
            c0 = 0
            for m, cw in enumerate(chunks_of(width)):
                ins = nc.tensor.transpose(bank[0:cw, m * C:(m + 1) * C], dn[u][:, c0:c0 + cw], w.ident[:])
                c0 += cw
            return ins

        def turn(i, u):
            pe.wait_ge(w_in[u], 16 * (NK + 1) * (i + 1))
            after(pe, w_out, WB * i + u - 1)
            for k in range(NK):
                up_tr(up_banks[u % 2][k], u, k)
            down_tr(down_banks[u % 2], u, I).then_inc(w_tr, 1)
        staged(pe, NE, (0, turn), unroll=WB)
        if layer == 0:
            pe.wait_ge(w_in[0], 16 * (NK + 1) * (NE // WB) + 16 * 3)
            pe.wait_ge(w_out, NE)
            for k in range(2):
                up_tr((up_banks[0] + up_banks[1])[k], 0, k)
            down_tr(down_banks[0], 0, SI).then_inc(w_tr, 1)
            pe.wait_ge(w_out, NE + 1)

    def copies(act):
        def down_out(dst, bank, width):
            cs = chunks_of(width)
            full = [m for m, cw in enumerate(cs) if cw == cs[0]]
            ins = nc.scalar.copy(dst[0:cs[0], 0:len(full), :], bank[0:cs[0], 0:len(full) * C].rearrange("p (m c) -> p m c", c=C))
            if len(full) < len(cs):
                ins = nc.scalar.copy(dst[0:cs[-1], len(full), :], bank[0:cs[-1], len(full) * C:len(cs) * C])
            return ins

        def turn(i, u):
            e = WB * i + u
            act.wait_ge(w_tr, e + 1)
            for k in range(NK):
                nc.scalar.copy(at(w.up, e)[:, k, :], up_banks[u % 2][k][:, 0:352])
            down_out(at(w.down, e), down_banks[u % 2], I).then_inc(w_out, 1)
        staged(act, NE, (0, turn), unroll=WB)
        if layer == 0:
            act.wait_ge(w_tr, NE + 1)
            for k in range(2):
                nc.scalar.copy(w.shgu[:, k, :], (up_banks[0] + up_banks[1])[k][:, 0:352])
            down_out(w.shd, down_banks[0], SI).then_inc(w_out, 1)
    return loads, transposes, copies


def route_phase(nc, w, d, layer):
    NR = NE + 1 if layer == 0 else NE
    cols = chunks_of(SI)
    with ExitStack() as ctx:
        sb = lambda n, s, t=F32: ctx.enter_context(nc.sbuf_tensor(f"{n}_{layer}", s, t))
        sem = lambda n: semaphore_of(nc, ctx, f"{n}_{layer}")
        hs = [sb(f"hs{u}", [P, 4, C]) for u in range(2)]
        hT = sb("hTr", [P, 2 * NB, ST])
        lg = sb("lg", [P, NT, NR])
        r_step, h_done, h_kept, tr_done, hT_done, lg_ps, lg_out = (sem("r_step"), sem("h_done"), sem("h_kept"), sem("tr_done"),
                                                                  sem("hT_done"), sem("lg_ps"), sem("lg_out"))
        with ExitStack() as banks:
            ps = lambda n, s, t=F32: banks.enter_context(nc.psum_tensor(f"{n}_{layer}", s, t))
            hr = [sb(f"hr{u}", [P, ST]) for u in range(2)]
            pT = ps("pTr", [P, 2, ST])
            pl = ps("pl", [P, 2, ST])
            with nc.Block() as block:
                @block.vector
                def _(dve):
                    def rows(b, u):
                        s = 2 * b + u
                        after(dve, tr_done, s - 1)
                        after(dve, h_kept, s - 1)
                        link = Chain(dve, r_step, 2 * s)
                        for j in range(4):
                            t = b * TPB + u * 4 + j
                            ins = nc.vector.tensor_scalar(hs[u][:, j, :], w.x[:, t, :], w.mean[:, bass.ds(t, 1)],
                                                          w.rstd[:, bass.ds(t, 1)], ALU.subtract, ALU.mult)
                        link(ins)
                        link(nc.vector.tensor_tensor(hs[u][:], hs[u][:], w.modr[:, 2 * layer + 1, bass.ds(b, 1), :].to_broadcast([P, 4, C]), ALU.mult))
                        nc.vector.tensor_tensor(hs[u][:], hs[u][:], w.modr[:, 2 * layer, bass.ds(b, 1), :].to_broadcast([P, 4, C]), ALU.add).then_inc(h_done, 1)

                    def logits(b, u):
                        dve.wait_ge(lg_ps, 2 * b + u + 1)
                        nc.vector.tensor_copy(lg[:, bass.ds(b * TPB + u * 4, 4), :],
                                              pl[:, u, 0:4 * NR].rearrange("p (j r) -> p j r", j=4)).then_inc(lg_out, 1)
                    staged(dve, 2 * NB, (0, rows), (2, logits))

                @block.gpsimd
                def _(pool):
                    def keep(b, u):
                        pool.wait_ge(h_done, 2 * b + u + 1)
                        nc.gpsimd.tensor_copy(w.h[:, bass.ds(b * TPB + u * 4, 4), 0:C], hs[u][:]).then_inc(h_kept, 1)
                    nc.gpsimd.iota(w.h[:, :, C:C + 1].bitcast(U32), pattern=[[P, NT], [0, 1]], base=0, channel_multiplier=1)
                    staged(pool, 2 * NB, (0, keep))

                @block.scalar
                def _(act):
                    def transposed(b, u):
                        s = 2 * b + u
                        act.wait_ge(tr_done, s + 1)
                        after(act, lg_ps, s - 1)
                        ins = nc.scalar.copy(hr[u][:], pT[:, u, :])
                        if layer == 0:
                            ins = nc.scalar.copy(hT[:, bass.ds(s, 1), :].rearrange("p o t -> p (o t)"), pT[:, u, :])
                        ins.then_inc(hT_done, 1)
                    staged(act, 2 * NB, (0, transposed))

                @block.tensor
                def _(pe):
                    def transpose(b, u):
                        s = 2 * b + u
                        pe.wait_ge(h_done, s + 1)
                        after(pe, hT_done, s - 1)
                        for j in range(4):
                            ins = nc.tensor.transpose(pT[:, u, j * C:(j + 1) * C], hs[u][:, j, :], w.ident[:])
                        ins.then_inc(tr_done, 1)

                    def logits(b, u):
                        s = 2 * b + u
                        pe.wait_ge(hT_done, s + 1)
                        after(pe, lg_out, s - 1)
                        for j in range(4):
                            ins = nc.tensor.matmul(pl[:, u, j * NR:(j + 1) * NR], hr[u][:, j * C:(j + 1) * C], w.rt[:],
                                                   start=True, stop=True)
                        ins.then_inc(lg_ps, 1)
                    staged(pe, 2 * NB, (2, logits), (0, transpose))

        sc = sb("sc", [P, NT, NE])
        m1 = sb("m1", [P, NT])
        top = sb("top", [P, NT, 8])
        idx = sb("idx", [P, NT, 8], U32)
        idf = sb("idf", [P, NT, 2])
        hot = [sb(f"hot{k}", [P, NE, NT]) for k in range(2)]
        both = sb("both", [P, NE, NT], BF16)
        bsum = sb("bsum", [P, NE * NT])
        ones = sb("ones", [P, NE * NT])
        excl = sb("excl", [P, NE, NT])
        base = sb("base", [P, NE])
        nt = sb("nt", [P, NE])
        off = sb("off", [P, NE])
        tmp = sb("tmp", [P, NE, NT])
        slf = sb("slf", [P, NT])
        ge = sb("ge", [P, NSLOT, NE])
        te = sb("te", [P, NSLOT + UN])
        word = sb("word", [P, NSLOT // UN + 1])
        ps = lambda n, s, t=F32: ctx.enter_context(nc.psum_tensor(f"{n}_{layer}", s, t))
        pp = ps("pp", [P, 2, NE * NT])
        if layer == 0:
            sg = [sb(f"sg{u}", [P, ST]) for u in range(2)]
            hid = [sb(f"hid{u}", [P, ST]) for u in range(2)]
            pg = ps("pg", [P, 2, 2, ST])
            pd = ps("pd", [P, 2, ST])
        g_ps, s_done, hid_done, d_ps, sh_out = sem("g_ps"), sem("s_done"), sem("hid_done"), sem("d_ps"), sem("sh_out")
        q_step, ex_done, both_done, pre_ps = sem("q_step"), sem("ex_done"), sem("both_done"), sem("pre_ps")
        slots_done, scattered, second = sem("slots_done"), w.scattered[layer], sem("second")
        if layer == 0:
            up_banks, down_banks = [[pg[:, 0, 0]], [pg[:, 0, 1]]], [pg[:, 1, 0], pg[:, 1, 1]]
        else:
            gp, dp = ps("gp", [P, 4, ST]), ps("dp", [P, 2, ST])
            up_banks, down_banks = [[gp[:, 2 * u + k] for k in range(2)] for u in range(2)], [dp[:, u] for u in range(2)]
        load_weights, transpose_weights, copy_weights = weights_parts(nc, w, d, layer, ctx, up_banks, down_banks)
        M = len(cols)
        NC = 2 * NB * M
        turn = lambda i, u: 2 * M * i + u
        with nc.Block() as block:
            @block.vector
            def _(dve):
                link = Chain(dve, q_step)
                v = nc.vector
                if layer == 0:
                    link(v.tensor_reduce(m1[:], lg[:, :, 0:NE], AX.X, ALU.max))
                    link(v.tensor_tensor(sc[:], lg[:, :, 0:NE], m1[:].rearrange("p (t o) -> p t o", o=1).to_broadcast([P, NT, NE]), ALU.subtract))
                    dve.wait_ge(ex_done, 2)
                    link(v.tensor_scalar(w.shw[:], w.shw[:], 1.0, None, ALU.add))
                    link(v.reciprocal(w.shw[:], w.shw[:]))
                    link(v.tensor_reduce(m1[:], sc[:], AX.X, ALU.add))
                    link(v.reciprocal(m1[:], m1[:]))
                    link(v.tensor_tensor(sc[:], sc[:], m1[:].rearrange("p (t o) -> p t o", o=1).to_broadcast([P, NT, NE]), ALU.mult))
                else:
                    link(v.tensor_copy(sc[:], lg[:]))
                for t in range(NT):
                    ins = v.max(top[:, t, :], sc[:, t, :])
                link(ins)
                for t in range(NT):
                    ins = v.max_index(idx[:, t, :], top[:, t, :], sc[:, t, :])
                link(ins)
                link(v.tensor_copy(idf[:], idx[:, :, 0:2]))
                eb = w.iota[:, 0:NE].rearrange("p (e o) -> p e o", o=1).to_broadcast([P, NE, NT])
                for k in range(2):
                    ins = v.tensor_tensor(hot[k][:], eb, idf[:, :, k:k + 1].rearrange("p t o -> p o t").to_broadcast([P, NE, NT]), ALU.is_equal)
                link(ins)
                v.tensor_tensor(both[:], hot[0][:], hot[1][:], ALU.add).then_inc(both_done, 1)
                for k in range(2):
                    link(v.tensor_tensor(tmp[:], hot[k][:], sc[:].rearrange("p t e -> p e t"), ALU.mult))
                    link(v.tensor_reduce(w.wt[k][:], tmp[:].rearrange("p e t -> p t e"), AX.X, ALU.add))
                link(v.memset(ones[:], 1.0))
                dve.wait_ge(pre_ps, 1)
                link(v.tensor_copy(bsum[:], pp[:, 1, 0:NE * NT]))
                link(v.tensor_tensor_scan(out=excl[:].rearrange("p e t -> p (e t)"), data0=ones[:], data1=bsum[:], initial=0.0,
                                          op0=ALU.mult, op1=ALU.add))
                link(v.tensor_tensor(excl[:], excl[:], bsum[:].rearrange("p (e t) -> p e t", e=NE), ALU.subtract))
                link(v.tensor_copy(base[:], excl[:, :, 0]))
                link(v.tensor_reduce(nt[:], bsum[:].rearrange("p (e t) -> p e t", e=NE), AX.X, ALU.add))
                link(v.tensor_scalar(nt[:], nt[:], 63.5, 1.0 / P, ALU.add, ALU.mult))
                link(v.tensor_scalar(nt[:], nt[:], 12582912.0, 12582912.0, ALU.add, ALU.subtract))
                link(v.tensor_tensor_scan(out=off[:], data0=ones[:, 0:NE], data1=nt[:], initial=0.0, op0=ALU.mult, op1=ALU.add))
                link(v.tensor_tensor(ge[:], w.iota[:, 0:NSLOT].rearrange("p (i o) -> p i o", o=1).to_broadcast([P, NSLOT, NE]),
                                     off[:].rearrange("p (o e) -> p o e", o=1).to_broadcast([P, NSLOT, NE]), ALU.is_ge))
                link(v.memset(te[:], 0.0))
                link(v.tensor_reduce(te[:, LAG:LAG + NSLOT], ge[:], AX.X, ALU.add))
                link(v.tensor_scalar(te[:, LAG:LAG + NSLOT], te[:, LAG:LAG + NSLOT], float(NE - 1), None, ALU.min))
                digits = te[:].rearrange("p (g j) -> p g j", j=UN)
                link(v.tensor_tensor(digits, digits, w.octal[:].rearrange("p (o j) -> p o j", o=1).to_broadcast([P, NSLOT // UN + 1, UN]), ALU.mult))
                link(v.tensor_reduce(word[:], digits, AX.X, ALU.add))
                link(v.tensor_copy(w.tile_expert[:], word[:]))
                link(v.tensor_tensor(off[:], off[:], nt[:], ALU.subtract))
                link(v.scalar_tensor_tensor(out=off[:], in0=off[:], scalar=float(P), in1=base[:], op0=ALU.mult, op1=ALU.subtract))
                link(v.tensor_tensor(excl[:], excl[:], off[:].rearrange("p (e o) -> p e o", o=1).to_broadcast([P, NE, NT]), ALU.add))
                link(v.tensor_tensor(excl[:], excl[:], pp[:, 0, 0:NE * NT].rearrange("p (e t) -> p e t", e=NE), ALU.add))
                for k in range(2):
                    link(v.tensor_tensor(tmp[:], hot[k][:], excl[:], ALU.mult))
                    link(v.tensor_reduce(slf[:], tmp[:].rearrange("p e t -> p t e"), AX.X, ALU.add))
                    link(v.tensor_copy(w.slot[k][:], slf[:]))
                dve.sem_inc(slots_done, 1)

                def product(i, u):
                    n = turn(i, u)
                    cw = cols[u % M]
                    dve.wait_ge(s_done, n + 1)
                    after(dve, d_ps, n - 1)
                    v.tensor_tensor(hid[u % 2][0:cw, :], sg[u % 2][0:cw, :], pg[0:cw, u % 2, 1, :], ALU.mult).then_inc(hid_done, 1)
                if layer == 0:
                    staged(dve, NC, (0, product), unroll=2 * M)

            @block.scalar
            def _(act):
                def silu(i, u):
                    n = turn(i, u)
                    cw = cols[u % M]
                    act.wait_ge(g_ps, n + 1)
                    after(act, hid_done, n - 1)
                    nc.scalar.activation(sg[u % 2][0:cw, :], pg[0:cw, u % 2, 0, :], ACT.Silu).then_inc(s_done, 1)

                def out(i, u):
                    if u % M == M - 1:
                        wait_before(act, count, d_ps, turn(i, u) + 1, g_ps)
                        for j in range(4):
                            t = i * TPB + u // M * 4 + j
                            ins = nc.scalar.activation(w.sh[:, bass.ds(t, 1), :].rearrange("p o c -> p (o c)"), pd[:, u // M, j * C:(j + 1) * C],
                                                       ACT.Copy, scale=w.shw[:, bass.ds(t, 1)])
                        ins.then_inc(sh_out, 1)
                count = act.alloc_register(f"shared_count_{layer}")
                if layer == 0:
                    act.wait_ge(q_step, 2)
                    nc.scalar.activation(sc[:], sc[:], ACT.Exp).then_inc(ex_done, 1)
                    nc.scalar.activation(w.shw[:], lg[:, :, NE], ACT.Exp, scale=-1.0).then_inc(ex_done, 1)
                copy_weights(act)
                if layer == 0:
                    staged(act, NC, (0, silu), (2, out), unroll=2 * M)

            @block.tensor
            def _(pe):
                def up(i, u):
                    n, m = turn(i, u), u % M
                    after(pe, hid_done, n - 1)
                    rhs = hT[:, bass.ds(2 * i + u // M, 1), :].rearrange("p o t -> p (o t)")
                    for k in range(2):
                        ins = nc.tensor.matmul(pg[0:cols[m], u % 2, k, :], w.shgu[:, k, m * P:m * P + cols[m]], rhs, start=True, stop=True)
                    ins.then_inc(g_ps, 1)

                def down(i, u):
                    n, m, h = turn(i, u), u % M, u // M
                    pe.wait_ge(hid_done, n + 1)
                    if m == 0:
                        after(pe, sh_out, 2 * i + h - 1)
                    for j in range(4):
                        ins = nc.tensor.matmul(pd[:, h, j * C:(j + 1) * C], hid[u % 2][0:cols[m], j * P:(j + 1) * P],
                                               w.shd[0:cols[m], m, :], start=m == 0 and j == 0, stop=m == M - 1, skip_group_check=True)
                    ins.then_inc(d_ps, 1)
                pe.wait_ge(both_done, 1)
                nc.tensor.matmul(pp[:, 0, 0:NE * NT], w.trib[:], both[:].rearrange("p e t -> p (e t)"), start=True, stop=True)
                nc.tensor.matmul(pp[:, 1, 0:NE * NT], w.onesb[:], both[:].rearrange("p e t -> p (e t)"), start=True, stop=True).then_inc(pre_ps, 1)
                transpose_weights(pe)
                if layer == 0:
                    staged(pe, NC, (0, up), (1, down), unroll=2 * M)

            @block.sync
            def _(sp):
                load_weights(sp)

            @block.gpsimd
            def _(pool):
                pool.wait_ge(slots_done, 1)
                weight = w.h[:, :, C + 1:C + 2].rearrange("p t o -> p (t o)")
                nc.gpsimd.tensor_copy(weight, w.wt[0][:]).then_inc(second, 1)
                pool.wait_ge(second, 1)
                for k in range(2):
                    if k == 1:
                        pool.wait_ge(scattered[0], 16 * NT)
                        index = w.h[:, :, C:C + 1].bitcast(U32)
                        nc.gpsimd.tensor_copy(weight, w.wt[1][:])
                        nc.gpsimd.iota(index, pattern=[[P, NT], [0, 1]], base=TOK, channel_multiplier=1).then_inc(second, 1)
                        pool.wait_ge(second, 2)
                    for t in range(NT):
                        nc.gpsimd.indirect_dma_start(out=d.xg[layer], out_offset=bass.IndirectOffsetOnAxis(ap=w.slot[k][:, t:t + 1], axis=0),
                                                     in_=w.h[:, t, :], in_offset=None).then_inc(scattered[k], 16)
                pool.wait_ge(scattered[1], 16 * NT)


def experts_phase(nc, w, d, layer):
    I = (176, 352)[layer]
    cols = chunks_of(I)
    M = len(cols)
    with ExitStack() as ctx:
        sb = lambda n, s, t=F32: ctx.enter_context(nc.sbuf_tensor(f"{n}_{layer}", s, t))
        ps = lambda n, s, t=F32: ctx.enter_context(nc.psum_tensor(f"{n}_{layer}", s, t))
        sem = lambda n: semaphore_of(nc, ctx, f"{n}_{layer}")
        xt = [sb(f"xt{u}", [P, XW]) for u in range(UN)]
        xT = [sb(f"xT{u}", [P, P]) for u in range(UN)]
        sg = [sb(f"esg{u}", [P, I]) for u in range(2)]
        hid = [sb(f"ehid{u}", [P, I]) for u in range(4)]
        hidT = [sb(f"ehidT{u}", [P, M, P]) for u in range(2)]
        yo = [sb(f"yo{u}", [P, C]) for u in range(UN)]
        place = sb("place", [P, UN], U32)
        pT = ps("epT", [P, ST])
        pg = ps("epg", [P, 2, 2, ST])
        ph = ps("eph", [P, 2, ST])
        pd = ps("epd", [P, ST])
        g_of = lambda u: pg[:, u, 0, 0:I]
        u_of = lambda u: pg[:, u, 1, 0:I]
        x_in = [sem(f"xin{u}") for u in range(UN)]
        y_out = w.y_out[layer]
        sh_gated = sem("sh_gated")
        in_ps, in_T, up_ps, s_done, hid_done, hid_ps, hid_T, dn_ps, y_done = (
            sem("in_ps"), sem("in_T"), sem("up_ps"), sem("s_done"), sem("ehid_done"), sem("hid_ps"), sem("hid_T"), sem("dn_ps"), sem("y_done"))
        const = lambda n: isinstance(n, int)

        def rows_of(a, n):
            v = a.rearrange("(i p) c -> i p c", p=P)
            return v[n] if const(n) else v[bass.ds(n, 1)][0]

        def loop(eng, step):
            for u in range(UN):
                step(u, u)
            with eng.Fori(1, NSLOT // UN) as i:
                for u in range(UN):
                    step(UN * i + u, u)

        def skewed(eng, *stages, begin=lambda i: None, tick=lambda u: None):
            def step(n, u, at):
                tick(at)
                for k, f in stages:
                    if not (const(n) and not 0 <= n + k < NSLOT):
                        f(n + k, (u + k) % UN)
            begin(0)
            for n in range(UN):
                step(n, n, n)
            with eng.Fori(1, NSLOT // UN - 1) as i:
                begin(i)
                for u in range(UN):
                    step(UN * i + u, u, u)
            begin(NSLOT // UN - 1)
            for u in range(UN + LAG):
                step(NSLOT - UN + u, u % UN, u)

        with nc.Block() as block:
            @block.sync
            def _(sp):
                def step(n, u):
                    after(sp, y_done, n - UN + 1)
                    sp.dma_start(xt[u][:], rows_of(d.xg[layer], n)).then_inc(x_in[u], 16)
                loop(sp, step)

            @block.gpsimd
            def _(pool):
                count = pool.alloc_register(f"y_count_{layer}")
                with pool.Fori(0, 3) as i:
                    for t in range(NSLOT // 3):
                        u = t % UN
                        wait_before(pool, count, y_done, NSLOT // 3 * i + t + 1, in_ps)
                        nc.gpsimd.indirect_dma_start(out=d.yk, out_offset=bass.IndirectOffsetOnAxis(ap=place[:, u:u + 1], axis=0),
                                                     in_=yo[u][:], in_offset=None).then_inc(y_out[u], 16)
                for u in range(UN):
                    pool.wait_ge(y_out[u], 16 * (NSLOT // UN))

            @block.scalar
            def _(act):
                def x_copy(n, u):
                    act.wait_ge(in_ps, n + 1)
                    nc.scalar.copy(xT[u][:], pT[:, 0:P]).then_inc(in_T, 1)

                def silu(n, u):
                    act.wait_ge(up_ps, n + 1)
                    nc.scalar.activation(sg[u % 2][:], g_of(u % 2), ACT.Silu).then_inc(s_done, 1)

                def y_copy(n, u):
                    act.wait_ge(dn_ps, n + 1)
                    if not (const(n) and n < UN):
                        act.wait_ge(y_out[u], (16 // UN) * (n - u))
                    nc.scalar.activation(yo[u][:], pd[:, 0:C], ACT.Copy, scale=xt[u][:, C + 1:C + 2]).then_inc(y_done, 1)

                x_copy(0, 0)
                x_copy(1, 1)
                silu(0, 0)
                skewed(act, (2, x_copy), (1, silu), (-LAG, y_copy))

            @block.vector
            def _(dve):
                def product(n, u):
                    dve.wait_ge(s_done, n + 1)
                    nc.vector.tensor_tensor(hid[u % 4][:], sg[u % 2][:], u_of(u % 2), ALU.mult).then_inc(hid_done, 1)

                def hid_copy(n, u):
                    dve.wait_ge(hid_ps, n + 1)
                    if not (const(n) and n < UN):
                        dve.wait_ge(y_out[u], (16 // UN) * (n - u))
                    nc.vector.tensor_copy(place[:, u:u + 1], xt[u][:, C:C + 1].bitcast(U32))
                    if I == 176:
                        ins = nc.vector.tensor_copy(hidT[u % 2][0:88, :, :], ph[0:88, u % 2, 0:M * P].rearrange("p (m c) -> p m c", m=M))
                    else:
                        nc.vector.tensor_copy(hidT[u % 2][:, 0:2, :], ph[:, u % 2, 0:2 * P].rearrange("p (m c) -> p m c", m=2))
                        ins = nc.vector.tensor_copy(hidT[u % 2][0:96, 2, :], ph[0:96, u % 2, 2 * P:3 * P])
                    ins.then_inc(hid_T, 1)

                if layer == 0:
                    for b in range(NB):
                        of_batch = w.sh[:, b * TPB:(b + 1) * TPB, :]
                        ins = nc.vector.tensor_tensor(of_batch, of_batch, w.gate[:, 1, b:b + 1, :].to_broadcast([P, TPB, C]), ALU.mult)
                    ins.then_inc(sh_gated, 1)
                product(0, 0)
                skewed(dve, (1, product), (-1, hid_copy))
                if layer == 0:
                    dve.wait_ge(sh_gated, 1)
                    nc.vector.tensor_tensor(w.x[:], w.x[:], w.sh[:], ALU.add)

            @block.tensor
            def _(pe):
                def t_in(n, u):
                    if const(n):
                        pe.wait_ge(x_in[u], 16 * (n // UN + 1))
                    else:
                        pe.wait_ge(x_in[u], (16 // UN) * (n - u) + 16)
                    after(pe, in_T, n)
                    nc.tensor.transpose(pT[:, 0:P], xt[u][:, 0:C], w.ident[:]).then_inc(in_ps, 1)

                def up(n, u):
                    e = expert(1)
                    pe.wait_ge(in_T, n + 1)
                    after(pe, hid_done, n - 1)
                    wt = w.up[:, bass.ds(e, 1)][:, 0]
                    for k in range(2):
                        rhs = wt[:, 0, k * I:(k + 1) * I] if layer == 0 else wt[:, k, :]
                        ins = nc.tensor.matmul((g_of, u_of)[k](u % 2), xT[u][:], rhs, start=True, stop=True)
                    ins.then_inc(up_ps, 1)
                    return e

                def t_hid(n, u):
                    pe.wait_ge(hid_done, n + 1)
                    after(pe, hid_T, n - 1)
                    c0 = 0
                    for m, cw in enumerate(cols):
                        ins = nc.tensor.transpose(ph[0:cw, u % 2, m * P:(m + 1) * P], hid[u % 4][:, c0:c0 + cw], w.ident[:])
                        c0 += cw
                    ins.then_inc(hid_ps, 1)

                def down(n, u):
                    e = expert(-LAG)
                    pe.wait_ge(hid_T, n + 1)
                    after(pe, y_done, n)
                    wt = w.down[:, bass.ds(e, 1)][:, 0]
                    for m, cw in enumerate(cols):
                        ins = nc.tensor.matmul(pd[:, 0:C], hidT[u % 2][0:cw, m, :], wt[0:cw, m, :], start=m == 0, stop=m == M - 1)
                    ins.then_inc(dn_ps, 1)

                place, words = [0], [None, None]

                def begin(i):
                    for k in range(2):
                        at = w.tile_expert[0:1, i + k:i + k + 1] if const(i) else w.tile_expert[0:1, bass.ds(i + k, 1)]
                        words[k] = pe.value_load(at, min_val=0, max_val=8 ** UN - 1)

                def tick(u):
                    place[0] = u

                def expert(k):
                    at = place[0] + LAG + k
                    return (words[at // UN] >> (3 * (at % UN))) & (NE - 1)
                t_in(0, 0)
                t_in(1, 1)
                begin(0)
                tick(-1)
                up(0, 0)
                skewed(pe, (2, t_in), (1, up), (-1, t_hid), (-LAG, down), begin=begin, tick=tick)


def combine_phase(nc, w, d, layer):
    with ExitStack() as ctx:
        sb = lambda n, s, t=F32: ctx.enter_context(nc.sbuf_tensor(f"{n}_{layer}", s, t))
        sem = lambda n: semaphore_of(nc, ctx, f"{n}_{layer}")
        gat = [[sb(f"gat{k}_{u}", [P, 4, C]) for u in range(4)] for k in range(2)]
        got = [sem(f"got{u}") for u in range(4)]
        c_step, x_done, stored = sem("c_step"), sem("x_done"), sem("stored")
        NSTEP = 3
        with nc.Block() as block:
            @block.scalar
            def _(act):
                for s in range(2 * NB):
                    u = s % 4
                    if s >= 4:
                        act.wait_ge(x_done, s - 3)
                    for k in range(2):
                        at = k * TOK + s * ST
                        act.dma_start(gat[k][u][:], d.yk[at:at + ST, :].rearrange("(j p) c -> p j c", p=P)).then_inc(got[u], 16)

            @block.vector
            def _(dve):
                v = nc.vector
                for s in range(2 * NB):
                    u, b = s % 4, s // 2
                    dve.wait_ge(got[u], 16 * 2 * (s // 4 + 1))
                    link = Chain(dve, c_step, NSTEP * s)
                    a0, a1 = gat[0][u][:], gat[1][u][:]
                    link(v.tensor_tensor(a0, a0, a1, ALU.add))
                    link(v.tensor_tensor(a0, a0, w.gate[:, 2 * layer + 1, b:b + 1, :].to_broadcast([P, 4, C]), ALU.mult))
                    link(v.tensor_tensor(w.x[:, 4 * s:4 * s + 4, :], w.x[:, 4 * s:4 * s + 4, :], a0, ALU.add))
                    dve.sem_inc(x_done, 1)

            @block.sync
            def _(sp):
                if layer == 1:
                    xo = d.out.rearrange("b (n p) c -> p (b n) c", p=P)
                    for s in range(2 * NB):
                        sp.wait_ge(x_done, s + 1)
                        sp.dma_start(xo[:, 4 * s:4 * s + 4, :], w.x[:, 4 * s:4 * s + 4, :]).then_inc(stored, 16)
                    sp.wait_ge(stored, 16 * 2 * NB)


NSTATE = 32
R_, PH_, CR_, CI_, DR_, DI_ = range(6)
CG = P // NSTATE
NG = C // CG
LW = P + 1
GI = 4
TWO_PI = 6.283185
ROUND = 12582912.0


def s4_phase(nc, w, d, m):
    with ExitStack() as whole:
        sb = lambda n, *s: whole.enter_context(nc.sbuf_tensor(n, list(s), F32))
        m.powr = sb("powr", P, 2, NG, LW)
        m.cdiag = sb("cdiag", P, NG, 2, NSTATE)
        m.s_all, m.h_all = sb("s_all", P, NG, 2, NB, TPB), sb("h_all", P, NG, 2, NB, TPB)
        m.h_c = sb("h_c", P, NG, 2, NT)
        m.u_all = w.v[:].rearrange("p a b c -> p (a b c)").rearrange("p (c t) -> p c t", t=NT)
        m.h_keep = w.sh
        s4_input(nc, w, d, m)
        s4_states(nc, w, d, m)
        s4_output(nc, w, d, m)
        s4_gate(nc, w, d, m)


def s4_coefficient_parts(nc, d, m, ctx):
    glub, inb, outb, dskip = m.glub, m.inb, m.outb, m.dskip
    sb = lambda n, s, t=F32: ctx.enter_context(nc.sbuf_tensor(n, s, t))
    ps = lambda n, s, t=F32: ctx.enter_context(nc.psum_tensor(n, s, t))
    sem = lambda n: semaphore_of(nc, ctx, n)
    wsrc = sb("wsrc", [P, 4, C])
    raw = sb("sraw", [P, 3, NSTATE])
    cc = sb("cc", [P, NSTATE, 2])
    ldt = sb("ldt", [P, 1])
    co = sb("co", [P, 6, NSTATE])
    ea = sb("ea", [P, NSTATE])
    tt = sb("tt", [P, 4, NSTATE])
    rn = sb("rn", [P, 4, NSTATE])
    ex = sb("ex", [P, 2, NSTATE])
    zz = sb("zz", [P, 4, NSTATE])
    q = sb("qtmp", [P, 4, NSTATE])
    den = sb("den", [P, NSTATE])
    rowsg = sb("rowsg", [NG, 6, P])
    pw = ps("pw", [P, ST])
    pc = ps("pc", [P, 6 * NG])
    s_in, w_tr, c_step, e_done, z_done, co_out, rows_in, cols_ps = (sem(n) for n in (
        "s_in", "sw_tr", "c_step", "e_done", "z_done", "co_out", "rows_in", "cols_ps4"))
    LOADS = 4 + 3 + 1 + GI + 2 + 2

    def loads(sp):
        srcs = [d.in_W, d.glu_W[0:C], d.glu_W[C:2 * C], d.out_W]
        for k, src in enumerate(srcs):
            sp.dma_start(wsrc[:, k, :], src).then_inc(s_in, 16)
        sp.dma_start(raw[:, 0, :], d.log_A_real).then_inc(s_in, 16)
        sp.dma_start(raw[:, 1, :], d.A_imag).then_inc(s_in, 16)
        sp.dma_start(cc[:], d.C).then_inc(s_in, 16)
        col = lambda a: a.rearrange("(p o) -> p o", o=1)
        with nc.allow_non_contiguous_dma(reason="vectors as columns"):
            sp.dma_start(ldt[:], col(d.log_dt)).then_inc(s_in, 16)
            for g in range(GI):
                sp.dma_start(dskip[g * NSTATE:g * NSTATE + CG, :],
                             d.D_skip.rearrange("(n g c) -> g c n", g=GI, c=CG)[g]).then_inc(s_in, 16)
            for k in range(2):
                sp.dma_start(glub[:, k:k + 1], col(d.glu_b[k * C:(k + 1) * C])).then_inc(s_in, 16)
        sp.dma_start(inb[:], d.in_b.rearrange("(o c) -> o c", o=1).to_broadcast([P, C])).then_inc(s_in, 16)
        sp.dma_start(outb[:], d.out_b.rearrange("(o c) -> o c", o=1).to_broadcast([P, C])).then_inc(s_in, 16)
        sp.wait_ge(z_done, 1)
        sp.dma_start(d.coef.rearrange("a (h n) -> h a n", n=NSTATE), co[:]).then_inc(co_out, 16)
        sp.wait_ge(co_out, 16)
        sp.dma_start(rowsg[:], d.coef.rearrange("a (g p) -> g a p", p=P)).then_inc(rows_in, 16)

    def transposes(pe):
        pe.wait_ge(s_in, 16 * LOADS)
        for k in range(4):
            ins = nc.tensor.transpose(pw[:, k * C:(k + 1) * C], wsrc[:, k, :], m.ident[:])
        ins.then_inc(w_tr, 1)
        pe.wait_ge(rows_in, 16)
        for a in range(6):
            ins = nc.tensor.transpose(pc[:, a * NG:(a + 1) * NG], rowsg[:, a, :], m.ident[0:NG, 0:NG])
        ins.then_inc(cols_ps, 1)

    def exponentials(act):
        act.wait_ge(s_in, 16 * LOADS)
        nc.scalar.activation(ldt[:], ldt[:], ACT.Exp).then_inc(e_done, 1)
        nc.scalar.activation(ea[:], raw[:, 0, :], ACT.Exp).then_inc(e_done, 1)
        act.wait_ge(c_step, 1)
        nc.scalar.activation(ex[:, 0, :], co[:, R_, :], ACT.Exp)
        nc.scalar.activation(ex[:, 1, :], co[:, R_, :], ACT.Exp, scale=float(P)).then_inc(e_done, 1)
        act.wait_ge(c_step, 5)
        nc.scalar.activation(zz[:], tt[:], ACT.Sin, scale=TWO_PI).then_inc(e_done, 1)

    def coefficients(dve):
        v = nc.vector
        link = Chain(dve, c_step)
        dve.wait_ge(e_done, 2)
        link(v.tensor_scalar(co[:, R_, :], ea[:], ldt[:], -1.0, ALU.mult, ALU.mult))
        link(v.tensor_scalar(co[:, PH_, :], raw[:, 1, :], ldt[:], 1.0 / (2.0 * np.pi), ALU.mult, ALU.mult))
        v.tensor_copy(tt[:, 0, :], co[:, PH_, :])
        v.tensor_scalar(tt[:, 1, :], co[:, PH_, :], 0.25, None, ALU.add)
        v.tensor_scalar(tt[:, 2, :], co[:, PH_, :], float(P), None, ALU.mult)
        link(v.tensor_scalar(tt[:, 3, :], co[:, PH_, :], float(P), 0.25, ALU.mult, ALU.add))
        link(v.tensor_scalar(rn[:], tt[:], ROUND, ROUND, ALU.add, ALU.subtract))
        link(v.tensor_tensor(tt[:], tt[:], rn[:], ALU.subtract))
        dve.wait_ge(e_done, 4)
        v.tensor_tensor(zz[:, 0:2, :], zz[:, 0:2, :], ex[:, 0:1, :].to_broadcast([P, 2, NSTATE]), ALU.mult)
        v.tensor_tensor(co[:, DI_, :], zz[:, 2, :], ex[:, 1, :], ALU.mult)
        v.tensor_tensor(co[:, DR_, :], zz[:, 3, :], ex[:, 1, :], ALU.mult)
        v.tensor_tensor(den[:], ea[:], ea[:], ALU.mult)
        link(v.tensor_tensor(q[:, 0, :], raw[:, 1, :], raw[:, 1, :], ALU.mult))
        link(v.tensor_tensor(den[:], den[:], q[:, 0, :], ALU.add))
        v.reciprocal(den[:], den[:])
        link(v.tensor_scalar(zz[:, 1, :], zz[:, 1, :], -1.0, None, ALU.add))
        def cmul(o_r, o_i, a_r, a_i, b_r, b_i):
            v.tensor_tensor(q[:, 0, :], a_r, b_r, ALU.mult)
            v.tensor_tensor(q[:, 1, :], a_i, b_i, ALU.mult)
            v.tensor_tensor(q[:, 2, :], a_r, b_i, ALU.mult)
            link(v.tensor_tensor(q[:, 3, :], a_i, b_r, ALU.mult))
            v.tensor_tensor(o_r, q[:, 0, :], q[:, 1, :], ALU.subtract)
            link(v.tensor_tensor(o_i, q[:, 2, :], q[:, 3, :], ALU.add))
        cmul(co[:, CR_, :], co[:, CI_, :], cc[:, :, 0], cc[:, :, 1], zz[:, 1, :], zz[:, 0, :])
        v.tensor_scalar(zz[:, 2, :], ea[:], -1.0, None, ALU.mult)
        link(v.tensor_scalar(zz[:, 3, :], raw[:, 1, :], -1.0, None, ALU.mult))
        cmul(zz[:, 0, :], zz[:, 1, :], co[:, CR_, :], co[:, CI_, :], zz[:, 2, :], zz[:, 3, :])
        link(v.tensor_scalar(den[:], den[:], 2.0, None, ALU.mult))
        v.tensor_tensor(co[:, CR_, :], zz[:, 0, :], den[:], ALU.mult)
        v.tensor_tensor(co[:, CI_, :], zz[:, 1, :], den[:], ALU.mult).then_inc(z_done, 1)

    def results(dve):
        v = nc.vector
        dve.wait_ge(w_tr, 1)
        v.tensor_copy(m.inT[:], pw[:, 0:C])
        v.tensor_copy(m.gluT[:], pw[:, C:3 * C].rearrange("p (a c) -> p a c", a=2))
        v.tensor_copy(m.outT[:], pw[:, 3 * C:4 * C])
        dve.wait_ge(cols_ps, 1)
        v.tensor_copy(m.cols[:], pc[:].rearrange("p (a g) -> p a g", a=6))
    return loads, transposes, exponentials, coefficients, results


def s4_input(nc, w, d, m):
    powr, cols, cdiag = m.powr, m.cols, m.cdiag
    inT, inb, u_all, h_keep = m.inT, m.inb, m.u_all, m.h_keep
    with ExitStack() as ctx:
        sb = lambda n, s, t=F32: ctx.enter_context(nc.sbuf_tensor(n, s, t))
        ps = lambda n, s, t=F32: ctx.enter_context(nc.psum_tensor(n, s, t))
        sem = lambda n: semaphore_of(nc, ctx, n)
        hs = [sb(f"shs{u}", [P, 4, C]) for u in range(2)]
        hT = [sb(f"shT{u}", [P, ST]) for u in range(2)]
        pT = ps("spT", [P, 2, ST])
        pu = ps("spu", [P, 2, ST])
        i_step, h_done, h_kept, tr_done, hT_done, u_ps, u_out = (sem(n) for n in (
            "i_step", "sh_done", "sh_kept", "str_done", "shT_done", "u_ps", "u_out"))
        rnd, mag = sb("rnd", [P, NG, LW]), sb("smag", [P, NG, LW])
        half_pi = sb("half_pi", [P, 1])
        p_step, r_done, m_done, sin_done = (sem(n) for n in ("p_step", "r_done", "m_done", "ssin_done"))
        by_l = w.iota[:, 0:LW].rearrange("p (o l) -> p o l", o=1).to_broadcast([P, NG, LW])
        by_g = lambda a: cols[:, a, :].rearrange("p (g o) -> p g o", o=1).to_broadcast([P, NG, LW])
        with nc.Block() as block:
            @block.vector
            def _(dve):
                v = nc.vector
                step = Chain(dve, p_step)
                v.memset(half_pi[:], np.pi / 2)
                step(v.tensor_tensor(powr[:, 1], by_l, by_g(PH_), ALU.mult))
                step(v.tensor_scalar(rnd[:], powr[:, 1], ROUND, ROUND, ALU.add, ALU.subtract))
                step(v.tensor_tensor(powr[:, 1], powr[:, 1], rnd[:], ALU.subtract))
                v.scalar_tensor_tensor(out=powr[:, 0], in0=powr[:, 1], scalar=-1.0, in1=powr[:, 1], op0=ALU.mult, op1=ALU.max).then_inc(p_step, 1)

                def rows(b, u):
                    s = 2 * b + u
                    after(dve, tr_done, s - 1)
                    after(dve, h_kept, s - 1)
                    link = Chain(dve, i_step, 2 * s)
                    for j in range(4):
                        t = b * TPB + u * 4 + j
                        ins = nc.vector.tensor_scalar(hs[u][:, j, :], w.x[:, t, :], w.mean[:, bass.ds(t, 1)],
                                                      w.rstd[:, bass.ds(t, 1)], ALU.subtract, ALU.mult)
                    link(ins)
                    link(nc.vector.tensor_tensor(hs[u][:], hs[u][:], w.moda[:, 1, bass.ds(b, 1), :].to_broadcast([P, 4, C]), ALU.mult))
                    nc.vector.tensor_tensor(hs[u][:], hs[u][:], w.moda[:, 0, bass.ds(b, 1), :].to_broadcast([P, 4, C]), ALU.add).then_inc(h_done, 1)

                def project(b, u):
                    dve.wait_ge(u_ps, 2 * b + u + 1)
                    dst = u_all.rearrange("p c t -> p t c")[:, bass.ds(b * TPB + u * 4, 4), :]
                    nc.vector.tensor_tensor(dst, pu[:, u, :].rearrange("p (j c) -> p j c", j=4),
                                            inb[:].rearrange("p (o c) -> p o c", o=1).to_broadcast([P, 4, C]), ALU.add).then_inc(u_out, 1)
                staged(dve, 2 * NB, (0, rows), (2, project))
                v.memset(cdiag[:], 0.0).then_inc(p_step, 1)
                dve.wait_ge(p_step, 5)
                for h in range(CG):
                    r = slice(h * NSTATE, (h + 1) * NSTATE)
                    v.tensor_copy(cdiag[r, :, 0, h], cols[r, CR_, :])
                    v.tensor_scalar(cdiag[r, :, 1, h], cols[r, CI_, :], -1.0, None, ALU.mult)
                dve.wait_ge(m_done, 1)
                dve.wait_ge(sin_done, 1)
                v.tensor_tensor(powr[:, 1], powr[:, 1], mag[:], ALU.mult)

            @block.gpsimd
            def _(pool):
                def keep(b, u):
                    pool.wait_ge(h_done, 2 * b + u + 1)
                    nc.gpsimd.tensor_copy(h_keep[:, bass.ds(b * TPB + u * 4, 4), :], hs[u][:]).then_inc(h_kept, 1)
                nc.gpsimd.tensor_tensor(mag[:], by_l, by_g(R_), ALU.mult).then_inc(r_done, 1)
                staged(pool, 2 * NB, (0, keep))
                pool.wait_ge(m_done, 1)
                pool.wait_ge(sin_done, 2)
                nc.gpsimd.tensor_tensor(powr[:, 0], powr[:, 0], mag[:], ALU.mult)

            @block.scalar
            def _(act):
                act.wait_ge(r_done, 1)
                nc.scalar.activation(mag[:], mag[:], ACT.Exp).then_inc(m_done, 1)
                act.wait_ge(p_step, 4)
                nc.scalar.activation(powr[:, 1], powr[:, 1], ACT.Sin, scale=TWO_PI).then_inc(sin_done, 1)
                nc.scalar.activation(powr[:, 0], powr[:, 0], ACT.Sin, scale=-TWO_PI, bias=half_pi[:]).then_inc(sin_done, 1)

                def transposed(b, u):
                    s = 2 * b + u
                    act.wait_ge(tr_done, s + 1)
                    after(act, u_ps, s - 1)
                    nc.scalar.copy(hT[u][:], pT[:, u, :]).then_inc(hT_done, 1)
                staged(act, 2 * NB, (0, transposed))

            @block.tensor
            def _(pe):
                def transpose(b, u):
                    s = 2 * b + u
                    pe.wait_ge(h_done, s + 1)
                    after(pe, hT_done, s - 1)
                    for j in range(4):
                        ins = nc.tensor.matmul(pT[:, u, j * C:(j + 1) * C], hs[u][:, j, :], w.flip[:], start=True, stop=True)
                    ins.then_inc(tr_done, 1)

                def project(b, u):
                    s = 2 * b + u
                    pe.wait_ge(hT_done, s + 1)
                    after(pe, u_out, s - 1)
                    for j in range(4):
                        ins = nc.tensor.matmul(pu[:, u, j * C:(j + 1) * C], hT[u][:, j * C:(j + 1) * C], inT[:], start=True, stop=True)
                    ins.then_inc(u_ps, 1)
                staged(pe, 2 * NB, (2, project), (0, transpose))


def s4_states(nc, w, d, m):
    powr, s_all, h_all, h_c, cdiag, u_all, cols, dskip = m.powr, m.s_all, m.h_all, m.h_c, m.cdiag, m.u_all, m.cols, m.dskip
    with ExitStack() as ctx:
        sb = lambda n, s, t=F32: ctx.enter_context(nc.sbuf_tensor(n, s, t))
        ps = lambda n, s, t=F32: ctx.enter_context(nc.psum_tensor(n, s, t))
        sem = lambda n: semaphore_of(nc, ctx, n)
        wr = [sb(f"wr{u}", [P, 2, GI, LW]) for u in range(4)]
        vr = [sb(f"vr{u}", [P, 2, GI, P]) for u in range(2)]
        cd = [sb(f"cd{u}", [P, GI, 2, NSTATE]) for u in range(2)]
        k_all = sb("k_all", [P, NG // GI, P])
        zk = sb("zk", [P, P])
        q = sb("hq", [P, 2, NG, 2, NB])
        qc = sb("hqc", [P, 4, NG, NT])
        pv = ps("spv", [P, 2, ST])
        pS = ps("sps4", [P, 4, ST])
        pk = ps("spk", [P, 2, ST])
        w_in = [sem(f"sw_in{u}") for u in range(4)]
        h_step = sem("h_step4")
        v_ps, v_out, s_ps, s_out, r_step, cd_in, k_done, k_stored, k_ps = (sem(n) for n in (
            "v_ps4", "v_out4", "s_ps4", "s_out4", "r_step4", "cd_in", "k_done", "k_stored", "k_ps"))
        NI = NG // GI
        with nc.Block() as block:
            @block.gpsimd
            def _(pool):
                h, x = m.h_keep, w.x
                nc.gpsimd.tensor_tensor(h[:], h[:], m.outb[:].rearrange("p (o c) -> p o c", o=1).to_broadcast([P, NT, C]),
                                        ALU.add).then_inc(h_step, 1)
                pool.wait_ge(h_step, 1)
                for b in range(NB):
                    hb = h[:, b * TPB:(b + 1) * TPB, :]
                    nc.gpsimd.tensor_tensor(hb, hb, w.gate[:, 2, b:b + 1, :].to_broadcast([P, TPB, C]), ALU.mult).then_inc(h_step, 1)
                pool.wait_ge(h_step, 1 + NB)
                nc.gpsimd.tensor_tensor(x[:], x[:], h[:], ALU.add)

            @block.sync
            def _(sp):
                def powers(i, u):
                    n = 4 * i + u
                    after(sp, k_ps, n - 3)
                    sp.dma_start(wr[u][:], powr[:, :, bass.ds(n * GI, GI), :]).then_inc(w_in[u], 16)
                staged(sp, NI, (0, powers), unroll=4)
                sp.wait_ge(k_done, 1)
                sp.dma_start(d.kpad[:, 0:P], zk[:]).then_inc(k_stored, 16)
                for g in range(GI):
                    sp.dma_start(d.kpad.rearrange("(n g c) l -> g c n l", g=GI, c=CG)[g, :, :, P:2 * P],
                                 k_all[g * NSTATE:g * NSTATE + CG, :, :]).then_inc(k_stored, 16)
                sp.wait_ge(k_stored, 16 * (1 + GI))

            @block.scalar
            def _(act):
                def powers_out(i, u):
                    n = 4 * i + u
                    act.wait_ge(v_ps, n + 1)
                    after(act, s_ps, n - 1)
                    for a in range(2):
                        ins = nc.scalar.copy(vr[u % 2][:, a], pv[:, a, :].rearrange("p (g l) -> p g l", g=GI))
                    ins.then_inc(v_out, 1)
                staged(act, NI, (0, powers_out), unroll=4)

            @block.tensor
            def _(pe):
                def transpose(i, u):
                    n = 4 * i + u
                    pe.wait_ge(w_in[u], 16 * i + 16)
                    after(pe, v_out, n)
                    for a in range(2):
                        for g in range(GI):
                            ins = nc.tensor.transpose(pv[:, a, g * P:(g + 1) * P], wr[u][:, a, g, 0:P], w.ident[:])
                    ins.then_inc(v_ps, 1)

                def states(i, u):
                    n = 4 * i + u
                    after(pe, s_out, n - 1)
                    pe.wait_ge(cd_in, n + 1)
                    for a in range(2):
                        for g in range(GI):
                            ins = nc.tensor.matmul(pk[g * NSTATE:(g + 1) * NSTATE, u % 2, 0:P], cd[u % 2][:, g, a, :], wr[u][:, a, g, 0:P],
                                                   start=a == 0, stop=a == 1, skip_group_check=True, tile_position=(0, g * NSTATE))
                    ins.then_inc(k_ps, 1)
                    pe.wait_ge(v_out, n + 1)
                    for a in range(2):
                        for g in range(GI):
                            ins = nc.tensor.matmul(pS[:, 2 * (u % 2) + a, g * P:(g + 1) * P], vr[u % 2][:, a, g, :],
                                                   u_all[:, bass.ds((n * GI + g) * CG, CG), :].rearrange("p c t -> p (c t)"),
                                                   start=True, stop=True)
                    ins.then_inc(s_ps, 1)
                staged(pe, NI, (0, transpose), (1, states), unroll=4)

            @block.vector
            def _(dve):
                v = nc.vector
                def states_out(i, u):
                    n = 4 * i + u
                    dve.wait_ge(s_ps, n + 1)
                    v.tensor_copy(k_all[:, bass.ds(n, 1), :].rearrange("p o l -> p (o l)"), pk[:, u % 2, 0:P])
                    for h in range(CG):
                        r = slice(h * NSTATE, (h + 1) * NSTATE)
                        src = pS[r, 2 * (u % 2):2 * (u % 2) + 2, :].rearrange("p a (g c t) -> p a g c t", g=GI, c=CG)[:, :, :, h, :]
                        dst = s_all[:].rearrange("p g a b t -> p a g (b t)")[r, :, bass.ds(n * GI, GI), :]
                        ins = v.tensor_copy(dst, src)
                    ins.then_inc(s_out, 1)

                def coefficients(i, u):
                    n = 4 * i + u
                    after(dve, k_ps, n - 1)
                    v.tensor_copy(cd[u % 2][:], cdiag[:, bass.ds(n * GI, GI), :, :]).then_inc(cd_in, 1)
                staged(dve, NI, (0, coefficients), (1, states_out), unroll=4)
                dve.wait_ge(s_out, NI)
                link = Chain(dve, r_step)
                for g in range(GI):
                    r = slice(g * NSTATE, g * NSTATE + CG)
                    v.tensor_tensor(k_all[r, :, 0], k_all[r, :, 0], dskip[r, :], ALU.add)
                v.memset(zk[:], 0.0).then_inc(k_done, 1)
                link(v.memset(h_all[:, :, :, :, 0], 0.0))
                for t in range(1, TPB):
                    hp = h_all[:, :, :, :, t - 1]
                    for k, a in enumerate((DR_, DI_)):
                        cb = cols[:, a, :].rearrange("p (g o) -> p g o", o=1).to_broadcast([P, NG, 2 * NB])
                        ins = v.tensor_tensor(q[:, k].rearrange("p g a b -> p g (a b)"), hp.rearrange("p g a b -> p g (a b)"), cb, ALU.mult)
                    link(ins)
                    link(v.tensor_tensor(q[:, 0], q[:, 0], s_all[:, :, :, :, t - 1], ALU.add))
                    v.tensor_tensor(h_all[:, :, 0, :, t], q[:, 0, :, 0, :], q[:, 1, :, 1, :], ALU.subtract)
                    link(v.tensor_tensor(h_all[:, :, 1, :, t], q[:, 0, :, 1, :], q[:, 1, :, 0, :], ALU.add))
                hr, hi = (h_all[:, :, a, :, :].rearrange("p g b t -> p g (b t)") for a in range(2))
                cb = lambda a: cols[:, a, :].rearrange("p (g o) -> p g o", o=1).to_broadcast([P, NG, NT])
                v.tensor_tensor(qc[:, 0], hr, cb(CR_), ALU.mult)
                v.tensor_tensor(qc[:, 1], hi, cb(CI_), ALU.mult)
                v.tensor_tensor(qc[:, 2], hr, cb(CI_), ALU.mult)
                link(v.tensor_tensor(qc[:, 3], hi, cb(CR_), ALU.mult))
                v.tensor_tensor(h_c[:, :, 0, :], qc[:, 0], qc[:, 1], ALU.subtract)
                v.scalar_tensor_tensor(out=h_c[:, :, 1, :], in0=qc[:, 2], scalar=-1.0, in1=qc[:, 3], op0=ALU.mult, op1=ALU.subtract)


def s4_output(nc, w, d, m):
    powr, h_c, u_all = m.powr, m.h_c, m.u_all
    NI = NG // GI
    CI = GI * CG
    with ExitStack() as ctx:
        sb = lambda n, s, t=F32: ctx.enter_context(nc.sbuf_tensor(n, s, t))
        ps = lambda n, s, t=F32: ctx.enter_context(nc.psum_tensor(n, s, t))
        sem = lambda n: semaphore_of(nc, ctx, n)
        tz = [sb(f"tz{u}", [P, CI, P]) for u in range(2)]
        hd = [sb(f"hd{u}", [P, GI, 2, CG, NT]) for u in range(2)]
        us = [sb(f"us{u}", [P, CI, NT]) for u in range(2)]
        yl = [sb(f"yl{u}", [P, GI, P]) for u in range(2)]
        py = ps("py", [P, 2, ST])
        k_in, y_st = [sem(f"k_in{u}") for u in range(2)], [sem(f"y_st{u}") for u in range(2)]
        z_set, in_done, y_ps, y_out = sem("z_set"), sem("in_done"), sem("y_ps"), sem("y_out4")
        with nc.Block() as block:
            @block.sync
            def _(sp):
                def load(i, u):
                    n = 2 * i + u
                    after(sp, y_ps, n - 1)
                    src = bass.AP(d.kpad.tensor, n * (CI * 2 * P) + 1, [[1, P], [2 * P, CI], [1, P]])
                    sp.dma_start(tz[u][:], src).then_inc(k_in[u], 16)
                staged(sp, NI, (0, load))
                for u in range(2):
                    sp.wait_ge(y_st[u], 16 * (NI // 2))

            @block.vector
            def _(dve):
                for u in range(2):
                    ins = nc.vector.memset(hd[u][:], 0.0)
                ins.then_inc(z_set, 1)
                dve.wait_ge(z_set, 1)

                def operands(i, u):
                    n = 2 * i + u
                    after(dve, y_ps, n - 1)
                    for h in range(CG):
                        r = slice(h * NSTATE, (h + 1) * NSTATE)
                        nc.vector.tensor_copy(hd[u][r, :, :, h, :], h_c[r, bass.ds(n * GI, GI), :, :])
                    nc.vector.tensor_copy(us[u][:], u_all[:, bass.ds(n * CI, CI), :]).then_inc(in_done, 1)
                staged(dve, NI, (0, operands))

            @block.tensor
            def _(pe):
                def convolve(i, u):
                    n = 2 * i + u
                    pe.wait_ge(in_done, n + 1)
                    after(pe, y_out, n - 1)
                    for g in range(GI):
                        for a in range(2):
                            nc.tensor.matmul(py[:, u, g * P:(g + 1) * P], hd[u][:, g, a].rearrange("p c t -> p (c t)"),
                                             powr[:, a, bass.ds(n * GI + g, 1), 1:LW].rearrange("p o l -> p (o l)"),
                                             start=g == 0 and a == 0, stop=False, skip_group_check=True)
                    pe.wait_ge(k_in[u], 16 * i + 16)
                    for g in range(GI):
                        for c in range(CG):
                            ins = nc.tensor.matmul(py[c * NT:(c + 1) * NT, u, g * P:(g + 1) * P], us[u][:, g * CG + c, :],
                                                   tz[u][:, g * CG + c, :], start=False, stop=True, skip_group_check=True,
                                                   tile_position=(0, c * NT))
                    ins.then_inc(y_ps, 1)
                staged(pe, NI, (0, convolve))

            @block.scalar
            def _(act):
                def gelu(i, u):
                    n = 2 * i + u
                    act.wait_ge(y_ps, n + 1)
                    after(act, y_st[u], 16 * i)
                    nc.scalar.activation(yl[u][:], py[:, u, :].rearrange("p (g l) -> p g l", g=GI), ACT.Gelu).then_inc(y_out, 1)

                def store(i, u):
                    n = 2 * i + u
                    act.wait_ge(y_out, n + 1)
                    dst = bass.AP(d.yt.tensor, n * (CI * TOK), [[P, P], [CG * TOK, GI], [1, P]])
                    act.dma_start(dst, yl[u][:]).then_inc(y_st[u], 16)
                staged(act, NI, (0, gelu), (0, store))


def s4_gate(nc, w, d, m):
    gluT, glub, outT = m.gluT, m.glub, m.outT
    with ExitStack() as ctx:
        sb = lambda n, s, t=F32: ctx.enter_context(nc.sbuf_tensor(n, s, t))
        ps = lambda n, s, t=F32: ctx.enter_context(nc.psum_tensor(n, s, t))
        sem = lambda n: semaphore_of(nc, ctx, n)
        yT = [sb(f"gyT{u}", [P, ST]) for u in range(2)]
        sig = [sb(f"gsig{u}", [P, ST]) for u in range(2)]
        y2 = [sb(f"gy2{u}", [P, ST]) for u in range(2)]
        o = [sb(f"go{u}", [P, 4, C]) for u in range(2)]
        pz = ps("gpz", [P, 4, ST])
        po = ps("gpo", [P, 2, ST])
        y_in = [sem(f"gy_in{u}") for u in range(2)]
        z_ps, sg_done, y2_done, o_ps, o_step, x_done = (sem("g" + n) for n in ("z_ps", "sg_done", "y2_done", "o_ps", "o_step", "x_done"))
        with nc.Block() as block:
            @block.sync
            def _(sp):
                def load(b, u):
                    s = 2 * b + u
                    after(sp, z_ps, s - 1)
                    sp.dma_start(yT[u][:], d.yt[:, bass.ds(s * ST, ST)]).then_inc(y_in[u], 16)
                staged(sp, 2 * NB, (0, load))

            @block.tensor
            def _(pe):
                def gates(b, u):
                    s = 2 * b + u
                    pe.wait_ge(y_in[u], 16 * b + 16)
                    after(pe, y2_done, s - 1)
                    for k in range(2):
                        ins = nc.tensor.matmul(pz[:, 2 * u + k, :], gluT[:, k, :], yT[u][:], start=True, stop=True)
                    ins.then_inc(z_ps, 1)

                def project(b, u):
                    s = 2 * b + u
                    pe.wait_ge(y2_done, s + 1)
                    after(pe, o_step, s)
                    for j in range(4):
                        ins = nc.tensor.matmul(po[:, u, j * C:(j + 1) * C], y2[u][:, j * C:(j + 1) * C], outT[:], start=True, stop=True)
                    ins.then_inc(o_ps, 1)
                staged(pe, 2 * NB, (0, gates), (1, project))

            @block.scalar
            def _(act):
                def sigmoid(b, u):
                    s = 2 * b + u
                    act.wait_ge(z_ps, s + 1)
                    after(act, y2_done, s - 1)
                    nc.scalar.activation(sig[u][:], pz[:, 2 * u + 1, :], ACT.Sigmoid, bias=glub[:, 1:2]).then_inc(sg_done, 1)
                staged(act, 2 * NB, (0, sigmoid))

            @block.vector
            def _(dve):
                v = nc.vector

                def gated(b, u):
                    s = 2 * b + u
                    dve.wait_ge(sg_done, s + 1)
                    after(dve, o_ps, s - 1)
                    v.scalar_tensor_tensor(out=y2[u][:], in0=pz[:, 2 * u, :], scalar=glub[:, 0:1], in1=sig[u][:],
                                           op0=ALU.add, op1=ALU.mult).then_inc(y2_done, 1)

                def residual(b, u):
                    s = 2 * b + u
                    dve.wait_ge(o_ps, s + 1)
                    link = Chain(dve, o_step, s)
                    link(v.tensor_tensor(o[u][:], po[:, u, :].rearrange("p (j c) -> p j c", j=4),
                                         w.gate[:, 2, bass.ds(b, 1), :].to_broadcast([P, 4, C]), ALU.mult))
                    xs = w.x[:, bass.ds(b * TPB + u * 4, 4), :]
                    v.tensor_tensor(xs, xs, o[u][:], ALU.add).then_inc(x_done, 1)
                staged(dve, 2 * NB, (0, gated), (1, residual))


def program(nc, d):
    d.qk = nc.dram_tensor("qk", [2, NB, 3, C, T], BF16, kind="Internal").ap()
    d.xg = [nc.dram_tensor(f"xg{layer}", [NSLOT * P, XW], F32, kind="Internal").ap() for layer in range(2)]
    d.yk = nc.dram_tensor("yk", [2 * TOK + NSLOT * P, C], F32, kind="Internal").ap()
    d.coef = nc.dram_tensor("coef", [6, C * NSTATE], F32, kind="Internal").ap()
    d.yt = nc.dram_tensor("yt", [C, TOK], F32, kind="Internal").ap()
    d.kpad = nc.dram_tensor("kpad", [C, 2 * P], F32, kind="Internal").ap()

    w = Work()
    with ExitStack() as ctx:
        sb = lambda n, shape, t=F32: ctx.enter_context(nc.sbuf_tensor(n, shape, t))
        w.x = sb("x", [P, NT, C])
        w.y = sb("y", [P, NQUAD, TPB, 32])
        w.v = sb("v", [P, NQUAD, TPB, 32])
        w.ident, w.flip = sb("ident", [P, P]), sb("flip", [P, P])
        w.identb, w.trib, w.onesb = (sb(n, [P, P], BF16) for n in ("identb", "trib", "onesb"))
        w.iota, w.octal = sb("iota", [P, P + 1]), sb("octal", [P, UN])
        w.bnst = sb("bnst", [P, NT, 6])
        w.mean, w.rstd, w.t0, w.t1 = (sb(n, [P, NT]) for n in ("mean", "rstd", "t0", "t1"))
        w.mod = sb("mod", [P, 2, 6, NB])
        w.gate, w.modr = sb("gate", [P, 4, NB, C]), sb("modr", [P, 4, NB, C])
        w.moda = sb("moda", [P, 2, NB, C])
        w.wo, w.bo = sb("wo", [P, C]), sb("bo", [P, C])
        w.maskb = sb("maskb", [P, P], BF16)
        w.scattered = [[ctx.enter_context(nc.semaphore(f"scattered{k}_{layer}")) for k in range(2)] for layer in range(2)]
        w.y_out = [[ctx.enter_context(nc.semaphore(f"tile_out{u}_{layer}")) for u in range(UN)] for layer in range(2)]
        w.sh = w.y[:].rearrange("p a b c -> p (a b c)").rearrange("p (t c) -> p t c", c=C)
        m = Work()
        m.ident = w.ident
        m.inT, m.gluT, m.outT = sb("inT", [P, C]), sb("gluT", [P, 2, C]), sb("outT", [P, C])
        m.glub, m.inb, m.outb = sb("glub", [P, 2]), sb("inb", [P, C]), sb("outb", [P, C])
        m.dskip = sb("dskip", [P, NG // GI])
        m.cols = sb("cols", [P, 6, NG])
        operands = ExitStack()
        w.operands = operands.enter_context(nc.sbuf_tensor("operands", [P, 4, HQ, T], BF16))
        with ExitStack() as first:
            sf = lambda n, shape, t=F32: first.enter_context(nc.sbuf_tensor(n, shape, t))
            w.wqkv, w.wqk = sf("wqkv", [P, 3 * C]), sf("wqk", [P, 4, C])
            w.bqk, w.bv = sf("bqk", [P, 4]), sf("bv", [P, C])
            w.rope = sf("rope", [P, 2, T])
            w.empty, w.empty_out = sf("empty", [P, NSLOT, XW]), semaphore_of(nc, first, "empty_out")
            setup_phase(nc, w, d, m)
            qkv_phase(nc, w, d)
        attention_phase(nc, w, d)
        operands.close()
        project_phase(nc, w, d)
        w.wt, w.slot = [sb(f"wt{k}", [P, NT]) for k in range(2)], [sb(f"slot{k}", [P, NT], U32) for k in range(2)]
        w.shw = sb("shw", [P, NT])
        w.tile_expert = sb("tile_expert", [P, NSLOT // UN + 1], mybir.dt.int32)
        for layer in range(2):
            if layer == 1:
                stats_phase(nc, w, "c")
                s4_phase(nc, w, d, m)
            with ExitStack() as own:
                so = lambda n, shape: own.enter_context(nc.sbuf_tensor(f"{n}{layer}", shape, F32))
                w.up = so("up", [P, NE, layer + 1, 352])
                w.down = so("down", [P, NE, (2, 3)[layer], C])
                w.h = so("h", [P, NT, XW])
                w.rt = so("rt", [P, (NE + 1, NE)[layer]])
                if layer == 0:
                    w.shgu, w.shd = so("shgu", [P, 2, SI]), so("shd", [P, 3, C])
                stats_phase(nc, w, "bd"[layer], d, layer)
                route_phase(nc, w, d, layer)
                experts_phase(nc, w, d, layer)
                combine_phase(nc, w, d, layer)


_INPUTS = {
    "x": "L0_attn_x", "w_attn": "L0_attn_W_attn", "b_attn": "L0_attn_b_attn", "w_proj": "L0_attn_W_proj", "b_proj": "L0_attn_b_proj",
    "gate_w": "L0_ffn_gate_w", "gu0": "L0_ffn_experts_gate_up", "dn0": "L0_ffn_experts_down", "sg": "L0_ffn_shared_gate_w",
    "su": "L0_ffn_shared_up_w", "sd": "L0_ffn_shared_down_w", "seg": "L0_ffn_shared_expert_gate_w", "c0": "L0_c", "wmod0": "L0_wmod",
    "in_W": "L1_attn_in_W", "in_b": "L1_attn_in_b", "log_dt": "L1_attn_log_dt", "C": "L1_attn_C", "log_A_real": "L1_attn_log_A_real",
    "A_imag": "L1_attn_A_imag", "D_skip": "L1_attn_D_skip", "glu_W": "L1_attn_glu_W", "glu_b": "L1_attn_glu_b",
    "out_W": "L1_attn_out_W", "out_b": "L1_attn_out_b", "wg": "L1_ffn_Wg", "w1": "L1_ffn_W1", "w2": "L1_ffn_W2", "w3": "L1_ffn_W3",
    "c1": "L1_c", "wmod1": "L1_wmod",
}


def _constants():
    bf16 = mybir.dt.np(BF16)
    at = np.arange(P)
    pos = np.arange(T, dtype=np.float32)
    timescale = np.float32(1250) ** (2.0 * np.arange(HD // 2, dtype=np.float32) / HD)
    angle = (pos[None, :] / timescale[:, None]).astype(np.float32)[at // HQ % (HD // 2)]
    return {
        "rope": np.stack([np.cos(angle), np.sin(angle)], 1).astype(np.float32),
        "ident": np.eye(P, dtype=np.float32),
        "flip": np.ascontiguousarray(np.eye(P, dtype=np.float32)[::-1]),
        "identb": np.eye(P).astype(bf16),
        "maskb": np.where(at[None, :] > at[:, None], NEG, 0).astype(bf16),
        "trib": (at[:, None] < at[None, :]).astype(bf16),
        "onesb": np.ones((P, P), bf16),
        "octal": np.tile(8.0 ** np.arange(UN, dtype=np.float32), (P, 1)).astype(np.float32),
        "iota": np.tile(np.arange(P + 1, dtype=np.float32), (P, 1)),
    }


def kernel(**inputs):
    from types import SimpleNamespace

    import concourse.bacc as bacc
    from concourse.bass_utils import run_bass_kernel_spmd

    nc = bacc.Bacc("TRN2", target_bir_lowering=False, num_devices=1)

    arrays, aps = {}, {}
    given = {short: inputs[name] for short, name in _INPUTS.items()}
    for short, a in {**given, **_constants()}.items():
        a = np.ascontiguousarray(a)
        arrays[f"in_{short}"] = a
        aps[short] = nc.dram_tensor(f"in_{short}", a.shape, mybir.dt.from_np(a.dtype), kind="ExternalInput").ap()
    d = SimpleNamespace(**aps)
    d.c, d.wmod = [d.c0, d.c1], [d.wmod0, d.wmod1]
    d.out = nc.dram_tensor("out", [NB, T, C], F32, kind="ExternalOutput").ap()
    program(nc, d)
    r = run_bass_kernel_spmd(nc, [arrays], core_ids=[0])
    return r.results[0]["out"]
```
